# Optimizing a Trainium2 kernel written in Bass

```python
import numpy as np
import jax
import jax.numpy as jnp

def _softmax(x, axis=-1):
    return jax.nn.softmax(x, axis=axis)

def _gelu(x):
    return jax.nn.gelu(x, approximate=True)

def _silu(x):
    return jax.nn.silu(x)

def _sigmoid(x):
    return jax.nn.sigmoid(x)

def _layernorm(x, axis=-1, eps=1e-05):
    m = jnp.mean(x, axis=axis, keepdims=True)
    v = jnp.var(x, axis=axis, keepdims=True)
    return (x - m) / jnp.sqrt(v + eps)

def _scatter_add(tgt, idx, src, axis=0):
    return tgt.at[idx].add(src)

def _segment_sum(src, seg, n):
    return jax.ops.segment_sum(src, seg, n)
kernel_name = 'mk_perceiver_d2_seqx_r8_040a48'

def setup_inputs(seed: int=0):
    np.random.seed(seed)
    _w = jnp.asarray

    def _rec_inputs():
        import jax
        import jax.numpy as jnp
        _rk = jax.random.key(seed)
        x = 7.22e-05 + 1 * jax.random.normal(jax.random.fold_in(_rk, 1), (16, 64, 128), jnp.float32)
        _lenS = 64 - jax.random.randint(jax.random.fold_in(_rk, 7), (16,), 0, max(1, 64 // 4) + 1, jnp.int32)
        _lenS2 = 1601 - jax.random.randint(jax.random.fold_in(_rk, 8), (16,), 0, max(1, 1601 // 4) + 1, jnp.int32)
        _ctx_1024P = jax.random.normal(jax.random.fold_in(_rk, 11), (16, 16, 128), jnp.float32)
        _ctx_1024c = jax.random.dirichlet(jax.random.fold_in(_rk, 511), 0.3 * jnp.ones((16,), jnp.float32), (16, 1601))
        _ctx_1024t = jnp.einsum('bsk,bkd->bsd', _ctx_1024c, _ctx_1024P)
        _ctx_1024t = _ctx_1024t * jax.lax.rsqrt(jnp.mean(jnp.square(_ctx_1024t)) + 1e-12) * 0.953939
        ctx_1024 = 4.13588e-05 + 0.999923 * (_ctx_1024t + 0.3 * jax.random.normal(jax.random.fold_in(_rk, 611), (16, 1601, 128), jnp.float32))
        return (x, ctx_1024)
    x, ctx_1024 = _rec_inputs()

    def _L0_xattn_setup():
        import jax, jax.numpy as jnp
        import numpy as np
        D_MODEL = 128
        NUM_HEADS = 16
        D_K = D_MODEL // NUM_HEADS
        SCALE = float(np.sqrt(D_K))
        key = jax.random.key(seed)
        ks = jax.random.split(key, 11)
        B, S, D = (4, 256, D_MODEL)
        w_std = 1.0 / np.sqrt(D)
        inp = {'query': jax.random.normal(ks[0], (B, S, D), jnp.float32), 'key': jax.random.normal(ks[1], (B, S, D), jnp.float32), 'value': jax.random.normal(ks[2], (B, S, D), jnp.float32), 'wq': jax.random.normal(ks[3], (D, D), jnp.float32) * w_std, 'bq': jax.random.normal(ks[4], (D,), jnp.float32) * w_std, 'wk': jax.random.normal(ks[5], (D, D), jnp.float32) * w_std, 'bk': jax.random.normal(ks[6], (D,), jnp.float32) * w_std, 'wv': jax.random.normal(ks[7], (D, D), jnp.float32) * w_std, 'bv': jax.random.normal(ks[8], (D,), jnp.float32) * w_std, 'wo': jax.random.normal(ks[9], (D, D), jnp.float32) * w_std, 'bo': jax.random.normal(ks[10], (D,), jnp.float32) * w_std}
        return inp
    _L0_xattn_all = _L0_xattn_setup()
    _L0_xattn_in = {k: v for k, v in _L0_xattn_all.items() if k in ('wq', 'bq', 'wk', 'bk', 'wv', 'bv', 'wo', 'bo')}
    del _L0_xattn_all

    def _L0_attn_setup():
        import jax, jax.numpy as jnp
        import numpy as np
        from math import sqrt
        D_MODEL = 128
        NUM_HEADS = 16
        D_HEAD = D_MODEL // NUM_HEADS
        THETA = 10000.0

        def _rope(x, freqs):
            xr = x[..., ::2]
            xi = x[..., 1::2]
            cos = jnp.cos(freqs)
            sin = jnp.sin(freqs)
            yr = xr * cos - xi * sin
            yi = xr * sin + xi * cos
            return jnp.stack([yr, yi], axis=-1).reshape(x.shape)
        key = jax.random.key(seed)
        k1, k2, k3 = jax.random.split(key, 3)
        X = jax.random.normal(k1, (4, 256, D_MODEL), dtype=jnp.float32)
        std_kqv = sqrt(2.0 / (D_MODEL + 3 * D_MODEL))
        W_KQV = std_kqv * jax.random.truncated_normal(k2, -3.0, 3.0, (3 * D_MODEL, D_MODEL), dtype=jnp.float32)
        std_o = sqrt(2.0 / (D_MODEL + D_MODEL))
        W_O = std_o * jax.random.truncated_normal(k3, -3.0, 3.0, (D_MODEL, D_MODEL), dtype=jnp.float32)
        return {'X': X, 'W_KQV': W_KQV, 'W_O': W_O}
    _L0_attn_all = _L0_attn_setup()
    _L0_attn_in = {k: v for k, v in _L0_attn_all.items() if k in ('W_KQV', 'W_O')}
    del _L0_attn_all

    def _L0_ffn_setup():
        import jax, jax.numpy as jnp
        import numpy as np
        TOP_K = 2
        key = jax.random.key(seed)
        k1, k2, k3, k4 = jax.random.split(key, 4)
        B, S, D = (2, 256, 128)
        E, W = (8, 128)
        x = jax.random.normal(k1, (B, S, D), dtype=jnp.float32)
        router_w = jax.random.normal(k2, (E, D), dtype=jnp.float32) * 0.02
        w1 = jax.random.normal(k3, (D, E * W), dtype=jnp.float32) * 0.02
        w2 = jax.random.normal(k4, (E * W, D), dtype=jnp.float32) * 0.02
        return {'x': x, 'router_w': router_w, 'w1': w1, 'w2': w2}
    _L0_ffn_all = _L0_ffn_setup()
    _L0_ffn_in = {k: v for k, v in _L0_ffn_all.items() if k in ('router_w', 'w1', 'w2')}
    del _L0_ffn_all

    def _L1_xattn_setup():
        import jax, jax.numpy as jnp
        import numpy as np
        DIM = 128
        HEADS = 16
        DIM_HEAD = 64
        INNER = HEADS * DIM_HEAD
        EPS = 1e-05

        def _layernorm(t, w, b):
            mu = jnp.mean(t, axis=-1, keepdims=True)
            var = jnp.mean(jnp.square(t - mu), axis=-1, keepdims=True)
            return (t - mu) * jax.lax.rsqrt(var + EPS) * w + b
        key = jax.random.key(seed)
        ks = jax.random.split(key, 8)
        b, n, l = (8, 512, 64)
        x = jax.random.normal(ks[0], (b, n, DIM), dtype=jnp.float32)
        latents = jax.random.normal(ks[1], (b, l, DIM), dtype=jnp.float32)
        ln1_w = jnp.ones((DIM,), jnp.float32)
        ln1_b = jnp.zeros((DIM,), jnp.float32)
        ln2_w = jnp.ones((DIM,), jnp.float32)
        ln2_b = jnp.zeros((DIM,), jnp.float32)
        Wq = jax.random.normal(ks[2], (DIM, INNER), dtype=jnp.float32) / np.sqrt(DIM)
        Wkv = jax.random.normal(ks[3], (DIM, 2 * INNER), dtype=jnp.float32) / np.sqrt(DIM)
        Wo = jax.random.normal(ks[4], (INNER, DIM), dtype=jnp.float32) / np.sqrt(INNER)
        return {'x': x, 'latents': latents, 'ln1_w': ln1_w, 'ln1_b': ln1_b, 'ln2_w': ln2_w, 'ln2_b': ln2_b, 'Wq': Wq, 'Wkv': Wkv, 'Wo': Wo}
    _L1_xattn_all = _L1_xattn_setup()
    _L1_xattn_in = {k: v for k, v in _L1_xattn_all.items() if k in ('ln1_w', 'ln1_b', 'ln2_w', 'ln2_b', 'Wq', 'Wkv', 'Wo')}
    del _L1_xattn_all

    def _L1_attn_setup():
        import jax, jax.numpy as jnp
        import numpy as np
        N_EMBD = 128
        N_ATTN = 128
        N_HEAD = 16
        N_LAYER = 12
        LAYER_ID = 5
        CTX = 256
        BATCH = 8
        HEAD_SIZE = N_ATTN // N_HEAD
        K_CLAMP = 60.0
        K_EPS = 1e-16

        def _time_decay_init():
            first = 1
            f1 = 3.0 + (LAYER_ID - first) / (N_LAYER - 1 - first) * (1.2 - 3.0)
            f2 = 0.65 + (LAYER_ID - first) / (N_LAYER - 1 - first) * (0.4 - 0.65)
            if LAYER_ID == first:
                f1 += 0.5
            if LAYER_ID == N_LAYER - 2:
                f2 = 0.4
            if LAYER_ID == N_LAYER - 1:
                f2 = 0.37
            h = np.arange(N_HEAD, dtype=np.float64)
            decay_speed = np.power(f2, h / (N_HEAD - 1) * 7) * f1
            return np.log(decay_speed).astype(np.float32)[:, None]
        key = jax.random.key(seed)
        ks = jax.random.split(key, 5)
        x = jax.random.normal(ks[0], (BATCH, CTX, N_EMBD), dtype=jnp.float32)
        tm = np.ones((1, 1, N_EMBD), dtype=np.float32)
        tm[0, 0, :N_EMBD // 2] = 0.0
        scale = 0.02
        return {'x': x, 'time_decay': jnp.asarray(_time_decay_init()), 'time_first': jnp.full((N_HEAD, 1), np.log(0.3), dtype=jnp.float32), 'time_mix': jnp.asarray(tm), 'Wk': jax.random.normal(ks[1], (N_ATTN, N_EMBD), dtype=jnp.float32) * scale, 'Wv': jax.random.normal(ks[2], (N_ATTN, N_EMBD), dtype=jnp.float32) * scale, 'Wr': jax.random.normal(ks[3], (N_ATTN, N_EMBD), dtype=jnp.float32) * scale, 'Wo': jax.random.normal(ks[4], (N_EMBD, N_ATTN), dtype=jnp.float32) * scale}
    _L1_attn_all = _L1_attn_setup()
    _L1_attn_in = {k: v for k, v in _L1_attn_all.items() if k in ('time_decay', 'time_first', 'time_mix', 'Wk', 'Wv', 'Wr', 'Wo')}
    del _L1_attn_all

    def _L1_ffn_setup():
        import jax, jax.numpy as jnp
        import numpy as np
        MANT_BITS = 8
        _PWL_X = jnp.linspace(-4.0, 4.0, 33, dtype=jnp.float32)
        _PWL_Y = 0.5 * _PWL_X * (1.0 + jax.lax.erf(_PWL_X / jnp.sqrt(jnp.float32(2.0))))

        def float2fix(x, mantissa_bits):
            s = jnp.float32(2.0 ** mantissa_bits)
            q = jnp.round(x * s) / s
            return x + jax.lax.stop_gradient(q - x)

        def pwlin_gelu_basic(x, mantissa_bits_in, mantissa_bits_out):
            xq = float2fix(x, mantissa_bits_in)
            y = jnp.interp(xq, _PWL_X, _PWL_Y)
            y = jnp.where(xq > 4.0, xq, jnp.where(xq < -4.0, jnp.float32(0.0), y))
            return float2fix(y, mantissa_bits_out)
        key = jax.random.key(seed)
        k_x, k_w1, k_b1, k_w2, k_b2 = jax.random.split(key, 5)
        dim, ff_dim = (128, 512)
        B, S = (32, 64)
        sc1 = 1.0 / np.sqrt(dim)
        sc2 = 1.0 / np.sqrt(ff_dim)
        return {'x': jax.random.normal(k_x, (B, S, dim), dtype=jnp.float32), 'w1': jax.random.uniform(k_w1, (dim, ff_dim), jnp.float32, -sc1, sc1), 'b1': jax.random.uniform(k_b1, (ff_dim,), jnp.float32, -sc1, sc1), 'w2': jax.random.uniform(k_w2, (ff_dim, dim), jnp.float32, -sc2, sc2), 'b2': jax.random.uniform(k_b2, (dim,), jnp.float32, -sc2, sc2)}
    _L1_ffn_all = _L1_ffn_setup()
    _L1_ffn_in = {k: v for k, v in _L1_ffn_all.items() if k in ('w1', 'b1', 'w2', 'b2')}
    del _L1_ffn_all
    return {'x': x, 'ctx_1024': ctx_1024, 'L0_xattn_wq': _L0_xattn_in['wq'], 'L0_xattn_bq': _L0_xattn_in['bq'], 'L0_xattn_wk': _L0_xattn_in['wk'], 'L0_xattn_bk': _L0_xattn_in['bk'], 'L0_xattn_wv': _L0_xattn_in['wv'], 'L0_xattn_bv': _L0_xattn_in['bv'], 'L0_xattn_wo': _L0_xattn_in['wo'], 'L0_xattn_bo': _L0_xattn_in['bo'], 'L0_attn_W_KQV': _L0_attn_in['W_KQV'], 'L0_attn_W_O': _L0_attn_in['W_O'], 'L0_ffn_router_w': _L0_ffn_in['router_w'], 'L0_ffn_w1': _L0_ffn_in['w1'], 'L0_ffn_w2': _L0_ffn_in['w2'], 'L1_xattn_ln1_w': _L1_xattn_in['ln1_w'], 'L1_xattn_ln1_b': _L1_xattn_in['ln1_b'], 'L1_xattn_ln2_w': _L1_xattn_in['ln2_w'], 'L1_xattn_ln2_b': _L1_xattn_in['ln2_b'], 'L1_xattn_Wq': _L1_xattn_in['Wq'], 'L1_xattn_Wkv': _L1_xattn_in['Wkv'], 'L1_xattn_Wo': _L1_xattn_in['Wo'], 'L1_attn_time_decay': _L1_attn_in['time_decay'], 'L1_attn_time_first': _L1_attn_in['time_first'], 'L1_attn_time_mix': _L1_attn_in['time_mix'], 'L1_attn_Wk': _L1_attn_in['Wk'], 'L1_attn_Wv': _L1_attn_in['Wv'], 'L1_attn_Wr': _L1_attn_in['Wr'], 'L1_attn_Wo': _L1_attn_in['Wo'], 'L1_ffn_w1': _L1_ffn_in['w1'], 'L1_ffn_b1': _L1_ffn_in['b1'], 'L1_ffn_w2': _L1_ffn_in['w2'], 'L1_ffn_b2': _L1_ffn_in['b2']}

def reference(x, ctx_1024, L0_xattn_wq, L0_xattn_bq, L0_xattn_wk, L0_xattn_bk, L0_xattn_wv, L0_xattn_bv, L0_xattn_wo, L0_xattn_bo, L0_attn_W_KQV, L0_attn_W_O, L0_ffn_router_w, L0_ffn_w1, L0_ffn_w2, L1_xattn_ln1_w, L1_xattn_ln1_b, L1_xattn_ln2_w, L1_xattn_ln2_b, L1_xattn_Wq, L1_xattn_Wkv, L1_xattn_Wo, L1_attn_time_decay, L1_attn_time_first, L1_attn_time_mix, L1_attn_Wk, L1_attn_Wv, L1_attn_Wr, L1_attn_Wo, L1_ffn_w1, L1_ffn_b1, L1_ffn_w2, L1_ffn_b2):
    import jax
    import jax.numpy as jnp

    def _L0_xattn_ref(query, key, value, wq, bq, wk, bk, wv, bv, wo, bo):
        import jax, jax.numpy as jnp
        import numpy as np
        D_MODEL = 128
        NUM_HEADS = 16
        D_K = D_MODEL // NUM_HEADS
        SCALE = float(np.sqrt(D_K))
        B, Sq, D = query.shape
        H, dk = (NUM_HEADS, D_K)
        q = query @ wq + bq
        k = key @ wk + bk
        v = value @ wv + bv
        q = q.reshape(B, Sq, H, dk).transpose(0, 2, 1, 3)
        k = k.reshape(B, -1, H, dk).transpose(0, 2, 1, 3)
        v = v.reshape(B, -1, H, dk).transpose(0, 2, 1, 3)
        att = jnp.einsum('bhqd,bhkd->bhqk', q, k) / SCALE
        att = jax.nn.softmax(att, axis=-1)
        out = jnp.einsum('bhqk,bhkd->bhqd', att, v)
        out = out.transpose(0, 2, 1, 3).reshape(B, Sq, D)
        return out @ wo + bo

    def _L0_attn_ref(X, W_KQV, W_O):
        import jax, jax.numpy as jnp
        import numpy as np
        from math import sqrt
        D_MODEL = 128
        NUM_HEADS = 16
        D_HEAD = D_MODEL // NUM_HEADS
        THETA = 10000.0

        def _rope(x, freqs):
            xr = x[..., ::2]
            xi = x[..., 1::2]
            cos = jnp.cos(freqs)
            sin = jnp.sin(freqs)
            yr = xr * cos - xi * sin
            yi = xr * sin + xi * cos
            return jnp.stack([yr, yi], axis=-1).reshape(x.shape)
        B, S, D = X.shape
        H, d = (NUM_HEADS, D_HEAD)
        KQV = jnp.einsum('bsd,ed->bse', X, W_KQV)
        K, Q, V = jnp.split(KQV, [D, 2 * D], axis=-1)

        def to_heads(t):
            return t.reshape(B, S, H, d).transpose(0, 2, 1, 3)
        K, Q, V = (to_heads(K), to_heads(Q), to_heads(V))
        inv_freq = 1.0 / THETA ** (jnp.arange(0, d, 2, dtype=jnp.float32) / d)
        pos = jnp.arange(S, dtype=jnp.float32)
        freqs = pos[:, None] * inv_freq[None, :]
        Q = _rope(Q, freqs)
        K = _rope(K, freqs)
        scores = jnp.einsum('bhqd,bhkd->bhqk', Q, K) / sqrt(d)
        causal = jnp.triu(jnp.ones((S, S), dtype=bool), k=1)
        scores = jnp.where(causal, -jnp.inf, scores)
        probs = jax.nn.softmax(scores, axis=-1)
        heads = jnp.einsum('bhqk,bhkd->bhqd', probs, V)
        acts = heads.transpose(0, 2, 1, 3).reshape(B, S, D)
        return jnp.einsum('bsd,ed->bse', acts, W_O)

    def _L0_ffn_ref(x, router_w, w1, w2):
        import jax, jax.numpy as jnp
        import numpy as np
        TOP_K = 2
        B, S, D = x.shape
        E = router_w.shape[0]
        W = w1.shape[1] // E
        T = B * S
        xf = x.reshape(T, D)
        router_logits = jnp.einsum('td,ed->te', xf, router_w)
        router_probs = jax.nn.sigmoid(router_logits.astype(jnp.float32))
        top_w, sel = jax.lax.top_k(router_probs, TOP_K)
        top_w = top_w / (top_w.sum(axis=-1, keepdims=True) + 1e-20)
        top_w = top_w.astype(x.dtype)
        W1e = w1.reshape(D, E, W).transpose(1, 0, 2)
        W2e = w2.reshape(E, W, D)
        h = jnp.einsum('td,edw->etw', xf, W1e)
        a = jnp.square(jax.nn.relu(h))
        y = jnp.einsum('etw,ewd->etd', a, W2e)
        cw = jnp.zeros((T, E), dtype=x.dtype).at[jnp.arange(T)[:, None], sel].set(top_w)
        out = jnp.einsum('etd,te->td', y, cw)
        return out.reshape(B, S, D)

    def _L1_xattn_ref(x, latents, ln1_w, ln1_b, ln2_w, ln2_b, Wq, Wkv, Wo):
        import jax, jax.numpy as jnp
        import numpy as np
        DIM = 128
        HEADS = 16
        DIM_HEAD = 64
        INNER = HEADS * DIM_HEAD
        EPS = 1e-05

        def _layernorm(t, w, b):
            mu = jnp.mean(t, axis=-1, keepdims=True)
            var = jnp.mean(jnp.square(t - mu), axis=-1, keepdims=True)
            return (t - mu) * jax.lax.rsqrt(var + EPS) * w + b
        xn = _layernorm(x, ln1_w, ln1_b)
        latn = _layernorm(latents, ln2_w, ln2_b)
        b, l, _ = latn.shape
        q = latn @ Wq
        kv_input = jnp.concatenate([xn, latn], axis=1)
        kv = kv_input @ Wkv
        k, v = jnp.split(kv, 2, axis=-1)

        def heads(t):
            return t.reshape(t.shape[0], t.shape[1], HEADS, DIM_HEAD).transpose(0, 2, 1, 3)
        q, k, v = (heads(q), heads(k), heads(v))
        scale = 1.0 / np.sqrt(np.sqrt(DIM_HEAD))
        weight = jnp.einsum('bhld,bhnd->bhln', q * scale, k * scale)
        weight = jax.nn.softmax(weight.astype(jnp.float32), axis=-1).astype(weight.dtype)
        out = jnp.einsum('bhln,bhnd->bhld', weight, v)
        out = out.transpose(0, 2, 1, 3).reshape(b, l, INNER)
        return out @ Wo

    def _L1_attn_ref(x, time_decay, time_first, time_mix, Wk, Wv, Wr, Wo):
        import jax, jax.numpy as jnp
        import numpy as np
        N_EMBD = 128
        N_ATTN = 128
        N_HEAD = 16
        N_LAYER = 12
        LAYER_ID = 5
        CTX = 256
        BATCH = 8
        HEAD_SIZE = N_ATTN // N_HEAD
        K_CLAMP = 60.0
        K_EPS = 1e-16

        def _time_decay_init():
            first = 1
            f1 = 3.0 + (LAYER_ID - first) / (N_LAYER - 1 - first) * (1.2 - 3.0)
            f2 = 0.65 + (LAYER_ID - first) / (N_LAYER - 1 - first) * (0.4 - 0.65)
            if LAYER_ID == first:
                f1 += 0.5
            if LAYER_ID == N_LAYER - 2:
                f2 = 0.4
            if LAYER_ID == N_LAYER - 1:
                f2 = 0.37
            h = np.arange(N_HEAD, dtype=np.float64)
            decay_speed = np.power(f2, h / (N_HEAD - 1) * 7) * f1
            return np.log(decay_speed).astype(np.float32)[:, None]
        B, T, C = x.shape
        H = time_decay.shape[0]
        D = Wk.shape[0] // H
        xs = jnp.pad(x, ((0, 0), (1, 0), (0, 0)))[:, :T]
        xm = x * time_mix + xs * (1.0 - time_mix)
        k = jnp.exp(jnp.minimum(xm @ Wk.T, K_CLAMP))
        v = xm @ Wv.T
        r = xm @ Wr.T
        kv = k * v
        lag = jnp.arange(T)[:, None] - jnp.arange(T)[None, :]
        dec = jnp.exp(time_decay[:, 0])[:, None, None]
        e = jnp.exp(-dec * jnp.maximum(lag - 1, 0).astype(jnp.float32))
        Wm = jnp.where(lag >= 1, e, 0.0)
        Wm = jnp.where(lag == 0, jnp.exp(time_first[:, 0])[:, None, None], Wm)
        kh = k.reshape(B, T, H, D)
        kvh = kv.reshape(B, T, H, D)
        wkv = jnp.einsum('htu,buhd->bthd', Wm, kvh).reshape(B, T, H * D)
        sum_k = jnp.einsum('htu,buhd->bthd', Wm, kh).reshape(B, T, H * D) + K_EPS
        rwkv = jax.nn.sigmoid(r) * wkv / sum_k
        return rwkv @ Wo.T

    def _L1_ffn_ref(x, w1, b1, w2, b2):
        import jax, jax.numpy as jnp
        import numpy as np
        MANT_BITS = 8
        _PWL_X = jnp.linspace(-4.0, 4.0, 33, dtype=jnp.float32)
        _PWL_Y = 0.5 * _PWL_X * (1.0 + jax.lax.erf(_PWL_X / jnp.sqrt(jnp.float32(2.0))))

        def float2fix(x, mantissa_bits):
            s = jnp.float32(2.0 ** mantissa_bits)
            q = jnp.round(x * s) / s
            return x + jax.lax.stop_gradient(q - x)

        def pwlin_gelu_basic(x, mantissa_bits_in, mantissa_bits_out):
            xq = float2fix(x, mantissa_bits_in)
            y = jnp.interp(xq, _PWL_X, _PWL_Y)
            y = jnp.where(xq > 4.0, xq, jnp.where(xq < -4.0, jnp.float32(0.0), y))
            return float2fix(y, mantissa_bits_out)
        h = jnp.einsum('bsd,df->bsf', x, w1) + b1
        h = float2fix(h, MANT_BITS)
        h = pwlin_gelu_basic(h, MANT_BITS, MANT_BITS)
        h = float2fix(h, MANT_BITS)
        out = jnp.einsum('bsf,fd->bsd', h, w2) + b2
        return float2fix(out, MANT_BITS)
    x = x + _L0_xattn_ref(_layernorm(x, axis=-1), ctx_1024, ctx_1024, L0_xattn_wq, L0_xattn_bq, L0_xattn_wk, L0_xattn_bk, L0_xattn_wv, L0_xattn_bv, L0_xattn_wo, L0_xattn_bo)
    x = x + _L0_attn_ref(_layernorm(x, axis=-1), L0_attn_W_KQV, L0_attn_W_O)
    x = x + _L0_ffn_ref(_layernorm(x, axis=-1), L0_ffn_router_w, L0_ffn_w1, L0_ffn_w2)
    x = x + _L1_xattn_ref(ctx_1024, _layernorm(x, axis=-1), L1_xattn_ln1_w, L1_xattn_ln1_b, L1_xattn_ln2_w, L1_xattn_ln2_b, L1_xattn_Wq, L1_xattn_Wkv, L1_xattn_Wo)
    x = x + _L1_attn_ref(_layernorm(x, axis=-1), L1_attn_time_decay, L1_attn_time_first, L1_attn_time_mix, L1_attn_Wk, L1_attn_Wv, L1_attn_Wr, L1_attn_Wo)
    x = x + _L1_ffn_ref(_layernorm(x, axis=-1), L1_ffn_w1, L1_ffn_b1, L1_ffn_w2, L1_ffn_b2)
    return x

_drawn_inputs = setup_inputs


def setup_inputs(seed=0):
    import zlib

    import numpy as np

    out = dict(_drawn_inputs(seed))
    spreads = {'L1_xattn_ln1_w': (1.0, 0.2),
     'L1_xattn_ln1_b': (0.0, 0.407),
     'L1_xattn_ln2_w': (1.0, 0.57),
     'L1_xattn_ln2_b': (0.0, 0.51),
     'L1_attn_time_first': (-1.2039728164672852, 0.6)}
    factors = {'L0_xattn_bq': 3.226,
     'L0_xattn_bk': 64.0,
     'L0_ffn_router_w': 8.0,
     'L0_ffn_w1': 8.0,
     'L0_ffn_w2': 7.464,
     'L1_attn_time_decay': 8.0,
     'L1_attn_time_mix': 8.0,
     'L1_attn_Wk': 8.0,
     'L1_attn_Wv': 4.034,
     'L1_attn_Wr': 8.0,
     'L1_attn_Wo': 4.066,
     'L1_ffn_b1': 19.467,
     'L1_ffn_b2': 13.42}
    for name, (base, spread) in spreads.items():
        noise = np.random.default_rng([zlib.crc32(name.encode()), seed]).standard_normal(out[name].shape)
        drawn = base * np.exp(spread * noise) if base else spread * noise
        out[name] = jnp.asarray(drawn.astype(out[name].dtype))
    for name, factor in factors.items():
        out[name] = (out[name] * factor).astype(out[name].dtype)
    return out
```

```python
from contextlib import ExitStack

import concourse.bass as bass
from concourse import mybir

ALU = mybir.AluOpType
ACT = mybir.ActivationFunctionType
AX_X = mybir.AxisListType.X
F32 = mybir.dt.float32
F32R = mybir.dt.float32r
U32 = mybir.dt.uint32

P = 128
D = 128
BATCH, SEQ, CTX = 16, 64, 1601
TOKENS = BATCH * SEQ
TOK_TILES = TOKENS // P
HEADS = 16
PAIRS = HEADS // 2
QUAD = 4
QUADS = PAIRS // QUAD
FULL = CTX // P
TAIL = CTX - FULL * P
BANK = 512
CHUNKS = 4
BODIES = BATCH // 2
SLOTS = 2 * PAIRS
LN_EPS = 1e-5
FIRST_SEMAPHORE = 128
E0 = 8

C_IDENT, C_PAIRROWS, C_HEADROWS, C_CAUSAL, C_COS, C_SIN, C_IOTA, C_SEQSTART, C_QUADROWS, C_GROUPROWS = 0, 128, 160, 168, 232, 296, 360, 368, 433, 437
C_END = C_GROUPROWS + 4


class Named:
    pass


def quad_chunk(c, width):
    return slice(c * BANK, min((c + 1) * BANK, width))


def semaphores_of_part(nc, ctx, tag):
    made = []

    def clear_all():
        nc.all_engine_barrier(sems_to_clear=range(FIRST_SEMAPHORE, FIRST_SEMAPHORE + len(made)))
        for s in reversed(made):
            nc.release_semaphore(s)

    def sem(name):
        made.append(nc.alloc_semaphore(tag + name, num=FIRST_SEMAPHORE + len(made)))
        return made[-1]

    ctx.callback(clear_all)
    return sem


def number_jobs(jobs, n_before):
    table = {}
    for kind in ("first", "mid", "last"):
        found, n = {}, 0
        for s in range(SLOTS):
            m, slot = divmod(s, PAIRS)
            for i, pos in enumerate("ba"):
                job = jobs[m][2 * slot + i]
                finishes = job is not None and job[0] in ("norm", "out")
                if job is None or (kind == "first" and finishes and s < 7) or (kind == "last" and m == 1 and not finishes):
                    continue
                found[s, pos] = (job, n)
                n += 1
        table[kind] = found
    per_body = len(table["mid"])
    skipped = per_body - len(table["first"])

    def base(kind, k):
        return n_before if kind == "first" else k * per_body + n_before - skipped

    return table, base


def number_after(table, base, k, kind, s, pos):
    if s < 0:
        return base(kind, k) - len(table["mid"]) + table["mid"][s + SLOTS, pos][1] + 1
    return base(kind, k) + table[kind][s, pos][1] + 1


def attend(nc, g, lay, ctx):
    tag = lay.tag

    def sb(name, shape, dt=F32):
        return ctx.enter_context(nc.sbuf_tensor(tag + name, shape, dt))

    sem = semaphores_of_part(nc, ctx, tag)

    keys, tiles = lay.keys, lay.tiles
    groups = [tiles[4 * c:4 * c + 4] for c in range(CHUNKS)]
    prob = [sb(f"prob{i}", [P, keys]) for i in range(2)]
    prob_t = [sb(f"prob_t{i}", [P, len(tiles), BANK]) for i in range(2)]
    chunk_max = sb("chunk_max", [P, 2, CHUNKS])
    neg_max = sb("neg_max", [P, 2])
    sums = sb("sums", [P, 2, QUAD, CHUNKS])
    den = sb("den", [P, QUAD])
    rden = sb("rden", [P, QUAD])
    diag = sb("diag", [P, QUAD, P])
    norm = sb("norm", [P, lay.norm_cols])

    score_ps = ctx.enter_context(nc.psum_tensor(tag + "score_ps", [P, CHUNKS * BANK], F32))
    turn_ps = [ctx.enter_context(nc.psum_tensor(f"{tag}turn_ps{i}", [P, BANK], F32)) for i in range(2)]
    pv_ps = ctx.enter_context(nc.psum_tensor(tag + "pv_ps", [P, BANK], F32))
    scratch = ctx.enter_context(nc.psum_tensor(tag + "scratch", [P, BANK], F32))

    scratch_ready, scratch_free, half_taken = sem("scratch_ready"), sem("scratch_free"), sem("half_taken")
    scores_ready, chunk_max_done, neg_max_done, exp_done = (sem(n) for n in ("scores", "chunk_max", "neg_max", "exp"))
    turned, copied_dve, copied_act = sem("turned"), sem("copied_dve"), sem("copied_act")
    den_done, rden_done, diag_done, pv_done = (sem(n) for n in ("den", "rden", "diag", "pv"))
    pv_taken = sem("pv_taken")

    own = Named()
    own.sb, own.sem, own.score_ps, own.turn_ps = sb, sem, score_ps, turn_ps
    own.pv_ps, own.scratch, own.prob_t, own.norm = pv_ps, scratch, prob_t, norm
    own.scratch_ready, own.scratch_free, own.half_taken, own.scores_ready = scratch_ready, scratch_free, half_taken, scores_ready
    own.pv_done, own.pv_taken = pv_done, pv_taken
    lay.allocate(own)
    prepare = [j for j in lay.jobs[0] if j and j[0] not in ("norm", "out")]
    table, base = number_jobs(lay.jobs, len(prepare))
    own.table, own.base = table, base
    own.number_after = lambda k, kind, s, pos: number_after(table, base, k, kind, s, pos)

    ctx.enter_context(nc.allow_non_contiguous_dma(reason="vectors: one element per partition"))
    block = ctx.enter_context(nc.Block())
    ident = g.consts[:, C_IDENT:C_IDENT + P]

    def quad_of(i):
        return i // QUADS % 2, i % QUADS

    @block.sync
    def _(sp):
        lay.sync_start(sp)
        for kind, ks in (("first", 0), ("mid", None)):
            if ks is None:
                with sp.Fori(1, BODIES - 1) as k:
                    lay.sync_body(sp, k, kind)
            else:
                lay.sync_body(sp, ks, kind)
        lay.sync_body(sp, BODIES - 1, "last")
        lay.sync_end(sp)

    @block.gpsimd
    def _(pool):
        def make_diag(q, taken):
            pool.wait_ge(rden_done, q + 1)
            if taken is not None:
                pool.wait_ge(scratch_free, taken)
            nc.gpsimd.tensor_tensor(diag[:], ident.unsqueeze(1).broadcast_to([P, QUAD, P]),
                                    rden[:].unsqueeze(2).broadcast_to([P, QUAD, P]), ALU.mult).then_inc(diag_done, 1)

        def body(k, kind):
            for m in range(2):
                if not (kind == "first" and m == 0):
                    make_diag(4 * k + 2 * m - 1, own.number_after(k, kind, PAIRS * m - 1, "a"))
                if not (kind == "last" and m == 1):
                    lay.pool_prepare(pool, k, kind, m)
                make_diag(4 * k + 2 * m, None if kind == "first" and m == 0 else own.number_after(k, kind, PAIRS * m + 3, "a"))

        lay.pool_start(pool)
        body(0, "first")
        with pool.Fori(1, BODIES - 1) as k:
            body(k, "mid")
        body(BODIES - 1, "last")
        make_diag(2 * BATCH - 1, own.number_after(BODIES - 1, "last", 15, "a"))

    @block.tensor
    def _(pe):
        def job(what, n, m, kind, k, s):
            if not (isinstance(n, int) and n == 0):
                pe.wait_ge(scratch_free, n)
            if what[0] == "norm":
                pe.wait_ge(diag_done, 4 * k + (s - 7) // QUAD + 1)
                lay.pe_norm(pe, diag).then_inc(scratch_ready, 1)
            else:
                lay.pe_job(pe, what, m, kind, k, s).then_inc(scratch_ready, 1)

        def turn(k, kind, s, c):
            pair = k * SLOTS + s - 1
            first = kind == "first" and s == 1
            if c == 0 and not first:
                pe.wait_ge(copied_act, pair)
            if c == 1 and not first:
                pe.wait_ge(copied_dve, 3 * pair)
            if c >= 2:
                pe.wait_ge(copied_dve, 3 * pair + c - 1)
            for i, (rows, col) in enumerate(groups[c]):
                last = nc.tensor.transpose(turn_ps[c % 2][0:rows, P * i:P * i + P], prob[(s - 1) % 2][:, col:col + rows], ident)
            last.then_inc(turned, 1)

        def weigh_values(k, i, part):
            q = 4 * k + i
            m, u = quad_of(i)
            if part == 0:
                pe.wait_ge(copied_dve, (q + 1) * QUAD * 3)
                pe.wait_ge(copied_act, (q + 1) * QUAD)
                if not (isinstance(q, int) and q == 0):
                    pe.wait_ge(pv_taken, q)
            last = lay.pe_values(pe, m, u, range(4 * part, min(4 * part + 4, len(tiles))))
            last.then_inc(pv_done, 1)

        def body(k, kind):
            for s in range(SLOTS):
                m, n = divmod(s, PAIRS)
                u, j = divmod(n, QUAD)
                pair = k * SLOTS + s
                before = not (kind == "first" and s == 0)
                if j == 0:
                    lay.pe_operands_ready(pe, k, kind, m, u)
                for c in range(CHUNKS):
                    if before:
                        pe.wait_ge(exp_done, (pair - 1) * CHUNKS + c + 1)
                    cols = slice(c * BANK, min(c * BANK + BANK, keys + keys % 2))
                    passes = lay.score_passes(m, u, j)
                    for i, (queries, keys_t) in enumerate(passes):
                        mm = nc.tensor.matmul(score_ps[:, cols], queries, keys_t[:, cols], start=(i == 0), stop=(i == len(passes) - 1))
                    mm.then_inc(scores_ready, 1)
                    if before and c < CHUNKS - 1:
                        turn(k, kind, s, c)
                    if c == 2 and (s, "b") in table[kind]:
                        what, number = table[kind][s, "b"]
                        job(what, base(kind, k) + number, m, kind, k, s)
                i, part = (s // QUAD - 1, s % QUAD - 1) if s % QUAD else (s // QUAD - 2, CHUNKS - 1)
                if not (kind == "first" and i < 0):
                    weigh_values(k, i, part)
                if (s, "a") in table[kind]:
                    what, number = table[kind][s, "a"]
                    job(what, base(kind, k) + number, m, kind, k, s)
                if before:
                    turn(k, kind, s, CHUNKS - 1)

        lay.pe_start(pe)
        for n, what in enumerate(prepare):
            job(what, n, 1, "start", 0, 0)
        body(0, "first")
        with pe.Fori(1, BODIES - 1) as k:
            body(k, "mid")
        body(BODIES - 1, "last")
        for c in range(CHUNKS):
            pe.wait_ge(exp_done, (BATCH * PAIRS - 1) * CHUNKS + c + 1)
            turn(BODIES, "mid", 0, c)
        weigh_values(BODIES, -2, CHUNKS - 1)
        job(("norm",), base("last", BODIES - 1) + len(table["last"]), 0, "mid", BODIES, 3)
        for part in range(CHUNKS):
            weigh_values(BODIES, -1, part)
        if lay.last_output:
            job(("out",), base("last", BODIES - 1) + len(table["last"]) + 1, 0, "mid", BODIES, 5)

    @block.scalar
    def _(act):
        def take(what, n, m, q):
            act.wait_ge(scratch_ready, n + 1)
            if what[0] == "norm":
                if not (isinstance(q, int) and q == 0):
                    act.wait_ge(pv_taken, q)
                nc.scalar.activation(norm[:], scratch[:, 0:lay.norm_cols], ACT.Copy).then_inc(scratch_free, 1)
            else:
                lay.act_take(act, what, m)

        def at(k, kind, s, pos):
            if (s, pos) in table[kind]:
                what, n = table[kind][s, pos]
                take(what, base(kind, k) + n, (s // PAIRS + 1) % 2, 4 * k + (s - 7) // QUAD)

        def copy_turned(k, kind, s):
            pair = k * SLOTS + s - 1
            u, j = (s - 1) // QUAD % QUADS, (s - 1) % QUAD
            act.wait_ge(turned, pair * CHUNKS + 3)
            if j == 0 and not (kind == "first" and s < 2 * QUAD):
                act.wait_ge(pv_done, CHUNKS * (4 * k + (s - 1) // QUAD - 1))
            nc.scalar.activation(prob_t[u][:, 8:12, P * j:P * j + P], turn_ps[0][:].rearrange("p (t q) -> p t q", t=4),
                                 ACT.Copy).then_inc(copied_act, 1)

        def body(k, kind):
            for s in range(SLOTS):
                if not (kind == "first" and s == 0):
                    copy_turned(k, kind, s)
                at(k, kind, s, "b")
                pair, j = k * SLOTS + s, s % QUAD
                if not (kind == "first" and s < 2):
                    act.wait_ge(turned, (pair - 1) * CHUNKS)
                if j == 0 and not (kind == "first" and s < 2 * QUAD):
                    act.wait_ge(den_done, 4 * k + s // QUAD - 1)
                act.wait_ge(neg_max_done, pair + 1)
                for c in range(CHUNKS):
                    cols = quad_chunk(c, keys)
                    nc.scalar.activation(prob[s % 2][:, cols], score_ps[:, cols], ACT.Exp, bias=neg_max[:, s % 2:s % 2 + 1],
                                         accum_out=sums[:, (s // QUAD) % 2, j, c:c + 1]).then_inc(exp_done, 1)
                    if c == 1:
                        at(k, kind, s, "a")

        lay.act_start(act)
        for n, what in enumerate(prepare):
            take(what, n, 0, None)
        body(0, "first")
        with act.Fori(1, BODIES - 1) as k:
            body(k, "mid")
        body(BODIES - 1, "last")
        copy_turned(BODIES, "mid", 0)
        take(("norm",), base("last", BODIES - 1) + len(table["last"]), 0, 2 * BATCH - 1)

    @block.vector
    def _(dve):
        def maximum(k, s, c):
            dve.wait_ge(scores_ready, (k * SLOTS + s) * CHUNKS + c + 1)
            nc.vector.reduce_max(chunk_max[:, s % 2, c:c + 1], score_ps[:, quad_chunk(c, keys)], AX_X).then_inc(chunk_max_done, 1)

        def copy_turned(k, kind, s, c):
            pair = k * SLOTS + s - 1
            u, j = (s - 1) // QUAD % QUADS, (s - 1) % QUAD
            if c == 0 and j == 0 and not (kind == "first" and s < 2 * QUAD):
                dve.wait_ge(pv_done, CHUNKS * (4 * k + (s - 1) // QUAD - 1))
            dve.wait_ge(turned, pair * CHUNKS + c + 1)
            if c < 3:
                last = nc.vector.tensor_copy(prob_t[u][:, 4 * c:4 * c + 4, P * j:P * j + P],
                                             turn_ps[c][:].rearrange("p (t q) -> p t q", t=4))
            else:
                for i, (rows, _) in enumerate(groups[c]):
                    last = nc.vector.tensor_copy(prob_t[u][0:rows, 12 + i, P * j:P * j + P], turn_ps[1][0:rows, P * i:P * i + P])
            last.then_inc(copied_dve, 1)

        def denominators(q, par):
            dve.wait_ge(exp_done, (q + 1) * QUAD * CHUNKS)
            if not (isinstance(q, int) and q == 0):
                dve.wait_ge(diag_done, q)
            nc.vector.tensor_reduce(den[:], sums[:, par], AX_X, ALU.add).then_inc(den_done, 1)
            dve.wait_ge(den_done, q + 1)
            nc.vector.reciprocal(rden[:], den[:]).then_inc(rden_done, 1)

        def finish_quad(k, i, taken):
            q = 4 * k + i
            dve.wait_ge(pv_done, CHUNKS * (q + 1))
            dve.wait_ge(scratch_free, taken)
            lay.dve_finish(dve, q, i, k)

        def body(k, kind):
            for s in range(SLOTS):
                before = not (kind == "first" and s == 0)
                maximum(k, s, 0)
                if s and (s - 1, "a") in table[kind]:
                    lay.dve_take(dve, table[kind][s - 1, "a"], base(kind, k), k, kind, s - 1)
                if before:
                    copy_turned(k, kind, s, 0)
                for c in range(1, CHUNKS):
                    maximum(k, s, c)
                pair = k * SLOTS + s
                dve.wait_ge(chunk_max_done, (pair + 1) * CHUNKS)
                if not (kind == "first" and s < 2):
                    dve.wait_ge(exp_done, (pair - 1) * CHUNKS)
                nc.vector.tensor_reduce(neg_max[:, s % 2:s % 2 + 1], chunk_max[:, s % 2, :], AX_X, ALU.max,
                                        negate=True).then_inc(neg_max_done, 1)
                if (s, "b") in table[kind]:
                    lay.dve_take(dve, table[kind][s, "b"], base(kind, k), k, kind, s)
                if s % QUAD == 1 and not (kind == "first" and s < 9):
                    finish_quad(k, s // QUAD - 2, own.number_after(k, kind, s - 2, "a"))
                if before:
                    copy_turned(k, kind, s, 1)
                    copy_turned(k, kind, s, 3)
                if s % QUAD == 0 and before:
                    denominators(4 * k + s // QUAD - 1, (s // QUAD - 1) % 2)
                lay.dve_extra(dve, k, kind, s)

        lay.dve_start(dve)
        body(0, "first")
        with dve.Fori(1, BODIES - 1) as k:
            body(k, "mid")
        body(BODIES - 1, "last")
        for c in (0, 1, 3):
            copy_turned(BODIES, "mid", 0, c)
        denominators(2 * BATCH - 1, 1)
        finish_quad(BODIES, -2, own.number_after(BODIES - 1, "last", 15, "a"))
        finish_quad(BODIES, -1, base("last", BODIES - 1) + len(table["last"]) + 1)
        lay.dve_end(dve)


def cross_attention_0(nc, g, dram):
    SCALE = E0 ** -0.5
    N_LOADED = 16 * (2 + 8 + 1 + 2 * QUAD)
    lay = Named()
    lay.tag, lay.keys, lay.norm_cols, lay.last_output = "a_", CTX, P, False
    lay.tiles = [(P if t < FULL else TAIL, P * t) for t in range(FULL + 1)]
    widths = [min(BANK, CTX - BANK * c) for c in range(CHUNKS)]
    jobs = [("ctx_t", 0), ("ctx_t", 1), ("ctx_t", 2), ("ctx_t", 3), ("k", 0, 0), ("k", 0, 1), ("k", 0, 2), ("norm",),
            ("k", 1, 0), ("tail",), ("k", 1, 1), ("k", 1, 2), ("v", 0), ("v", 1), ("v", 2), ("norm",)]
    lay.jobs = [jobs, jobs]
    K_JOBS = 7
    k_number = {job: i for i, job in enumerate(j for j in jobs if j[0] in ("k", "tail"))}

    with ExitStack() as ctx:
        t = Named()

        def allocate(own):
            sb, sem = own.sb, own.sem
            lay.own = own
            t.xn = sb("xn", [P, TOK_TILES, D])
            t.xn_t = sb("xn_t", [P, TOKENS])
            t.stats = sb("stats", [P, TOK_TILES, 6])
            t.mean_var = sb("mean_var", [P, TOK_TILES, 2])
            t.rstd = sb("rstd", [P, TOK_TILES])
            t.half = sb("half", [P, TOK_TILES])
            t.wq2 = sb("wq2", [P, QUADS, 2, 64])
            t.wk2 = sb("wk2", [P, QUADS, 2, 64])
            t.wv = sb("wv", [P, D])
            t.bq2, t.bqs, t.bk2, t.bv_rows = (sb(n, [P, QUADS]) for n in ("bq2", "bqs", "bk2", "bv_rows"))
            t.q2 = sb("q2", [P, QUADS, TOKENS])
            t.q_hi = sb("q_hi", [P, QUADS, TOKENS])
            t.q_lo = sb("q_lo", [P, QUADS, TOKENS])
            t.q_bd = sb("q_bd", [P, 2, QUADS, 2, 8, SEQ], F32R)
            t.ctx = sb("ctx", [P, FULL + 1, D])
            t.ctx_t = sb("ctx_t", [P, CTX])
            t.k_sp = [[sb(f"k{m}{u}", [P, CTX + 1], F32R) for u in range(QUADS)] for m in range(2)]
            t.val = [sb(f"val{m}", [P, FULL + 1, D + 16]) for m in range(2)]
            t.heads = sb("heads", [P, P])
            t.loaded, t.ctx_loaded, t.zeroed, t.stat, t.aggr = (sem(n) for n in ("loaded", "ctx_loaded", "zeroed", "stat", "aggr"))
            t.eps, t.rstd_done, t.xn_done, t.xn_turned, t.xn_t_done = (sem(n) for n in ("eps", "rstd_done", "xn_done", "xn_turned", "xn_t_done"))
            t.q_proj, t.q_done, t.q_split, t.bqs_done, t.pads_set = (sem(n) for n in ("q_proj", "q_done", "q_split", "bqs_done", "pads_set"))
            t.q_bd_done, t.masked = (sem(n) for n in ("q_bd_done", "masked"))

        lay.allocate = allocate

        def load_ctx(sp, b):
            sp.dma_start(t.ctx[:, 0:FULL, :],
                         dram.ctx[bass.ds(b, 1), 0:FULL * P, :].rearrange("o (p t) d -> p (o t) d", t=FULL)).then_inc(t.ctx_loaded, 16)
            sp.dma_start(t.ctx[0:TAIL, FULL, :],
                         dram.ctx[bass.ds(b, 1), FULL * P:CTX, :].rearrange("o p d -> p (o d)")).then_inc(t.ctx_loaded, 16)

        def sync_start(sp):
            own = lay.own
            sp.dma_start(g.x_tok[:], dram.x.rearrange("(t b) s d -> (b s) t d", b=2)).then_inc(t.loaded, 16)
            sp.dma_start(g.consts[:], dram.consts).then_inc(t.loaded, 16)
            load_ctx(sp, 0)
            for half in range(2):
                rows = slice(64 * half, 64 * half + 64)
                for dst, src in ((t.bq2, dram.L0_xattn_bq), (t.bk2, dram.L0_xattn_bk)):
                    sp.dma_start(dst[rows, :], src.rearrange("(u r) -> r u", u=QUADS)).then_inc(t.loaded, 16)
                for dst, src in ((t.wq2, dram.L0_xattn_wq), (t.wk2, dram.L0_xattn_wk)):
                    sp.dma_start(dst[:, :, half, :], src.rearrange("d (u r) -> d u r", u=QUADS)).then_inc(t.loaded, 16)
            sp.dma_start(t.wv[:], dram.L0_xattn_wv).then_inc(t.loaded, 16)
            sp.wait_ge(t.zeroed, 5)
            for j in range(QUAD):
                sp.dma_start(t.bv_rows[32 * j:32 * j + 16, :],
                             dram.L0_xattn_bv.rearrange("(u j r) -> j r u", u=QUADS, j=QUAD)[j]).then_inc(t.loaded, 16)
                sp.dma_start(g.wo_rows[32 * j:32 * j + 16, :, :],
                             dram.L0_xattn_wo.rearrange("(u j r) n -> j r u n", u=QUADS, j=QUAD)[j]).then_inc(t.loaded, 16)
            sp.wait_ge(own.scratch_ready, CHUNKS)
            load_ctx(sp, 1)

        def sync_body(sp, k, kind):
            if kind != "last":
                for m in range(2):
                    sp.wait_ge(lay.own.scratch_ready, lay.own.number_after(k, kind, PAIRS * m + 1, "a"))
                    load_ctx(sp, 2 * k + m + 2)

        lay.sync_start, lay.sync_body, lay.sync_end = sync_start, sync_body, lambda sp: sp.wait_ge(t.loaded, N_LOADED)

        def block_diagonal(b, m):
            heads = g.consts[:, C_HEADROWS:C_HEADROWS + 8].unsqueeze(2).broadcast_to([P, 8, SEQ])
            for u in range(QUADS):
                for part, q in enumerate((t.q_hi, t.q_lo)):
                    mine = q[:, u, bass.ds(b * SEQ, SEQ)].unsqueeze(1).broadcast_to([P, 8, SEQ])
                    nc.gpsimd.tensor_tensor(t.q_bd[:, m, u, part], mine, heads, ALU.mult).then_inc(t.q_bd_done, 1)

        def pool_start(pool):
            nc.gpsimd.memset(t.half[:], -0.5).then_inc(t.zeroed, 1)
            nc.gpsimd.memset(t.bv_rows[:], 0.0).then_inc(t.zeroed, 1)
            nc.gpsimd.memset(g.wo_rows[:], 0.0).then_inc(t.zeroed, 1)
            for m in range(2):
                nc.gpsimd.memset(t.val[m][:, :, D:], 0.0).then_inc(t.zeroed, 1)
            pool.wait_ge(t.eps, 1)
            pool.wait_ge(t.zeroed, 5)
            nc.gpsimd.tensor_tensor(t.rstd[:], t.rstd[:], t.half[:], ALU.pow).then_inc(t.rstd_done, 1)
            pool.wait_ge(t.q_split, 2 * QUADS)
            block_diagonal(0, 0)

        def pool_prepare(pool, k, kind, m):
            b = 2 * k + m + 1
            if not (kind == "first" and m == 0):
                pool.wait_ge(lay.own.scores_ready, (b - 1) * PAIRS * CHUNKS)
            block_diagonal(b, (m + 1) % 2)

        lay.pool_start, lay.pool_prepare = pool_start, pool_prepare

        def q_bank(own, i):
            return (own.score_ps[:, 2 * BANK:3 * BANK], own.score_ps[:, 3 * BANK:4 * BANK], own.turn_ps[0][:], own.turn_ps[1][:])[i]

        def pe_start(pe):
            own = lay.own
            pe.wait_ge(t.loaded, N_LOADED)
            for i in range(TOK_TILES):
                pe.wait_ge(t.xn_done, i + 1)
                nc.tensor.transpose(own.score_ps[:, P * i:P * i + P], t.xn[:, i, :], g.consts[:, C_IDENT:C_IDENT + P]).then_inc(t.xn_turned, 1)
            for c in range(2):
                pe.wait_ge(t.xn_t_done, c + 1)
            for u in range(QUADS):
                for c in range(2):
                    nc.tensor.matmul(q_bank(own, 2 * u + c), t.wq2[:, u], t.xn_t[:, c * BANK:c * BANK + BANK],
                                     start=True, stop=True).then_inc(t.q_proj, 1)
            pe.wait_ge(t.q_done, 2 * QUADS)
            pe.wait_ge(t.pads_set, 2 * QUADS)

        def values(pe, tiles, c0):
            for i, (rows, col) in enumerate(tiles):
                last = nc.tensor.matmul(lay.own.scratch[0:rows, c0 + P * i:c0 + P * i + D], t.ctx_t[:, col:col + rows], t.wv[:],
                                        start=True, stop=True)
            return last

        def pe_job(pe, what, m, kind, k, s):
            scratch = lay.own.scratch
            if what[0] == "ctx_t":
                c = what[1]
                if c == 0:
                    pe.wait_ge(t.ctx_loaded, 32 if kind == "start" else (2 * k + m + 2) * 32)
                for i in range(4 * c, min(4 * c + 4, FULL + 1)):
                    rows = lay.tiles[i][0]
                    last = nc.tensor.transpose(scratch[:, P * (i - 4 * c):P * (i - 4 * c) + rows], t.ctx[0:rows, i, :],
                                               g.consts[0:rows, C_IDENT:C_IDENT + rows])
                return last
            if what[0] == "k":
                _, u, c = what
                return nc.tensor.matmul(scratch[:, 0:BANK], t.wk2[:, u], t.ctx_t[:, quad_chunk(c, CTX)], start=True, stop=True)
            if what[0] == "v":
                return values(pe, lay.tiles[4 * what[1]:4 * what[1] + 4], 0)
            for u in range(QUADS):
                nc.tensor.matmul(scratch[:, P * u:P * u + TAIL], t.wk2[:, u], t.ctx_t[:, quad_chunk(3, CTX)], start=True, stop=True)
            return values(pe, lay.tiles[FULL:], 2 * P)

        def pe_norm(pe, diag):
            for j in range(QUAD):
                last = nc.tensor.matmul(lay.own.scratch[32 * j:32 * j + 32, 0:P], g.consts[:, C_PAIRROWS:C_PAIRROWS + 32],
                                        diag[:, j, :], start=True, stop=True)
            return last

        def pe_operands_ready(pe, k, kind, m, u):
            pe.wait_ge(t.q_bd_done, (2 * k + m) * 4 + 2 * u + 2)
            if u == 0 and not (kind == "first" and m == 0):
                pe.wait_ge(lay.own.scratch_free, lay.own.number_after(k, kind, PAIRS * m - 1, "b"))
            elif u == 0:
                pe.wait_ge(lay.own.scratch_free, len(jobs) - 2)

        def pe_values(pe, m, u, tiles):
            for i in tiles:
                rows = lay.tiles[i][0]
                for j in range(QUAD):
                    v0 = 16 * (QUAD * u + j)
                    last = nc.tensor.matmul(lay.own.pv_ps[32 * j:32 * j + 32, 0:P], t.val[m][0:rows, i, v0:v0 + 32],
                                            lay.own.prob_t[u][0:rows, i, P * j:P * j + P], start=(i == 0), stop=(i == FULL))
            return last

        lay.pe_start, lay.pe_job, lay.pe_norm = pe_start, pe_job, pe_norm
        lay.pe_operands_ready, lay.pe_values = pe_operands_ready, pe_values
        lay.score_passes = lambda m, u, j: [(t.q_bd[:, m, u, part, 2 * j:2 * j + 2, :], t.k_sp[m][u]) for part in range(2)]

        def act_start(act):
            own = lay.own
            act.wait_ge(t.loaded, N_LOADED)
            act.wait_ge(t.bqs_done, 1)
            for u in range(QUADS):
                for c in range(2):
                    act.wait_ge(t.q_proj, 2 * u + c + 1)
                    nc.scalar.activation(t.q2[:, u, c * BANK:c * BANK + BANK], q_bank(own, 2 * u + c), ACT.Identity,
                                         bias=t.bqs[:, u:u + 1], scale=SCALE).then_inc(t.q_done, 1)

        def act_take(act, what, m):
            own = lay.own
            scratch = own.scratch
            if what[0] == "ctx_t":
                c = what[1]
                nc.scalar.activation(t.ctx_t[:, quad_chunk(c, CTX)], scratch[:, 0:widths[c]], ACT.Copy).then_inc(own.scratch_free, 1)
            elif what[0] == "k":
                _, u, c = what
                nc.scalar.activation(t.k_sp[m][u][:, quad_chunk(c, CTX)], scratch[:, 0:BANK], ACT.Identity,
                                     bias=t.bk2[:, u:u + 1]).then_inc(own.half_taken, 1)
            elif what[0] == "v":
                c = what[1]
                nc.scalar.activation(t.val[m][:, 4 * c:4 * c + 4, 0:D], scratch[:].rearrange("p (t d) -> p t d", t=4),
                                     ACT.Copy).then_inc(own.scratch_free, 1)
            else:
                nc.scalar.activation(t.val[m][0:TAIL, FULL, 0:D], scratch[0:TAIL, 2 * P:3 * P], ACT.Copy)
                for u in range(QUADS):
                    last = nc.scalar.activation(t.k_sp[m][u][:, quad_chunk(3, CTX)], scratch[:, P * u:P * u + TAIL], ACT.Identity,
                                                bias=t.bk2[:, u:u + 1])
                last.then_inc(own.half_taken, 1)

        lay.act_start, lay.act_take = act_start, act_take

        def keys_low(dve, what, b, m):
            own = lay.own
            dve.wait_ge(own.half_taken, K_JOBS * b + k_number[what] + 1)
            parts = [(what[1], what[2], 0)] if what[0] == "k" else [(u, 3, P * u) for u in range(QUADS)]
            for u, c, c0 in parts:
                lo = t.k_sp[m][u][64:P, quad_chunk(c, CTX)]
                last = nc.vector.scalar_tensor_tensor(lo, own.scratch[64:P, c0:c0 + widths[c]], t.bk2[64:P, u:u + 1], lo.bitcast(F32),
                                                      ALU.add, ALU.subtract)
            last.then_inc(own.scratch_free, 1)

        def dve_take(dve, entry, base, k, kind, s):
            what = entry[0]
            if what[0] in ("k", "tail"):
                m = s // PAIRS
                keys_low(dve, what, 2 * k + m + 1, (m + 1) % 2)

        def dve_start(dve):
            own = lay.own
            for m in range(2):
                for u in range(QUADS):
                    nc.vector.memset(t.k_sp[m][u][:, CTX:CTX + 1].bitcast(U32), 0).then_inc(t.pads_set, 1)
            dve.wait_ge(t.loaded, N_LOADED)
            nc.vector.tensor_scalar(t.bqs[:], t.bq2[:], SCALE, None, ALU.mult).then_inc(t.bqs_done, 1)
            for i in range(TOK_TILES):
                nc.vector.bn_stats(t.stats[:, i, :], g.x_tok[:, i, :]).then_inc(t.stat, 1)
            dve.wait_ge(t.stat, TOK_TILES)
            for i in range(TOK_TILES):
                nc.vector.bn_aggr(t.mean_var[:, i, :], t.stats[:, i, :]).then_inc(t.aggr, 1)
            dve.wait_ge(t.aggr, TOK_TILES)
            nc.vector.tensor_scalar(t.rstd[:], t.mean_var[:, :, 1], LN_EPS, None, ALU.add).then_inc(t.eps, 1)
            dve.wait_ge(t.rstd_done, 1)
            for i in range(TOK_TILES):
                nc.vector.tensor_scalar(t.xn[:, i, :], g.x_tok[:, i, :], t.mean_var[:, i, 0:1], t.rstd[:, i:i + 1],
                                        ALU.subtract, ALU.mult).then_inc(t.xn_done, 1)
            for c in range(2):
                dve.wait_ge(t.xn_turned, 4 * c + 4)
                nc.vector.tensor_copy(t.xn_t[:, c * BANK:c * BANK + BANK], own.score_ps[:, c * BANK:c * BANK + BANK]).then_inc(t.xn_t_done, 1)
            for u in range(QUADS):
                dve.wait_ge(t.q_done, 2 * u + 2)
                nc.vector.tensor_copy(t.q_hi[:, u, :].bitcast(F32R), t.q2[:, u, :]).then_inc(t.q_split, 1)
                dve.wait_ge(t.q_split, 2 * u + 1)
                nc.vector.tensor_tensor(t.q_lo[:, u, :], t.q2[:, u, :], t.q_hi[:, u, :], ALU.subtract).then_inc(t.q_split, 1)
            for what in jobs:
                if what[0] in ("k", "tail"):
                    keys_low(dve, what, 0, 0)

        def dve_finish(dve, q, i, k):
            own = lay.own
            b, u = 2 * k + i // QUADS, i % QUADS
            nc.vector.tensor_tensor(t.heads[:], own.pv_ps[:, 0:P], own.norm[:], ALU.mult).then_inc(t.masked, 1)
            dve.wait_ge(t.masked, q + 1)
            nc.vector.scalar_tensor_tensor(g.act_t[:, u, bass.ds(b * SEQ, SEQ)], t.heads[:, 0:SEQ], t.bv_rows[:, u:u + 1],
                                           t.heads[:, SEQ:P], ALU.add, ALU.add).then_inc(own.pv_taken, 1)

        lay.dve_start, lay.dve_take, lay.dve_finish = dve_start, dve_take, dve_finish
        lay.dve_extra, lay.dve_end = (lambda *a: None), (lambda dve: None)
        attend(nc, g, lay, ctx)


WIDTH = 2
ROUNDS = TOK_TILES // WIDTH


def scope(nc, ctx, tag):
    def sb(name, shape, dt=F32):
        return ctx.enter_context(nc.sbuf_tensor(tag + name, shape, dt))

    def pair(name, shape, dt=F32):
        return [sb(f"{name}{j}", shape, dt) for j in range(WIDTH)]

    def bank(name, shape):
        return [ctx.enter_context(nc.psum_tensor(f"{tag}{name}{j}", shape, F32)) for j in range(WIDTH)]

    sem = semaphores_of_part(nc, ctx, tag)

    def sems(names):
        return [sem(n) for n in names.split()]

    return sb, pair, bank, sem, sems


def tile_of(x_tok, tile):
    return x_tok[:, bass.ds(tile, 1), :].rearrange("p o d -> p (o d)")


def wait_apart(engine, sem, count, waits):
    engine.wait_ge(sem, count)
    engine.sem_inc(waits, 1)


class Norm:

    def __init__(self, nc, name, pair, sem, half, waits):
        self.nc, self.half, self.waits = nc, half, waits
        self.stats, self.mean_var, self.eps, self.rstd = (pair(name + n, shape) for n, shape in (
            ("_stats", [P, 6]), ("_mean_var", [P, 2]), ("_eps", [P, 1]), ("_rstd", [P, 1])))
        self.out = pair(name + "_out", [P, D])
        self.stat_done, self.aggr_done, self.eps_done, self.rstd_done, self.done = (
            sem(f"{name}_{n}") for n in ("stat_done", "aggr_done", "eps_done", "rstd_done", "done"))

    def statistics(self, dve, j, count, rows):
        self.nc.vector.bn_stats(self.stats[j][:], rows).then_inc(self.stat_done, 1)
        wait_apart(dve, self.stat_done, count, self.waits)
        self.nc.vector.bn_aggr(self.mean_var[j][:], self.stats[j][:]).then_inc(self.aggr_done, 1)
        dve.wait_ge(self.aggr_done, count)
        self.nc.vector.tensor_scalar(self.eps[j][:], self.mean_var[j][:, 1:2], LN_EPS, None, ALU.add).then_inc(self.eps_done, 1)

    def root(self, pool, j, count):
        pool.wait_ge(self.eps_done, count)
        self.nc.gpsimd.tensor_tensor(self.rstd[j][:], self.eps[j][:], self.half[:], ALU.pow).then_inc(self.rstd_done, 1)

    def normalise(self, dve, j, count, rows):
        dve.wait_ge(self.rstd_done, count)
        self.nc.vector.tensor_scalar(self.out[j][:], rows, self.mean_var[j][:, 0:1], self.rstd[j][:], ALU.subtract,
                                     ALU.mult).then_inc(self.done, 1)


def fold_resampler_weights(nc, g, dram):
    TURNED = 3 * PAIRS
    with ExitStack() as ctx:
        sb, _, _, _, sems = scope(nc, ctx, "f_")
        raw, raw_o = sb("raw", [P, TURNED, P]), sb("raw_o", [P, PAIRS, D])
        turned = sb("turned", [P, TURNED, P])
        ps = [ctx.enter_context(nc.psum_tensor(f"f_ps{i}", [P, 4, P], F32)) for i in range(2)]
        s = Named()
        s.loaded, s.turned, s.copied, s.made, s.taken = sems("loaded turned copied made taken")
        GROUPS = TURNED // 4
        ctx.enter_context(nc.allow_non_contiguous_dma(reason="small vectors and permuted weights"))
        block = ctx.enter_context(nc.Block())

        @block.sync
        def _(sp):
            sp.dma_start(raw[:, 0:PAIRS, :], dram.L1_xattn_Wq.rearrange("d (n k) -> d n k", k=P)).then_inc(s.loaded, 16)
            sp.dma_start(raw[:, PAIRS:TURNED, :], dram.L1_xattn_Wkv.rearrange("d (n k) -> d n k", k=P)).then_inc(s.loaded, 16)
            sp.dma_start(raw_o[:], dram.L1_xattn_Wo.rearrange("(n k) d -> k n d", k=P)).then_inc(s.loaded, 16)

        @block.tensor
        def _(pe):
            pe.wait_ge(s.loaded, 48)
            for i in range(GROUPS):
                if i >= 2:
                    pe.wait_ge(s.copied, i - 1)
                for n in range(4):
                    last = nc.tensor.transpose(ps[i % 2][:, n, :], raw[:, 4 * i + n, :], g.consts[:, C_IDENT:C_IDENT + P])
                last.then_inc(s.turned, 1)
            pe.wait_ge(s.copied, GROUPS)
            for i in range(HEADS // 2):
                if i >= 2:
                    pe.wait_ge(s.taken, i - 1)
                half = slice(64 * (i % 2), 64 * (i % 2) + 64)
                for n in range(2):
                    b = 2 * (i // 2) + n
                    nc.tensor.matmul(ps[i % 2][:, n, :], turned[half, b, :], turned[half, PAIRS + b, :], start=True, stop=True)
                    last = nc.tensor.matmul(ps[i % 2][:, 2 + n, :], turned[half, 2 * PAIRS + b, :], raw_o[half, b, :],
                                            start=True, stop=True)
                last.then_inc(s.made, 1)

        @block.scalar
        def _(act):
            for i in range(0, GROUPS, 2):
                act.wait_ge(s.turned, i + 1)
                nc.scalar.activation(turned[:, 4 * i:4 * i + 4, :], ps[0][:], ACT.Copy).then_inc(s.copied, 1)
                act.wait_ge(s.copied, i + 2)

        @block.vector
        def _(dve):
            for i in range(1, GROUPS, 2):
                dve.wait_ge(s.turned, i + 1)
                dve.wait_ge(s.copied, i)
                nc.vector.tensor_copy(turned[:, 4 * i:4 * i + 4, :], ps[1][:]).then_inc(s.copied, 1)
            for i in range(HEADS // 2):
                heads = slice(i // 2 * 4 + i % 2, i // 2 * 4 + i % 2 + 3, 2)
                dve.wait_ge(s.made, i + 1)
                nc.vector.tensor_copy(g.qk[:, heads, :], ps[i % 2][:, 0:2, :])
                nc.vector.tensor_copy(g.wvo[:, heads, :], ps[i % 2][:, 2:4, :]).then_inc(s.taken, 1)


def rest_of_layer_0(nc, g, dram):
    EXPERTS = 8
    SCALE = E0 ** -0.5
    with ExitStack() as ctx:
        sb, pair, bank, sem, sems = scope(nc, ctx, "b_")
        ident = g.consts[:, C_IDENT:C_IDENT + P]
        raw = sb("raw", [P, 4, D])
        router = sb("router", [EXPERTS, D])
        w_t = sb("w_t", [P, 4, D])
        w_swap = sb("w_swap", [P, 2, D])
        router_t = sb("router_t", [P, EXPERTS])
        w1, w2 = sb("w1", [P, EXPERTS, P]), sb("w2", [P, EXPERTS, D])
        bo, ln2_w, ln2_b = sb("bo", [P, D]), sb("ln2_w", [P, D]), sb("ln2_b", [P, D])
        half = sb("half", [P, 1])
        heads_t = pair("heads_t", [P, QUADS, P])
        x1, x2, x3 = pair("x1", [P, D]), pair("x2", [P, D]), pair("x3", [P, D])
        xn_t, xn2_t, lat_t = pair("xn_t", [P, P]), pair("xn2_t", [P, P]), pair("lat_t", [P, P])
        rot1, rot2, kq = pair("rot1", [P, 4, SEQ]), pair("rot2", [P, 4, SEQ]), pair("kq", [P, 4, SEQ])
        k_bd = pair("k_bd", [P, 2, 4, SEQ])
        q_bd = pair("q_bd", [P, 4, 2, SEQ])
        v_bd = pair("v_bd", [P, 2 * PAIRS, 16])
        sc = pair("sc", [P, HEADS, SEQ])
        top, den, rden = pair("top", [P, HEADS]), pair("den", [P, HEADS]), pair("rden", [P, HEADS])
        prob_t = pair("prob_t", [P, PAIRS, P])
        attn, attn_t = pair("attn", [P, D]), pair("attn_t", [P, P])
        gate = pair("gate", [P, EXPERTS])
        best, place, place_f = pair("best", [P, 8]), pair("place", [P, 8], U32), pair("place_f", [P, 2])
        total, share = pair("total", [P, 1]), pair("share", [P, 2])
        cw1, cw = pair("cw1", [P, EXPERTS]), pair("cw", [P, EXPERTS])
        relu, act = pair("relu", [P, EXPERTS, P]), pair("act", [P, EXPERTS, P])
        weighted, mixed = pair("weighted", [P, EXPERTS, D]), pair("mixed", [P, D])
        lat_w, lat = pair("lat_w", [P, D]), pair("lat", [P, D])
        q_out = pair("q_out", [P, 2, HEADS, SEQ])
        ps_a, ps_b, ps_c = bank("ps_a", [P, BANK]), bank("ps_b", [P, BANK]), bank("ps_c", [P, 2 * BANK])
        s = Named()
        s.waits, s.loaded, s.half_set, s.w_turned, s.w_copied = sems("waits loaded half_set w_turned w_copied")
        s.w_swapped, s.staged, s.projected, s.x1_part, s.x1_done = sems("w_swapped staged projected x1_part x1_done")
        s.xn_turned, s.xn_copied, s.qkv_done, s.rot1_done, s.rot2_done = sems("xn_turned xn_copied qkv_done rot1_done rot2_done")
        s.kq_done, s.k_bd_done, s.q_bd_done, s.v_bd_done, s.scored = sems("kq_done k_bd_done q_bd_done v_bd_done scored")
        s.scaled, s.max_done, s.shifted, s.exp_done, s.den_done = sems("scaled max_done shifted exp_done den_done")
        s.rden_done, s.p_turned, s.p_copied, s.weighed, s.attn_done = sems("rden_done p_turned p_copied weighed attn_done")
        s.attn_turned, s.attn_copied, s.attended, s.x2_done, s.xn2_turned = sems("attn_turned attn_copied attended x2_done xn2_turned")
        s.xn2_copied, s.routed, s.gated, s.best_done, s.place_done = sems("xn2_copied routed gated best_done place_done")
        s.placef_done, s.total_done, s.inverse_done, s.share_done, s.cw1_done = sems("placef_done total_done inverse_done share_done cw1_done")
        s.cw_done, s.hidden, s.relu_done, s.act_done, s.expert_done = sems("cw_done hidden relu_done act_done expert_done")
        s.weighted_done, s.mixed_done, s.x3_done, s.latw_done, s.lat_done = sems("weighted_done mixed_done x3_done latw_done lat_done")
        s.rows_copied, s.lat_turned, s.lat_copied, s.q_made, s.q_copied = sems("rows_copied lat_turned lat_copied q_made q_copied")
        s.stored = sem("stored")
        ln_a, ln_b, ln_c, ln_d = (Norm(nc, n, pair, sem, half, s.waits) for n in ("ln_a", "ln_b", "ln_c", "ln_d"))
        tiles = range(WIDTH)
        LOADS = 16 * 8
        ctx.enter_context(nc.allow_non_contiguous_dma(reason="small vectors and permuted weights"))
        block = ctx.enter_context(nc.Block())

        @block.sync
        def _(sp):
            sp.dma_start(raw[:, 0:3, :], dram.L0_attn_W_KQV.rearrange("(m k) d -> k m d", k=P)).then_inc(s.loaded, 16)
            sp.dma_start(raw[:, 3, :], dram.L0_attn_W_O).then_inc(s.loaded, 16)
            sp.dma_start(router[:], dram.L0_ffn_router_w).then_inc(s.loaded, 16)
            sp.dma_start(w1[:], dram.L0_ffn_w1.rearrange("d (e w) -> d e w", e=EXPERTS)).then_inc(s.loaded, 16)
            sp.dma_start(w2[:], dram.L0_ffn_w2.rearrange("(e w) d -> w e d", e=EXPERTS)).then_inc(s.loaded, 16)
            sp.dma_start(bo[:], dram.L0_xattn_bo.partition_broadcast(P)).then_inc(s.loaded, 16)
            sp.dma_start(ln2_w[:], dram.L1_xattn_ln2_w.partition_broadcast(P)).then_inc(s.loaded, 16)
            sp.dma_start(ln2_b[:], dram.L1_xattn_ln2_b.partition_broadcast(P)).then_inc(s.loaded, 16)
            sp.sem_inc(s.stored, 16)
            with sp.Fori(0, ROUNDS) as k:
                for j in tiles:
                    sp.wait_ge(s.q_copied, 4 * k + 2 + j + 1)
                    for b in range(2):
                        sp.dma_start(dram.q1[bass.ds(2 * (2 * k + j) + b, 1)].rearrange("o p n -> p (o n)"),
                                     q_out[j][:, b].rearrange("p h q -> p (h q)")).then_inc(s.stored, 16)
            sp.wait_ge(s.stored, 16 * (BATCH + 1))

        @block.tensor
        def _(pe):
            def turn(out, block):
                return nc.tensor.transpose(out, block, ident)

            pe.wait_ge(s.loaded, LOADS)
            for i in range(4):
                turn(ps_b[0][:, P * i:P * i + P], raw[:, i, :])
            nc.tensor.transpose(ps_a[0][:, 0:EXPERTS], router[:], g.consts[0:EXPERTS, C_IDENT:C_IDENT + EXPERTS]).then_inc(s.w_turned, 1)
            pe.wait_ge(s.w_swapped, 2)
            with pe.Fori(0, ROUNDS) as k:
                for j in tiles:
                    pe.wait_ge(s.staged, 2 * k + j + 1)
                    for u in range(QUADS):
                        mm = nc.tensor.matmul(ps_a[j][:, 0:D], heads_t[j][:, u], g.wo_rows[:, u], start=(u == 0), stop=(u == QUADS - 1))
                    mm.then_inc(s.projected, 1)
                for j in tiles:
                    pe.wait_ge(ln_a.done, 2 * k + j + 1)
                    turn(ps_a[j][:, 128:256], ln_a.out[j][:]).then_inc(s.xn_turned, 1)
                for j in tiles:
                    pe.wait_ge(s.xn_copied, 2 * k + j + 1)
                    for i, w in enumerate((w_t[:, 0], w_t[:, 1], w_swap[:, 0], w_swap[:, 1])):
                        nc.tensor.matmul(ps_b[j][:, P * i:P * i + P], w, xn_t[j][:], start=True, stop=True)
                    for b in range(2):
                        for h in range(2):
                            mm = nc.tensor.matmul(ps_a[j][64 * h:64 * h + 64, 256 + P * b:256 + P * b + P],
                                                  xn_t[j][:, 64 * b:64 * b + 64], w_t[:, 2], start=True, stop=True)
                    mm.then_inc(s.qkv_done, 1)
                for j in tiles:
                    pe.wait_ge(s.k_bd_done, 2 * k + j + 1)
                    pe.wait_ge(s.q_bd_done, 2 * k + j + 1)
                    for b in range(2):
                        for r in range(4):
                            mm = nc.tensor.matmul(ps_c[j][64 * b:64 * b + 64, 256 * r:256 * r + 256], q_bd[j][:, r, b, :],
                                                  k_bd[j][:, b].rearrange("p h k -> p (h k)"), start=True, stop=True)
                    mm.then_inc(s.scored, 1)
                for j in tiles:
                    pe.wait_ge(s.exp_done, 2 * k + j + 1)
                    for i in range(PAIRS):
                        mm = turn(ps_c[j][:, P * i:P * i + P], sc[j][:, 2 * i:2 * i + 2, :].rearrange("p h k -> p (h k)"))
                    mm.then_inc(s.p_turned, 1)
                for j in tiles:
                    pe.wait_ge(s.p_copied, 2 * k + j + 1)
                    pe.wait_ge(s.v_bd_done, 2 * k + j + 1)
                    for b in range(2):
                        for i in range(PAIRS):
                            mm = nc.tensor.matmul(ps_b[j][64 * b:64 * b + 64, 16 * i:16 * i + 16], prob_t[j][:, i, 64 * b:64 * b + 64],
                                                  v_bd[j][:, PAIRS * b + i, :], start=True, stop=True)
                    mm.then_inc(s.weighed, 1)
                for j in tiles:
                    pe.wait_ge(s.attn_done, 2 * k + j + 1)
                    turn(ps_b[j][:, 128:256], attn[j][:]).then_inc(s.attn_turned, 1)
                for j in tiles:
                    pe.wait_ge(s.attn_copied, 2 * k + j + 1)
                    nc.tensor.matmul(ps_b[j][:, 256:384], attn_t[j][:], w_t[:, 3], start=True, stop=True).then_inc(s.attended, 1)
                for j in tiles:
                    pe.wait_ge(ln_b.done, 2 * k + j + 1)
                    turn(ps_b[j][:, 384:512], ln_b.out[j][:]).then_inc(s.xn2_turned, 1)
                for j in tiles:
                    pe.wait_ge(s.xn2_copied, 2 * k + j + 1)
                    nc.tensor.matmul(ps_a[j][:, 0:EXPERTS], xn2_t[j][:], router_t[:], start=True, stop=True).then_inc(s.routed, 1)
                    for e in range(EXPERTS):
                        mm = nc.tensor.matmul(ps_c[j][:, P * e:P * e + P], w1[:, e, :], xn2_t[j][:], start=True, stop=True)
                    mm.then_inc(s.hidden, 1)
                for j in tiles:
                    pe.wait_ge(s.act_done, 2 * k + j + 1)
                    for e in range(EXPERTS):
                        mm = nc.tensor.matmul(ps_c[j][:, P * e:P * e + P], act[j][:, e, :], w2[:, e, :], start=True, stop=True)
                    mm.then_inc(s.expert_done, 1)
                for j in tiles:
                    pe.wait_ge(s.lat_done, 2 * k + j + 1)
                    turn(ps_a[j][:, 128:256], lat[j][:]).then_inc(s.lat_turned, 1)
                for part in range(2):
                    for j in tiles:
                        pe.wait_ge(s.lat_copied, 2 * k + j + 1)
                        if part:
                            pe.wait_ge(s.q_copied, 2 * 2 * k + j + 1)
                        for h in range(8):
                            mm = nc.tensor.matmul(ps_c[j][:, P * h:P * h + P], g.qk[:, 8 * part + h, :], lat_t[j][:], start=True, stop=True)
                        mm.then_inc(s.q_made, 1)

        @block.scalar
        def _(sc_e):
            def copy(out, in_, done, **kw):
                nc.scalar.activation(out, in_, ACT.Copy, **kw).then_inc(done, 1)

            sc_e.wait_ge(s.w_turned, 1)
            copy(w_t[:].rearrange("p m k -> p (m k)"), ps_b[0][:], s.w_copied)
            copy(router_t[:], ps_a[0][:, 0:EXPERTS], s.w_copied)
            with sc_e.Fori(0, ROUNDS) as k:
                sc_e.wait_ge(s.stored, 16 * (4 * k + 1))
                sc_e.wait_ge(s.rows_copied, 2 * k + 1)
                for j in tiles:
                    copy(heads_t[j][:], g.act_t[:, :, bass.ds(P * (2 * k + j), P)], s.staged)
                for j in tiles:
                    sc_e.wait_ge(s.xn_turned, 2 * k + j + 1)
                    copy(xn_t[j][:], ps_a[j][:, 128:256], s.xn_copied)
                for j in tiles:
                    sc_e.wait_ge(s.shifted, 2 * k + j + 1)
                    nc.scalar.activation(sc[j][:], sc[j][:], ACT.Exp).then_inc(s.exp_done, 1)
                for j in tiles:
                    sc_e.wait_ge(s.p_turned, 2 * k + j + 1)
                    copy(prob_t[j][:].rearrange("p i q -> p (i q)"), ps_c[j][:], s.p_copied)
                for j in tiles:
                    sc_e.wait_ge(s.attn_turned, 2 * k + j + 1)
                    copy(attn_t[j][:], ps_b[j][:, 128:256], s.attn_copied)
                for j in tiles:
                    sc_e.wait_ge(s.xn2_turned, 2 * k + j + 1)
                    copy(xn2_t[j][:], ps_b[j][:, 384:512], s.xn2_copied)
                for j in tiles:
                    sc_e.wait_ge(s.routed, 2 * k + j + 1)
                    nc.scalar.activation(gate[j][:], ps_a[j][:, 0:EXPERTS], ACT.Sigmoid).then_inc(s.gated, 1)
                for j in tiles:
                    sc_e.wait_ge(s.hidden, 2 * k + j + 1)
                    nc.scalar.activation(relu[j][:].rearrange("p e w -> p (e w)"), ps_c[j][:], ACT.Relu).then_inc(s.relu_done, 1)
                for j in tiles:
                    sc_e.wait_ge(s.lat_turned, 2 * k + j + 1)
                    copy(lat_t[j][:], ps_a[j][:, 128:256], s.lat_copied)
                for part in range(2):
                    for j in tiles:
                        sc_e.wait_ge(s.q_made, 2 * 2 * k + 2 * part + j + 1)
                        copy(q_out[j][:, :, 8 * part:8 * part + 8, :], ps_c[j][:].rearrange("p (h b q) -> p b h q", h=8, b=2),
                             s.q_copied, scale=SEQ ** -0.5)

        @block.gpsimd
        def _(pool):
            nc.gpsimd.memset(half[:], -0.5).then_inc(s.half_set, 1)
            pool.wait_ge(s.half_set, 1)
            pool.wait_ge(s.loaded, LOADS)
            with pool.Fori(0, ROUNDS) as k:
                pool.wait_ge(s.stored, 16 * (4 * k + 1))
                pool.wait_ge(s.rows_copied, 2 * k + 1)
                for j in tiles:
                    ln_a.root(pool, j, 2 * k + j + 1)
                for j in tiles:
                    pool.wait_ge(s.rot1_done, 2 * k + j + 1)
                    pool.wait_ge(s.rot2_done, 2 * k + j + 1)
                    nc.gpsimd.tensor_tensor(kq[j][:], rot1[j][:], rot2[j][:], ALU.add).then_inc(s.kq_done, 1)
                for ln in (ln_b, ln_c, ln_d):
                    for j in tiles:
                        ln.root(pool, j, 2 * k + j + 1)
                for j in tiles:
                    pool.wait_ge(ln_d.done, 2 * k + j + 1)
                    nc.gpsimd.tensor_tensor(lat_w[j][:], ln_d.out[j][:], ln2_w[:], ALU.mult).then_inc(s.latw_done, 1)
                    pool.wait_ge(s.latw_done, 2 * k + j + 1)
                    nc.gpsimd.tensor_tensor(lat[j][:], lat_w[j][:], ln2_b[:], ALU.add).then_inc(s.lat_done, 1)

        @block.vector
        def _(dve):
            tt, ts, stt, reduce = nc.vector.tensor_tensor, nc.vector.tensor_scalar, nc.vector.scalar_tensor_tensor, nc.vector.tensor_reduce
            dve.wait_ge(s.w_copied, 2)
            dve.wait_ge(s.loaded, LOADS)
            for odd in range(2):
                nc.vector.tensor_copy(w_swap[:].rearrange("p m (r o) -> p m r o", o=2)[:, :, :, odd],
                                      w_t[:, 0:2].rearrange("p m (r o) -> p m r o", o=2)[:, :, :, 1 - odd]).then_inc(s.w_swapped, 1)
            cos, sin = (g.consts[:, c:c + SEQ].unsqueeze(1).broadcast_to([P, 4, SEQ]) for c in (C_COS, C_SIN))
            causal = g.consts[:, C_CAUSAL:C_CAUSAL + SEQ].unsqueeze(1).broadcast_to([P, HEADS, SEQ])
            iota = g.consts[:, C_IOTA:C_IOTA + EXPERTS]
            dve.sem_inc(s.rows_copied, 1)
            with dve.Fori(0, ROUNDS) as k:
                dve.wait_ge(s.stored, 16 * (4 * k + 1))
                dve.wait_ge(s.rows_copied, 2 * k + 1)
                for j in tiles:
                    n = 2 * k + j + 1
                    dve.wait_ge(s.projected, n)
                    tt(x1[j][:], ps_a[j][:, 0:D], tile_of(g.x_tok, 2 * k + j), ALU.add).then_inc(s.x1_part, 1)
                    dve.wait_ge(s.x1_part, n)
                    tt(x1[j][:], x1[j][:], bo[:], ALU.add).then_inc(s.x1_done, 1)
                for j in tiles:
                    dve.wait_ge(s.x1_done, 2 * k + j + 1)
                    ln_a.statistics(dve, j, 2 * k + j + 1, x1[j][:])
                for j in tiles:
                    ln_a.normalise(dve, j, 2 * k + j + 1, x1[j][:])
                for j in tiles:
                    dve.wait_ge(s.qkv_done, 2 * k + j + 1)
                    tt(rot1[j][:], ps_b[j][:, 0:256].rearrange("p (m q) -> p m q", q=SEQ), cos, ALU.mult).then_inc(s.rot1_done, 1)
                    tt(rot2[j][:], ps_b[j][:, 256:512].rearrange("p (m q) -> p m q", q=SEQ), sin, ALU.mult).then_inc(s.rot2_done, 1)
                for j in tiles:
                    tt(v_bd[j][:], ps_a[j][:, 256:512].rearrange("p (m r) -> p m r", r=16),
                       g.consts[:, C_PAIRROWS:C_PAIRROWS + 16].unsqueeze(1).broadcast_to([P, 2 * PAIRS, 16]), ALU.mult).then_inc(s.v_bd_done, 1)
                for j in tiles:
                    dve.wait_ge(s.kq_done, 2 * k + j + 1)
                    tt(k_bd[j][:], kq[j][:, 0:2, :].unsqueeze(2).broadcast_to([P, 2, 4, SEQ]),
                       g.consts[:, C_QUADROWS:C_QUADROWS + 4].unsqueeze(1).unsqueeze(3).broadcast_to([P, 2, 4, SEQ]),
                       ALU.mult).then_inc(s.k_bd_done, 1)
                    tt(q_bd[j][:], kq[j][:, 2:4, :].unsqueeze(1).broadcast_to([P, 4, 2, SEQ]),
                       g.consts[:, C_GROUPROWS:C_GROUPROWS + 4].unsqueeze(2).unsqueeze(3).broadcast_to([P, 4, 2, SEQ]),
                       ALU.mult).then_inc(s.q_bd_done, 1)
                for j in tiles:
                    dve.wait_ge(s.scored, 2 * k + j + 1)
                    stt(sc[j][:], ps_c[j][:].rearrange("p (h q) -> p h q", q=SEQ), SCALE, causal, ALU.mult, ALU.add).then_inc(s.scaled, 1)
                for j in tiles:
                    dve.wait_ge(s.scaled, 2 * k + j + 1)
                    reduce(top[j][:], sc[j][:], AX_X, ALU.max).then_inc(s.max_done, 1)
                for j in tiles:
                    dve.wait_ge(s.max_done, 2 * k + j + 1)
                    tt(sc[j][:], sc[j][:], top[j][:].unsqueeze(2).broadcast_to([P, HEADS, SEQ]), ALU.subtract).then_inc(s.shifted, 1)
                for j in tiles:
                    dve.wait_ge(s.exp_done, 2 * k + j + 1)
                    reduce(den[j][:], sc[j][:], AX_X, ALU.add).then_inc(s.den_done, 1)
                for j in tiles:
                    dve.wait_ge(s.den_done, 2 * k + j + 1)
                    nc.vector.reciprocal(rden[j][:], den[j][:]).then_inc(s.rden_done, 1)
                for j in tiles:
                    dve.wait_ge(s.weighed, 2 * k + j + 1)
                    dve.wait_ge(s.rden_done, 2 * k + j + 1)
                    tt(attn[j][:].rearrange("p (h e) -> p h e", e=E0), ps_b[j][:, 0:D].rearrange("p (h e) -> p h e", e=E0),
                       rden[j][:].unsqueeze(2).broadcast_to([P, HEADS, E0]), ALU.mult).then_inc(s.attn_done, 1)
                for j in tiles:
                    dve.wait_ge(s.attended, 2 * k + j + 1)
                    tt(x2[j][:], ps_b[j][:, 256:384], x1[j][:], ALU.add).then_inc(s.x2_done, 1)
                for j in tiles:
                    dve.wait_ge(s.x2_done, 2 * k + j + 1)
                    ln_b.statistics(dve, j, 2 * k + j + 1, x2[j][:])
                for j in tiles:
                    ln_b.normalise(dve, j, 2 * k + j + 1, x2[j][:])
                for j in tiles:
                    dve.wait_ge(s.relu_done, 2 * k + j + 1)
                    tt(act[j][:], relu[j][:], relu[j][:], ALU.mult).then_inc(s.act_done, 1)
                for j in tiles:
                    n = 2 * k + j + 1
                    wait_apart(dve, s.gated, n, s.waits)
                    nc.vector.max(best[j][:], gate[j][:]).then_inc(s.best_done, 1)
                    wait_apart(dve, s.best_done, n, s.waits)
                    nc.vector.max_index(place[j][:], best[j][:], gate[j][:]).then_inc(s.place_done, 1)
                    ts(total[j][:], best[j][:, 0:1], best[j][:, 1:2], 1e-20, ALU.add, ALU.add).then_inc(s.total_done, 1)
                    dve.wait_ge(s.place_done, n)
                    nc.vector.tensor_copy(place_f[j][:], place[j][:, 0:2]).then_inc(s.placef_done, 1)
                    dve.wait_ge(s.total_done, n)
                    nc.vector.reciprocal(total[j][:], total[j][:]).then_inc(s.inverse_done, 1)
                    dve.wait_ge(s.inverse_done, n)
                    ts(share[j][:], best[j][:, 0:2], total[j][:], None, ALU.mult).then_inc(s.share_done, 1)
                    dve.wait_ge(s.share_done, n)
                    dve.wait_ge(s.placef_done, n)
                    ts(cw1[j][:], iota, place_f[j][:, 0:1], share[j][:, 0:1], ALU.is_equal, ALU.mult).then_inc(s.cw1_done, 1)
                    ts(cw[j][:], iota, place_f[j][:, 1:2], share[j][:, 1:2], ALU.is_equal, ALU.mult).then_inc(s.cw1_done, 1)
                    dve.wait_ge(s.cw1_done, 2 * n)
                    tt(cw[j][:], cw[j][:], cw1[j][:], ALU.add).then_inc(s.cw_done, 1)
                for j in tiles:
                    dve.wait_ge(s.expert_done, 2 * k + j + 1)
                    dve.wait_ge(s.cw_done, 2 * k + j + 1)
                    tt(weighted[j][:], ps_c[j][:].rearrange("p (e d) -> p e d", d=D), cw[j][:].unsqueeze(2).broadcast_to([P, EXPERTS, D]),
                       ALU.mult).then_inc(s.weighted_done, 1)
                for j in tiles:
                    dve.wait_ge(s.weighted_done, 2 * k + j + 1)
                    reduce(mixed[j][:], weighted[j][:].rearrange("p e d -> p d e"), AX_X, ALU.add).then_inc(s.mixed_done, 1)
                for j in tiles:
                    dve.wait_ge(s.mixed_done, 2 * k + j + 1)
                    tt(x3[j][:], mixed[j][:], x2[j][:], ALU.add).then_inc(s.x3_done, 1)
                for j in tiles:
                    dve.wait_ge(s.x3_done, 2 * k + j + 1)
                    ln_c.statistics(dve, j, 2 * k + j + 1, x3[j][:])
                for j in tiles:
                    ln_c.normalise(dve, j, 2 * k + j + 1, x3[j][:])
                    nc.vector.tensor_copy(tile_of(g.x_tok, 2 * k + j), x3[j][:])
                for j in tiles:
                    dve.wait_ge(ln_c.done, 2 * k + j + 1)
                    ln_d.statistics(dve, j, 2 * k + j + 1, ln_c.out[j][:])
                for j in tiles:
                    ln_d.normalise(dve, j, 2 * k + j + 1, ln_c.out[j][:])
                for j in tiles:
                    dve.wait_ge(s.lat_done, 2 * k + j + 1)
                    row = 2 * (2 * k + j)
                    for b in range(2):
                        cp = nc.vector.tensor_copy(g.lat_rows[:, bass.ds(row + b, 1), :].rearrange("p o d -> p (o d)"),
                                                   lat[j][64 * b:64 * b + 64, :])
                    cp.then_inc(s.rows_copied, 1)


def rest_of_layer_1(nc, g, dram, out):
    K_CLAMP, K_EPS = 60.0, 1e-16
    FF_BLOCKS = 4
    TO_256TH, TO_QUARTER = 1.5 * 2.0 ** 15, 1.5 * 2.0 ** 21
    with ExitStack() as ctx:
        sb, pair, bank, sem, sems = scope(nc, ctx, "d_")
        ident = g.consts[:, C_IDENT:C_IDENT + P]
        raw, w_t = sb("raw", [P, 4, D]), sb("w_t", [P, 4, D])
        mix, unmix = sb("mix", [P, 1]), sb("unmix", [P, 1])
        decay_in, first_in, decay, first = (sb(n, [P, 1]) for n in ("decay_in", "first_in", "decay", "first"))
        decay_rows = sb("decay_rows", [P, 4, SEQ + 1])
        w1, b1, w2, b2 = sb("w1", [P, FF_BLOCKS * P]), sb("b1", [P, FF_BLOCKS]), sb("w2", [P, FF_BLOCKS, D]), sb("b2", [P, D])
        half, quarter = sb("half", [P, 1]), sb("quarter", [P, 1])
        x = pair("x", [P, D])
        xp = pair("xp", [P, 2, SEQ + 1])
        xm1, xm = pair("xm1", [P, 2, SEQ]), pair("xm", [P, 2, SEQ])
        kc = pair("kc", [P, 2, SEQ])
        kv = pair("kv", [P, 4, SEQ + 1])
        gate = pair("gate", [P, 2, SEQ])
        past, sums = pair("past", [P, 4, SEQ + 1]), pair("sums", [P, 4, SEQ])
        ratio, rwkv = pair("ratio", [P, 2, SEQ]), pair("rwkv", [P, 2, SEQ])
        x5, xn_t = pair("x5", [P, D]), pair("xn_t", [P, P])
        h, hq, over, low, left, rest, g_left, g_right, val = (pair(n, [P, BANK]) for n in (
            "h", "hq", "over", "low", "left", "rest", "g_left", "g_right", "val"))
        o, oq = pair("o", [P, D]), pair("oq", [P, D])
        ps_a, ps_b, ps_c = bank("ps_a", [P, BANK]), bank("ps_b", [P, BANK]), bank("ps_c", [P, BANK])
        s = Named()
        s.waits, s.pool_waits, s.loaded, s.set_up, s.w_turned = sems("waits pool_waits loaded set_up w_turned")
        s.w_copied, s.w_exp, s.w_scaled, s.copied, s.xn_turned = sems("w_copied w_exp w_scaled copied xn_turned")
        s.xp_done, s.xm1_done, s.xm_done, s.kvr_done, s.clamped = sems("xp_done xm1_done xm_done kvr_done clamped")
        s.k_done, s.r_done, s.kv_done, s.past_done, s.sums_done = sems("k_done r_done kv_done past_done sums_done")
        s.eps_done, s.inverse_done, s.ratio_done, s.rwkv_done, s.projected = sems("eps_done inverse_done ratio_done rwkv_done projected")
        s.x5_done, s.xn2_turned, s.xn2_copied, s.hidden, s.h_done = sems("x5_done xn2_turned xn2_copied hidden h_done")
        s.hq_done, s.over_done, s.clamp_done, s.low_done, s.left_done = sems("hq_done over_done clamp_done low_done left_done")
        s.left1_done, s.left2_done, s.rest_done, s.gl_done, s.gr_done = sems("left1_done left2_done rest_done gl_done gr_done")
        s.slope_done, s.rise_done, s.val_done, s.val2_done, s.rounded = sems("slope_done rise_done val_done val2_done rounded")
        s.act_done, s.final, s.o_done, s.oq_done, s.out_done = sems("act_done final o_done oq_done out_done")
        s.stored = sem("stored")
        ln_a, ln_b = (Norm(nc, n, pair, sem, half, s.waits) for n in ("ln_a", "ln_b"))
        tiles = range(WIDTH)
        LOADS = 16 * 11

        ctx.enter_context(nc.allow_non_contiguous_dma(reason="small vectors and permuted weights"))
        block = ctx.enter_context(nc.Block())

        @block.sync
        def _(sp):
            for i, w in enumerate((dram.L1_attn_Wk, dram.L1_attn_Wv, dram.L1_attn_Wr, dram.L1_attn_Wo)):
                sp.dma_start(raw[:, i, :], w).then_inc(s.loaded, 16)
            sp.dma_start(mix[:], dram.L1_attn_time_mix.rearrange("a b d -> d (a b)")).then_inc(s.loaded, 16)
            sp.dma_start(decay_in[:], dram.L1_attn_time_decay.broadcast_to([HEADS, E0])).then_inc(s.loaded, 16)
            sp.dma_start(first_in[:], dram.L1_attn_time_first.broadcast_to([HEADS, E0])).then_inc(s.loaded, 16)
            sp.dma_start(w1[:], dram.L1_ffn_w1).then_inc(s.loaded, 16)
            sp.dma_start(b1[:], dram.L1_ffn_b1.rearrange("(m f) -> f m", f=P)).then_inc(s.loaded, 16)
            sp.dma_start(w2[:], dram.L1_ffn_w2.rearrange("(m f) d -> f m d", f=P)).then_inc(s.loaded, 16)
            sp.dma_start(b2[:], dram.L1_ffn_b2.partition_broadcast(P)).then_inc(s.loaded, 16)
            sp.sem_inc(s.stored, 16)
            with sp.Fori(0, ROUNDS) as k:
                for j in tiles:
                    sp.wait_ge(s.out_done, 2 * k + j + 2)
                    sp.dma_start(out[bass.ds(2 * (2 * k + j), 2)].rearrange("b s d -> (b s) d"), x[j][:]).then_inc(s.stored, 16)
            sp.wait_ge(s.stored, 16 * (TOK_TILES + 1))

        @block.tensor
        def _(pe):
            pe.wait_ge(s.loaded, LOADS)
            for i in range(4):
                tr = nc.tensor.transpose(ps_b[0][:, P * i:P * i + P], raw[:, i, :], ident)
            tr.then_inc(s.w_turned, 1)
            pe.wait_ge(s.w_copied, 1)
            with pe.Fori(0, ROUNDS) as k:
                for j in tiles:
                    pe.wait_ge(ln_a.done, 2 * k + j + 1)
                    nc.tensor.transpose(ps_a[j][:, 0:P], ln_a.out[j][:], ident).then_inc(s.xn_turned, 1)
                for j in tiles:
                    pe.wait_ge(s.xm_done, 2 * k + j + 1)
                    for i in range(3):
                        mm = nc.tensor.matmul(ps_b[j][:, P * i:P * i + P], w_t[:, i], xm[j][:].rearrange("p b q -> p (b q)"),
                                              start=True, stop=True)
                    mm.then_inc(s.kvr_done, 1)
                for j in tiles:
                    pe.wait_ge(s.rwkv_done, 2 * k + j + 1)
                    nc.tensor.matmul(ps_b[j][:, 384:512], rwkv[j][:].rearrange("p b q -> p (b q)"), w_t[:, 3], start=True,
                                     stop=True).then_inc(s.projected, 1)
                for j in tiles:
                    pe.wait_ge(ln_b.done, 2 * k + j + 1)
                    nc.tensor.transpose(ps_a[j][:, 128:256], ln_b.out[j][:], ident).then_inc(s.xn2_turned, 1)
                for j in tiles:
                    pe.wait_ge(s.xn2_copied, 2 * k + j + 1)
                    for m in range(FF_BLOCKS):
                        mm = nc.tensor.matmul(ps_c[j][:, P * m:P * m + P], w1[:, P * m:P * m + P], xn_t[j][:], start=True, stop=True)
                    mm.then_inc(s.hidden, 1)
                for j in tiles:
                    pe.wait_ge(s.act_done, 2 * k + j + 1)
                    for m in range(FF_BLOCKS):
                        mm = nc.tensor.matmul(ps_a[j][:, 256:384], val[j][:, P * m:P * m + P], w2[:, m], start=(m == 0),
                                              stop=(m == FF_BLOCKS - 1))
                    mm.then_inc(s.final, 1)

        @block.scalar
        def _(act):
            act.wait_ge(s.w_turned, 1)
            nc.scalar.activation(w_t[:].rearrange("p m k -> p (m k)"), ps_b[0][:], ACT.Copy).then_inc(s.w_copied, 1)
            act.wait_ge(s.loaded, LOADS)
            act.wait_ge(s.set_up, 2 + 2 * WIDTH)
            nc.scalar.activation(decay[:], decay_in[:], ACT.Exp).then_inc(s.w_exp, 1)
            nc.scalar.activation(first[:], first_in[:], ACT.Exp).then_inc(s.w_exp, 1)
            act.wait_ge(s.w_exp, 2)
            nc.scalar.activation(decay[:], decay[:], ACT.Exp, scale=-1.0).then_inc(s.w_exp, 1)
            with act.Fori(0, ROUNDS) as k:
                act.wait_ge(s.out_done, 2 * k + 1)
                for j in tiles:
                    act.wait_ge(s.xn_turned, 2 * k + j + 1)
                    nc.scalar.activation(xp[j][:, :, 1:SEQ + 1], ps_a[j][:, 0:P].rearrange("p (b q) -> p b q", b=2),
                                         ACT.Copy).then_inc(s.xp_done, 1)
                for j in tiles:
                    act.wait_ge(s.kvr_done, 2 * k + j + 1)
                    nc.scalar.activation(gate[j][:], ps_b[j][:, 256:384].rearrange("p (b q) -> p b q", b=2), ACT.Sigmoid).then_inc(s.r_done, 1)
                for j in tiles:
                    act.wait_ge(s.clamped, 2 * k + j + 1)
                    nc.scalar.activation(kv[j][:, 2:4, 1:SEQ + 1], kc[j][:], ACT.Exp).then_inc(s.k_done, 1)
                for j in tiles:
                    act.wait_ge(s.xn2_turned, 2 * k + j + 1)
                    nc.scalar.activation(xn_t[j][:], ps_a[j][:, 128:256], ACT.Copy).then_inc(s.xn2_copied, 1)
                for j in tiles:
                    act.wait_ge(s.hidden, 2 * k + j + 1)
                    for m in range(FF_BLOCKS):
                        cols = slice(P * m, P * m + P)
                        op = nc.scalar.activation(h[j][:, cols], ps_c[j][:, cols], ACT.Identity, bias=b1[:, m:m + 1])
                    op.then_inc(s.h_done, 1)
                for j in tiles:
                    act.wait_ge(s.left2_done, 2 * k + j + 1)
                    nc.scalar.activation(g_left[j][:], left[j][:], ACT.Gelu).then_inc(s.gl_done, 1)
                    nc.scalar.activation(g_right[j][:], left[j][:], ACT.Gelu, bias=quarter[:]).then_inc(s.gr_done, 1)

        @block.gpsimd
        def _(pool):
            nc.gpsimd.memset(half[:], -0.5).then_inc(s.set_up, 1)
            nc.gpsimd.memset(quarter[:], 0.25).then_inc(s.set_up, 1)
            for j in tiles:
                nc.gpsimd.memset(xp[j][:], 0.0).then_inc(s.set_up, 1)
                nc.gpsimd.memset(kv[j][:], 0.0).then_inc(s.set_up, 1)
            pool.wait_ge(s.set_up, 2 + 2 * WIDTH)
            pool.wait_ge(s.loaded, LOADS)
            nc.gpsimd.tensor_scalar(unmix[:], mix[:], -1.0, 1.0, ALU.mult, ALU.add).then_inc(s.set_up, 1)
            pool.wait_ge(s.w_exp, 3)
            nc.gpsimd.tensor_scalar(decay_rows[:], g.consts[:, C_SEQSTART:C_SEQSTART + SEQ + 1].unsqueeze(1).broadcast_to([P, 4, SEQ + 1]),
                                    decay[:], None, ALU.mult).then_inc(s.set_up, 1)
            with pool.Fori(0, ROUNDS) as k:
                pool.wait_ge(s.out_done, 2 * k + 1)
                for j in tiles:
                    ln_a.root(pool, j, 2 * k + j + 1)
                for j in tiles:
                    ln_b.root(pool, j, 2 * k + j + 1)
                for j in tiles:
                    wait_apart(pool, s.hq_done, 2 * k + j + 1, s.pool_waits)
                    nc.gpsimd.tensor_scalar(over[j][:], hq[j][:], TO_256TH + 4.0, 0.0, ALU.subtract, ALU.max).then_inc(s.over_done, 1)
                for j in tiles:
                    pool.wait_ge(s.left2_done, 2 * k + j + 1)
                    nc.gpsimd.tensor_tensor(rest[j][:], low[j][:], left[j][:], ALU.subtract).then_inc(s.rest_done, 1)

        @block.vector
        def _(dve):
            tt, ts, stt = nc.vector.tensor_tensor, nc.vector.tensor_scalar, nc.vector.scalar_tensor_tensor
            HALF_STEP = 2.0 ** -9

            def flat(rows):
                return rows[:].rearrange("p m q -> p (m q)")

            dve.wait_ge(s.set_up, 4 + 2 * WIDTH)
            dve.wait_ge(s.loaded, LOADS)
            dve.sem_inc(s.out_done, 1)
            with dve.Fori(0, ROUNDS) as k:
                dve.wait_ge(s.stored, 16 * (2 * k + 1))
                for j in tiles:
                    nc.vector.tensor_copy(x[j][:], tile_of(g.x_tok, 2 * k + j)).then_inc(s.copied, 1)
                for j in tiles:
                    dve.wait_ge(s.copied, 2 * k + j + 1)
                    ln_a.statistics(dve, j, 2 * k + j + 1, x[j][:])
                for j in tiles:
                    ln_a.normalise(dve, j, 2 * k + j + 1, x[j][:])
                for j in tiles:
                    dve.wait_ge(s.xp_done, 2 * k + j + 1)
                    ts(xm1[j][:], xp[j][:, :, 0:SEQ], unmix[:], None, ALU.mult).then_inc(s.xm1_done, 1)
                for j in tiles:
                    dve.wait_ge(s.xm1_done, 2 * k + j + 1)
                    stt(xm[j][:], xp[j][:, :, 1:SEQ + 1], mix[:], xm1[j][:], ALU.mult, ALU.add).then_inc(s.xm_done, 1)
                for j in tiles:
                    dve.wait_ge(s.r_done, 2 * k + j + 1)
                    ts(kc[j][:], ps_b[j][:, 0:P].rearrange("p (b q) -> p b q", b=2), K_CLAMP, None, ALU.min).then_inc(s.clamped, 1)
                for j in tiles:
                    dve.wait_ge(s.k_done, 2 * k + j + 1)
                    tt(kv[j][:, 0:2, 1:SEQ + 1], kv[j][:, 2:4, 1:SEQ + 1], ps_b[j][:, 128:256].rearrange("p (b q) -> p b q", b=2),
                       ALU.mult).then_inc(s.kv_done, 1)
                for j in tiles:
                    dve.wait_ge(s.kv_done, 2 * k + j + 1)
                    nc.vector.tensor_tensor_scan(flat(past[j]), flat(decay_rows), flat(kv[j]), 0.0, ALU.mult, ALU.add).then_inc(s.past_done, 1)
                for j in tiles:
                    dve.wait_ge(s.past_done, 2 * k + j + 1)
                    stt(sums[j][:], kv[j][:, :, 1:SEQ + 1], first[:], past[j][:, :, 0:SEQ], ALU.mult, ALU.add).then_inc(s.sums_done, 1)
                for j in tiles:
                    dve.wait_ge(s.sums_done, 2 * k + j + 1)
                    ts(sums[j][:, 2:4, :], sums[j][:, 2:4, :], K_EPS, None, ALU.add).then_inc(s.eps_done, 1)
                    tt(ratio[j][:], gate[j][:], sums[j][:, 0:2, :], ALU.mult).then_inc(s.ratio_done, 1)
                for j in tiles:
                    dve.wait_ge(s.eps_done, 2 * k + j + 1)
                    nc.vector.reciprocal(sums[j][:, 2:4, :], sums[j][:, 2:4, :]).then_inc(s.inverse_done, 1)
                for j in tiles:
                    dve.wait_ge(s.inverse_done, 2 * k + j + 1)
                    dve.wait_ge(s.ratio_done, 2 * k + j + 1)
                    tt(rwkv[j][:], ratio[j][:], sums[j][:, 2:4, :], ALU.mult).then_inc(s.rwkv_done, 1)
                for j in tiles:
                    dve.wait_ge(s.projected, 2 * k + j + 1)
                    tt(x5[j][:], ps_b[j][:, 384:512], x[j][:], ALU.add).then_inc(s.x5_done, 1)
                for j in tiles:
                    dve.wait_ge(s.x5_done, 2 * k + j + 1)
                    ln_b.statistics(dve, j, 2 * k + j + 1, x5[j][:])
                for j in tiles:
                    ln_b.normalise(dve, j, 2 * k + j + 1, x5[j][:])
                for j in tiles:
                    dve.wait_ge(s.h_done, 2 * k + j + 1)
                    ts(hq[j][:], h[j][:], TO_256TH, None, ALU.add).then_inc(s.hq_done, 1)
                for j in tiles:
                    dve.wait_ge(s.hq_done, 2 * k + j + 1)
                    ts(low[j][:], hq[j][:], TO_256TH - 4.0, TO_256TH + 4.0, ALU.max, ALU.min).then_inc(s.clamp_done, 1)
                for j in tiles:
                    dve.wait_ge(s.clamp_done, 2 * k + j + 1)
                    ts(low[j][:], low[j][:], TO_256TH, None, ALU.subtract).then_inc(s.low_done, 1)
                for j in tiles:
                    dve.wait_ge(s.low_done, 2 * k + j + 1)
                    ts(left[j][:], low[j][:], 0.125 - HALF_STEP, None, ALU.subtract).then_inc(s.left_done, 1)
                for j in tiles:
                    dve.wait_ge(s.left_done, 2 * k + j + 1)
                    ts(left[j][:], left[j][:], TO_QUARTER, None, ALU.add).then_inc(s.left1_done, 1)
                for j in tiles:
                    dve.wait_ge(s.left1_done, 2 * k + j + 1)
                    ts(left[j][:], left[j][:], TO_QUARTER, None, ALU.subtract).then_inc(s.left2_done, 1)
                for j in tiles:
                    dve.wait_ge(s.gl_done, 2 * k + j + 1)
                    dve.wait_ge(s.gr_done, 2 * k + j + 1)
                    tt(g_right[j][:], g_right[j][:], g_left[j][:], ALU.subtract).then_inc(s.slope_done, 1)
                for j in tiles:
                    dve.wait_ge(s.slope_done, 2 * k + j + 1)
                    dve.wait_ge(s.rest_done, 2 * k + j + 1)
                    stt(val[j][:], rest[j][:], 4.0, g_right[j][:], ALU.mult, ALU.mult).then_inc(s.rise_done, 1)
                for j in tiles:
                    dve.wait_ge(s.rise_done, 2 * k + j + 1)
                    tt(val[j][:], val[j][:], g_left[j][:], ALU.add).then_inc(s.val_done, 1)
                for j in tiles:
                    dve.wait_ge(s.val_done, 2 * k + j + 1)
                    dve.wait_ge(s.over_done, 2 * k + j + 1)
                    tt(val[j][:], val[j][:], over[j][:], ALU.add).then_inc(s.val2_done, 1)
                for j in tiles:
                    dve.wait_ge(s.val2_done, 2 * k + j + 1)
                    ts(val[j][:], val[j][:], TO_256TH, None, ALU.add).then_inc(s.rounded, 1)
                for j in tiles:
                    dve.wait_ge(s.rounded, 2 * k + j + 1)
                    ts(val[j][:], val[j][:], TO_256TH, None, ALU.subtract).then_inc(s.act_done, 1)
                for j in tiles:
                    n = 2 * k + j + 1
                    dve.wait_ge(s.final, n)
                    tt(o[j][:], ps_a[j][:, 256:384], b2[:], ALU.add).then_inc(s.o_done, 1)
                    dve.wait_ge(s.o_done, n)
                    ts(oq[j][:], o[j][:], TO_256TH, None, ALU.add).then_inc(s.oq_done, 1)
                    dve.wait_ge(s.oq_done, n)
                    stt(x[j][:], oq[j][:], TO_256TH, x5[j][:], ALU.subtract, ALU.add).then_inc(s.out_done, 1)


def cross_attention_1(nc, g, dram):
    LAT = FULL + 1
    KEYS = CTX + SEQ
    lay = Named()
    lay.tag, lay.keys, lay.norm_cols, lay.last_output = "c_", KEYS, BANK, True
    lay.tiles = [(P if t < FULL else TAIL, P * t) for t in range(FULL + 1)] + [(SEQ, CTX)]
    xt = [("x_t", c) for c in range(CHUNKS)]
    half = [None] * 7 + [("norm",), xt[0], xt[1], xt[2], None, xt[3], None, None, ("norm",)]
    lay.jobs = [half[:11] + [("out",)] + half[12:], half]

    with ExitStack() as ctx:
        t = Named()

        def allocate(own):
            sb, sem = own.sb, own.sem
            lay.own = own
            t.ctx = sb("ctx", [P, FULL + 1, D])
            t.stats = sb("stats", [P, FULL + 1, 6])
            t.mean_var = sb("mean_var", [P, FULL + 1, 2])
            t.rstd, t.shift, t.half = (sb(n, [P, FULL + 1]) for n in ("rstd", "shift", "half"))
            t.weight, t.bias = sb("ln_w", [P, D]), sb("ln_b", [P, D])
            t.xn = [sb(f"xn{m}", [P, LAT + 1, D]) for m in range(2)]
            t.x_hi = [sb(f"x_hi{m}", [P, KEYS + 1], F32R) for m in range(2)]
            t.x_lo = [sb(f"x_lo{m}", [P, KEYS + 1], F32R) for m in range(2)]
            t.q_raw = sb("q_raw", [P, HEADS * SEQ])
            t.q_hi = [sb(f"q_hi{m}", [P, HEADS * SEQ], F32R) for m in range(2)]
            t.q_lo = [sb(f"q_lo{m}", [P, HEADS * SEQ], F32R) for m in range(2)]
            t.u_t = sb("u_t", [P, HEADS, 2, SEQ])
            t.ones = sb("ones", [P, P])
            t.waits, t.pool_waits, t.loaded, t.ctx_loaded, t.q_loaded, t.set_up, t.stat = (sem(n) for n in ("waits", "pool_waits", "loaded", "ctx_loaded", "q_loaded", "set_up", "stat"))
            t.aggr, t.eps, t.rstd_done, t.shift_done, t.centred = (sem(n) for n in ("aggr", "eps", "rstd_done", "shift_done", "centred"))
            t.weighted, t.xn_done, t.q_split, t.pads_set, t.added = (sem(n) for n in ("weighted", "xn_done", "q_split", "pads_set", "added"))

        lay.allocate = allocate

        def load_ctx(sp, b):
            sp.dma_start(t.ctx[:, 0:FULL, :],
                         dram.ctx[bass.ds(b, 1), 0:FULL * P, :].rearrange("o (p t) d -> p (o t) d", t=FULL)).then_inc(t.ctx_loaded, 16)
            sp.dma_start(t.ctx[0:TAIL, FULL, :],
                         dram.ctx[bass.ds(b, 1), FULL * P:CTX, :].rearrange("o p d -> p (o d)")).then_inc(t.ctx_loaded, 16)

        def load_q(sp, b):
            sp.dma_start(t.q_raw[:], dram.q1[bass.ds(b, 1)].rearrange("o p n -> p (o n)")).then_inc(t.q_loaded, 16)

        def sync_start(sp):
            load_ctx(sp, 0)
            load_q(sp, 0)
            sp.dma_start(t.weight[:], dram.L1_xattn_ln1_w.partition_broadcast(P)).then_inc(t.loaded, 16)
            sp.dma_start(t.bias[:], dram.L1_xattn_ln1_b.partition_broadcast(P)).then_inc(t.loaded, 16)
            sp.wait_ge(t.q_split, 2)
            load_q(sp, 1)
            sp.wait_ge(t.xn_done, CHUNKS)
            load_ctx(sp, 1)

        def sync_body(sp, k, kind):
            if kind != "last":
                for m in range(2):
                    b = 2 * k + m + 2
                    sp.wait_ge(t.q_split, 2 * b)
                    load_q(sp, b)
                    sp.wait_ge(t.xn_done, CHUNKS * b)
                    load_ctx(sp, b)

        lay.sync_start, lay.sync_body, lay.sync_end = sync_start, sync_body, lambda sp: None

        def prepare(pool, b, m, first):
            wait_apart(pool, t.q_loaded, (b + 1) * 16, t.pool_waits)
            nc.gpsimd.tensor_copy(t.q_hi[m][:], t.q_raw[:]).then_inc(t.q_split, 1)
            pool.wait_ge(t.q_split, 2 * b + 1)
            nc.gpsimd.tensor_tensor(t.q_lo[m][:], t.q_raw[:], t.q_hi[m][:].bitcast(F32), ALU.subtract).then_inc(t.q_split, 1)
            pool.wait_ge(t.eps, 2 * (b + 1))
            nc.gpsimd.tensor_tensor(t.rstd[:], t.rstd[:], t.half[:], ALU.pow).then_inc(t.rstd_done, 1)
            pool.wait_ge(t.rstd_done, b + 1)
            nc.gpsimd.tensor_tensor(t.shift[:], t.shift[:], t.rstd[:], ALU.mult).then_inc(t.shift_done, 1)
            wait_apart(pool, t.shift_done, b + 1, t.pool_waits)
            for i in range(FULL + 1):
                rows = lay.tiles[i][0]
                nc.gpsimd.tensor_scalar(t.ctx[0:rows, i, :], t.ctx[0:rows, i, :], t.rstd[0:rows, i:i + 1], t.shift[0:rows, i:i + 1],
                                        ALU.mult, ALU.add).then_inc(t.centred, 1)
            for c in range(CHUNKS):
                n = 4 if c < 3 else 1
                rows, tiles = (P if c < 3 else TAIL), slice(4 * c, 4 * c + n)
                pool.wait_ge(t.centred, (FULL + 1) * b + 4 * c + n)
                w, bias = (v[0:rows].unsqueeze(1).broadcast_to([rows, n, D]) for v in (t.weight, t.bias))
                nc.gpsimd.tensor_tensor(t.ctx[0:rows, tiles, :], t.ctx[0:rows, tiles, :], w, ALU.mult).then_inc(t.weighted, 1)
                if not first:
                    pool.wait_ge(lay.own.pv_done, CHUNKS * (QUADS * (b - 1) - 1) + c + 1)
                pool.wait_ge(t.weighted, CHUNKS * b + c + 1)
                if c == 3:
                    nc.gpsimd.tensor_copy(t.xn[m][0:SEQ, LAT, :], g.lat_rows[:, bass.ds(b, 1), :].rearrange("p o d -> p (o d)"))
                nc.gpsimd.tensor_tensor(t.xn[m][0:rows, tiles, :], t.ctx[0:rows, tiles, :], bias, ALU.add).then_inc(t.xn_done, 1)

        def pool_start(pool):
            nc.gpsimd.memset(t.half[:], -0.5).then_inc(t.set_up, 1)
            nc.gpsimd.memset(t.ones[:], 1.0).then_inc(t.set_up, 1)
            pool.wait_ge(t.set_up, 2)
            pool.wait_ge(t.loaded, 32)
            prepare(pool, 0, 0, True)

        def pool_prepare(pool, k, kind, m):
            b = 2 * k + m + 1
            first = kind == "first" and m == 0
            if not first:
                pool.wait_ge(lay.own.scores_ready, (b - 1) * PAIRS * CHUNKS)
            prepare(pool, b, (m + 1) % 2, first)

        lay.pool_start, lay.pool_prepare = pool_start, pool_prepare

        def pe_start(pe):
            pe.wait_ge(t.set_up, 2)
            pe.wait_ge(t.pads_set, 4)

        def pe_job(pe, what, m, kind, k, s):
            own = lay.own
            if what[0] == "x_t":
                c = what[1]
                b = 0 if kind == "start" else 2 * k + m + 1
                par = 0 if kind == "start" else (m + 1) % 2
                pe.wait_ge(t.xn_done, CHUNKS * b + c + 1)
                for i, (rows, col) in enumerate(lay.tiles[4 * c:4 * c + 4]):
                    c0 = col - BANK * c
                    last = nc.tensor.transpose(own.scratch[:, c0:c0 + rows], t.xn[par][0:rows, 4 * c + i, :],
                                               g.consts[0:rows, C_IDENT:C_IDENT + rows])
                return last
            pe.wait_ge(own.pv_taken, 4 * k)
            for h in range(HEADS):
                last = nc.tensor.matmul(own.scratch[:, 0:D], t.u_t[:, h], g.wvo[:, h, :], start=(h == 0), stop=(h == HEADS - 1))
            return last

        def pe_operands_ready(pe, k, kind, m, u):
            if u == 0:
                pe.wait_ge(t.q_split, 2 * (2 * k + m) + 2)
                pe.wait_ge(lay.own.scratch_free, CHUNKS if kind == "first" and m == 0 else
                           lay.own.number_after(k, kind, PAIRS * m - 2, "b"))

        def pe_values(pe, m, u, tiles):
            for i in tiles:
                if i < len(lay.tiles):
                    rows = lay.tiles[i][0]
                    last = nc.tensor.matmul(lay.own.pv_ps[:], t.xn[m][0:rows, i, :], lay.own.prob_t[u][0:rows, i, :],
                                            start=(i == 0), stop=(i == LAT))
            return last

        lay.pe_start, lay.pe_job = pe_start, pe_job
        lay.pe_norm = lambda pe, diag: nc.tensor.matmul(lay.own.scratch[:], t.ones[:], diag[:], start=True, stop=True)
        lay.pe_operands_ready, lay.pe_values = pe_operands_ready, pe_values

        def score_passes(m, u, j):
            cols = slice(P * (QUAD * u + j), P * (QUAD * u + j) + P)
            return [(t.q_hi[m][:, cols], t.x_hi[m]), (t.q_hi[m][:, cols], t.x_lo[m]), (t.q_lo[m][:, cols], t.x_hi[m])]

        lay.score_passes = score_passes

        def act_take(act, what, m):
            if what[0] == "x_t":
                cols = quad_chunk(what[1], KEYS)
                nc.scalar.activation(t.x_hi[m][:, cols], lay.own.scratch[:, 0:cols.stop - cols.start], ACT.Copy).then_inc(lay.own.half_taken, 1)

        lay.act_start, lay.act_take = (lambda act: None), act_take

        def x_low(dve, c, b, m):
            cols = quad_chunk(c, KEYS)
            dve.wait_ge(lay.own.half_taken, CHUNKS * b + c + 1)
            nc.vector.tensor_tensor(t.x_lo[m][:, cols], lay.own.scratch[:, 0:cols.stop - cols.start], t.x_hi[m][:, cols].bitcast(F32),
                                    ALU.subtract).then_inc(lay.own.scratch_free, 1)

        def add_output(dve, tile):
            row = g.x_tok[:, bass.ds(tile, 1), :].rearrange("p o d -> p (o d)")
            nc.vector.tensor_tensor(row, lay.own.scratch[:, 0:D], row, ALU.add).then_inc(lay.own.scratch_free, 1)

        def dve_take(dve, entry, base, k, kind, s):
            what, n = entry
            if what[0] == "x_t":
                x_low(dve, what[1], 2 * k + s // PAIRS + 1, (s // PAIRS + 1) % 2)
            elif what[0] == "out":
                dve.wait_ge(lay.own.scratch_ready, base + n + 1)
                add_output(dve, k - 1)

        def statistics(dve, b, tiles):
            if tiles[0] == 0:
                dve.wait_ge(t.ctx_loaded, (b + 1) * 32)
            for i in tiles:
                rows = lay.tiles[i][0]
                nc.vector.bn_stats(t.stats[0:rows, i, :], t.ctx[0:rows, i, :]).then_inc(t.stat, 1)
            wait_apart(dve, t.stat, (FULL + 1) * b + tiles[-1] + 1, t.waits)
            for i in tiles:
                rows = lay.tiles[i][0]
                nc.vector.bn_aggr(t.mean_var[0:rows, i, :], t.stats[0:rows, i, :]).then_inc(t.aggr, 1)
            if tiles[-1] == FULL:
                dve.wait_ge(t.aggr, (FULL + 1) * (b + 1))
                if not (isinstance(b, int) and b == 0):
                    dve.wait_ge(t.xn_done, CHUNKS * b)
                nc.vector.tensor_scalar(t.rstd[:], t.mean_var[:, :, 1], LN_EPS, None, ALU.add).then_inc(t.eps, 1)
                nc.vector.tensor_scalar(t.shift[:], t.mean_var[:, :, 0], -1.0, None, ALU.mult).then_inc(t.eps, 1)

        def dve_start(dve):
            for v in t.x_hi + t.x_lo:
                nc.vector.memset(v[:, KEYS:KEYS + 1].bitcast(U32), 0).then_inc(t.pads_set, 1)
            nc.vector.memset(t.mean_var[:], 0.0).then_inc(t.pads_set, 1)
            dve.wait_ge(t.pads_set, 5)
            statistics(dve, 0, list(range(FULL + 1)))
            for c in range(CHUNKS):
                x_low(dve, c, 0, 0)

        def dve_extra(dve, k, kind, s):
            m, n = divmod(s, PAIRS)
            if n < 2 and not (kind == "last" and m == 1):
                statistics(dve, 2 * k + m + 1, list(range(7)) if n == 0 else list(range(7, FULL + 1)))

        def dve_finish(dve, q, i, k):
            own = lay.own
            m, u = i // QUADS % 2, i % QUADS
            if i == 0 and not (isinstance(k, int) and k == 0):
                dve.wait_ge(own.scratch_ready, own.number_after(k, "mid" if not isinstance(k, int) else "last", 5, "a"))
            nc.vector.tensor_tensor(t.u_t[:, 8 * u:8 * u + 8, m, :], own.pv_ps[:].rearrange("p (h q) -> p h q", h=8),
                                    own.norm[:].rearrange("p (h q) -> p h q", h=8), ALU.mult).then_inc(own.pv_taken, 1)

        def dve_end(dve):
            own = lay.own
            n = own.base("last", BODIES - 1) + len(own.table["last"]) + 2
            dve.wait_ge(own.scratch_ready, n)
            add_output(dve, BODIES - 1)

        lay.dve_start, lay.dve_take, lay.dve_finish, lay.dve_extra, lay.dve_end = dve_start, dve_take, dve_finish, dve_extra, dve_end
        attend(nc, g, lay, ctx)


def constant_columns():
    import numpy as np
    p = np.arange(P)
    c = np.zeros((P, C_END), np.float32)
    c[:, C_IDENT:C_IDENT + P] = np.eye(P)
    r = np.arange(32)
    c[:, C_PAIRROWS:C_PAIRROWS + 32] = (p[:, None] // SEQ == r[None] // E0) & (r[None] < 2 * E0)
    c[:, C_HEADROWS:C_HEADROWS + 8] = (p[:, None] % 64) // E0 == np.arange(8)[None]
    c[:, C_CAUSAL:C_CAUSAL + SEQ] = np.where(np.arange(SEQ)[None] <= p[:, None] % SEQ, 0.0, -1e30)
    freq = (1.0 / 10000.0 ** (np.arange(0, E0, 2, dtype=np.float32) / E0)).astype(np.float32)
    angle = np.arange(SEQ, dtype=np.float32)[None] * freq[(p % E0) // 2][:, None]
    c[:, C_COS:C_COS + SEQ] = np.cos(angle)
    c[:, C_SIN:C_SIN + SEQ] = np.sin(angle) * np.where(p % 2 == 0, -1.0, 1.0)[:, None]
    c[:, C_IOTA:C_IOTA + 8] = np.arange(8)[None]
    c[:, C_SEQSTART:C_SEQSTART + SEQ + 1] = (np.arange(SEQ + 1) > 0)[None]
    c[:, C_QUADROWS:C_QUADROWS + 4] = p[:, None] % 32 // E0 == np.arange(4)[None]
    c[:, C_GROUPROWS:C_GROUPROWS + 4] = p[:, None] // 32 == np.arange(4)[None]
    return c


def build(nc, tensors, consts, out):
    dram = Named()
    dram.x, dram.ctx, dram.consts = tensors["x"], tensors["ctx_1024"], consts
    dram.L0_xattn_wq, dram.L0_xattn_bq, dram.L0_xattn_wk, dram.L0_xattn_bk = (
        tensors["L0_xattn_wq"], tensors["L0_xattn_bq"], tensors["L0_xattn_wk"], tensors["L0_xattn_bk"])
    dram.L0_xattn_wv, dram.L0_xattn_bv, dram.L0_xattn_wo, dram.L0_xattn_bo = (
        tensors["L0_xattn_wv"], tensors["L0_xattn_bv"], tensors["L0_xattn_wo"], tensors["L0_xattn_bo"])
    dram.L0_attn_W_KQV, dram.L0_attn_W_O = (
        tensors["L0_attn_W_KQV"], tensors["L0_attn_W_O"])
    dram.L0_ffn_router_w, dram.L0_ffn_w1, dram.L0_ffn_w2 = (
        tensors["L0_ffn_router_w"], tensors["L0_ffn_w1"], tensors["L0_ffn_w2"])
    dram.L1_xattn_ln1_w, dram.L1_xattn_ln1_b, dram.L1_xattn_ln2_w, dram.L1_xattn_ln2_b = (
        tensors["L1_xattn_ln1_w"], tensors["L1_xattn_ln1_b"], tensors["L1_xattn_ln2_w"], tensors["L1_xattn_ln2_b"])
    dram.L1_xattn_Wq, dram.L1_xattn_Wkv, dram.L1_xattn_Wo = (
        tensors["L1_xattn_Wq"], tensors["L1_xattn_Wkv"], tensors["L1_xattn_Wo"])
    dram.L1_attn_time_decay, dram.L1_attn_time_first, dram.L1_attn_time_mix, dram.L1_attn_Wk = (
        tensors["L1_attn_time_decay"], tensors["L1_attn_time_first"], tensors["L1_attn_time_mix"], tensors["L1_attn_Wk"])
    dram.L1_attn_Wv, dram.L1_attn_Wr, dram.L1_attn_Wo = (
        tensors["L1_attn_Wv"], tensors["L1_attn_Wr"], tensors["L1_attn_Wo"])
    dram.L1_ffn_w1, dram.L1_ffn_b1, dram.L1_ffn_w2, dram.L1_ffn_b2 = (
        tensors["L1_ffn_w1"], tensors["L1_ffn_b1"], tensors["L1_ffn_w2"], tensors["L1_ffn_b2"])
    dram.q1 = nc.dram_tensor("absorbed_queries", (BATCH, P, HEADS * SEQ), F32, kind="Internal").ap()
    with ExitStack() as kept:
        def sb(name, shape):
            return kept.enter_context(nc.sbuf_tensor(name, shape, F32))

        g = Named()
        g.x_tok = sb("x_tok", [P, TOK_TILES, D])
        g.consts = sb("consts", [P, C_END])
        g.lat_rows = sb("lat_rows", [SEQ, BATCH, D])
        g.wvo = sb("wvo", [P, HEADS, D])
        with ExitStack() as early:
            g.act_t = early.enter_context(nc.sbuf_tensor("act_t", [P, QUADS, TOKENS], F32))
            g.wo_rows = early.enter_context(nc.sbuf_tensor("wo_rows", [P, QUADS, D], F32))
            cross_attention_0(nc, g, dram)
            with nc.sbuf_tensor("qk", [P, HEADS, D], F32) as qk:
                g.qk = qk
                fold_resampler_weights(nc, g, dram)
                rest_of_layer_0(nc, g, dram)
        cross_attention_1(nc, g, dram)
        rest_of_layer_1(nc, g, dram, out)


_OUT = ((BATCH, SEQ, D), "float32")


def kernel(**inputs):
    import numpy as _np
    import concourse.bacc as _bacc
    from concourse import mybir as _mybir
    from concourse.bass_utils import run_bass_kernel_spmd as _run

    nc = _bacc.Bacc("TRN2", target_bir_lowering=False, num_devices=1)
    arrays, tensors = {}, {}
    for name in inputs:
        a = _np.ascontiguousarray(inputs[name])
        arrays[f"in_{name}_dram"] = a
        tensors[name] = nc.dram_tensor(f"in_{name}_dram", a.shape, _mybir.dt.from_np(a.dtype), kind="ExternalInput").ap()
    table = constant_columns()
    arrays["in_consts_dram"] = table
    consts = nc.dram_tensor("in_consts_dram", table.shape, _mybir.dt.from_np(table.dtype), kind="ExternalInput").ap()
    out = nc.dram_tensor("out_0_dram", _OUT[0], _mybir.dt.from_np(_np.dtype(_OUT[1])), kind="ExternalOutput").ap()
    build(nc, tensors, consts, out)
    r = _run(nc, [arrays], core_ids=[0])
    return r.results[0]["out_0_dram"]
```

```python
from contextlib import ExitStack

import concourse.bass as bass
from concourse import mybir

ALU = mybir.AluOpType
ACT = mybir.ActivationFunctionType
AX_X = mybir.AxisListType.X
F32 = mybir.dt.float32
F32R = mybir.dt.float32r
U32 = mybir.dt.uint32

P = 128
D = 128
BATCH, SEQ, CTX = 16, 64, 1601
TOKENS = BATCH * SEQ
TOK_TILES = TOKENS // P
HEADS = 16
PAIRS = HEADS // 2
QUAD = 4
QUADS = PAIRS // QUAD
FULL = CTX // P
TAIL = CTX - FULL * P
BANK = 512
CHUNKS = 4
BODIES = BATCH // 2
SLOTS = 2 * PAIRS
LN_EPS = 1e-5
FIRST_SEMAPHORE = 128
E0 = 8

C_IDENT, C_PAIRROWS, C_HEADROWS, C_CAUSAL, C_COS, C_SIN, C_IOTA, C_SEQSTART, C_QUADROWS, C_GROUPROWS = 0, 128, 160, 168, 232, 296, 360, 368, 433, 437
C_END = C_GROUPROWS + 4


class Named:
    pass


def quad_chunk(c, width):
    return slice(c * BANK, min((c + 1) * BANK, width))


def semaphores_of_part(nc, ctx, tag):
    made = []

    def clear_all():
        nc.all_engine_barrier(sems_to_clear=range(FIRST_SEMAPHORE, FIRST_SEMAPHORE + len(made)))
        for s in reversed(made):
            nc.release_semaphore(s)

    def sem(name):
        made.append(nc.alloc_semaphore(tag + name, num=FIRST_SEMAPHORE + len(made)))
        return made[-1]

    ctx.callback(clear_all)
    return sem


def number_jobs(jobs, n_before):
    table = {}
    for kind in ("first", "mid", "last"):
        found, n = {}, 0
        for s in range(SLOTS):
            m, slot = divmod(s, PAIRS)
            for i, pos in enumerate("ba"):
                job = jobs[m][2 * slot + i]
                finishes = job is not None and job[0] in ("norm", "out")
                if job is None or (kind == "first" and finishes and s < 7) or (kind == "last" and m == 1 and not finishes):
                    continue
                found[s, pos] = (job, n)
                n += 1
        table[kind] = found
    per_body = len(table["mid"])
    skipped = per_body - len(table["first"])

    def base(kind, k):
        return n_before if kind == "first" else k * per_body + n_before - skipped

    return table, base


def number_after(table, base, k, kind, s, pos):
    if s < 0:
        return base(kind, k) - len(table["mid"]) + table["mid"][s + SLOTS, pos][1] + 1
    return base(kind, k) + table[kind][s, pos][1] + 1


def attend(nc, g, lay, ctx):
    tag = lay.tag

    def sb(name, shape, dt=F32):
        return ctx.enter_context(nc.sbuf_tensor(tag + name, shape, dt))

    sem = semaphores_of_part(nc, ctx, tag)

    keys, tiles = lay.keys, lay.tiles
    groups = [tiles[4 * c:4 * c + 4] for c in range(CHUNKS)]
    prob = [sb(f"prob{i}", [P, keys]) for i in range(2)]
    prob_t = [sb(f"prob_t{i}", [P, len(tiles), BANK]) for i in range(2)]
    chunk_max = sb("chunk_max", [P, 2, CHUNKS])
    neg_max = sb("neg_max", [P, 2])
    sums = sb("sums", [P, 2, QUAD, CHUNKS])
    den = sb("den", [P, QUAD])
    rden = sb("rden", [P, QUAD])
    diag = sb("diag", [P, QUAD, P])
    norm = sb("norm", [P, lay.norm_cols])

    score_ps = ctx.enter_context(nc.psum_tensor(tag + "score_ps", [P, CHUNKS * BANK], F32))
    turn_ps = [ctx.enter_context(nc.psum_tensor(f"{tag}turn_ps{i}", [P, BANK], F32)) for i in range(2)]
    pv_ps = ctx.enter_context(nc.psum_tensor(tag + "pv_ps", [P, BANK], F32))
    scratch = ctx.enter_context(nc.psum_tensor(tag + "scratch", [P, BANK], F32))

    scratch_ready, scratch_free, half_taken = sem("scratch_ready"), sem("scratch_free"), sem("half_taken")
    scores_ready, chunk_max_done, neg_max_done, exp_done = (sem(n) for n in ("scores", "chunk_max", "neg_max", "exp"))
    turned, copied_dve, copied_act = sem("turned"), sem("copied_dve"), sem("copied_act")
    den_done, rden_done, diag_done, pv_done = (sem(n) for n in ("den", "rden", "diag", "pv"))
    pv_taken = sem("pv_taken")

    own = Named()
    own.sb, own.sem, own.score_ps, own.turn_ps = sb, sem, score_ps, turn_ps
    own.pv_ps, own.scratch, own.prob_t, own.norm = pv_ps, scratch, prob_t, norm
    own.scratch_ready, own.scratch_free, own.half_taken, own.scores_ready = scratch_ready, scratch_free, half_taken, scores_ready
    own.pv_done, own.pv_taken = pv_done, pv_taken
    own.rden_done = rden_done
    lay.allocate(own)
    prepare = [j for j in lay.jobs[0] if j and j[0] not in ("norm", "out")]
    table, base = number_jobs(lay.jobs, len(prepare))
    own.table, own.base = table, base
    own.number_after = lambda k, kind, s, pos: number_after(table, base, k, kind, s, pos)

    ctx.enter_context(nc.allow_non_contiguous_dma(reason="vectors: one element per partition"))
    block = ctx.enter_context(nc.Block())
    ident = g.consts[:, C_IDENT:C_IDENT + P]

    def quad_of(i):
        return i // QUADS % 2, i % QUADS

    @block.sync
    def _(sp):
        lay.sync_start(sp)
        for kind, ks in (("first", 0), ("mid", None)):
            if ks is None:
                with sp.Fori(1, BODIES - 1) as k:
                    lay.sync_body(sp, k, kind)
            else:
                lay.sync_body(sp, ks, kind)
        lay.sync_body(sp, BODIES - 1, "last")
        lay.sync_end(sp)

    @block.gpsimd
    def _(pool):
        def make_diag(q, taken):
            pool.wait_ge(rden_done, q + 1)
            if taken is not None:
                pool.wait_ge(scratch_free, taken)
            if lay.split_diag:
                lay.split_diag(pool, q, rden, ident, diag_done)
                return
            nc.gpsimd.tensor_tensor(diag[:], ident.unsqueeze(1).broadcast_to([P, QUAD, P]),
                                    rden[:].unsqueeze(2).broadcast_to([P, QUAD, P]), ALU.mult).then_inc(diag_done, 1)

        def body(k, kind):
            for m in range(2):
                if not (kind == "first" and m == 0):
                    make_diag(4 * k + 2 * m - 1, own.number_after(k, kind, PAIRS * m - 1, "a"))
                if not (kind == "last" and m == 1):
                    lay.pool_prepare(pool, k, kind, m)
                make_diag(4 * k + 2 * m, None if kind == "first" and m == 0 else own.number_after(k, kind, PAIRS * m + 3, "a"))

        lay.pool_start(pool)
        body(0, "first")
        with pool.Fori(1, BODIES - 1) as k:
            body(k, "mid")
        body(BODIES - 1, "last")
        make_diag(2 * BATCH - 1, own.number_after(BODIES - 1, "last", 15, "a"))

    @block.tensor
    def _(pe):
        def job(what, n, m, kind, k, s):
            if not (isinstance(n, int) and n == 0):
                pe.wait_ge(scratch_free, n)
            if what[0] == "norm":
                pe.wait_ge(diag_done, 4 * k + (s - 7) // QUAD + 1)
                lay.pe_norm(pe, diag).then_inc(scratch_ready, 1)
            else:
                lay.pe_job(pe, what, m, kind, k, s).then_inc(scratch_ready, 1)

        def turn(k, kind, s, c):
            pair = k * SLOTS + s - 1
            first = kind == "first" and s == 1
            if c == 0 and not first:
                pe.wait_ge(copied_act, pair)
            if c == 1 and not first:
                pe.wait_ge(copied_dve, 3 * pair)
            if c >= 2:
                pe.wait_ge(copied_dve, 3 * pair + c - 1)
            for i, (rows, col) in enumerate(groups[c]):
                last = nc.tensor.transpose(turn_ps[c % 2][0:rows, P * i:P * i + P], prob[(s - 1) % 2][:, col:col + rows], ident)
            last.then_inc(turned, 1)

        def weigh_values(k, i, part):
            q = 4 * k + i
            m, u = quad_of(i)
            if part == 0:
                pe.wait_ge(copied_dve, (q + 1) * QUAD * 3)
                pe.wait_ge(copied_act, (q + 1) * QUAD)
                if not (isinstance(q, int) and q == 0):
                    pe.wait_ge(pv_taken, q)
            last = lay.pe_values(pe, m, u, range(4 * part, min(4 * part + 4, len(tiles))))
            last.then_inc(pv_done, 1)

        def body(k, kind):
            for s in range(SLOTS):
                m, n = divmod(s, PAIRS)
                u, j = divmod(n, QUAD)
                pair = k * SLOTS + s
                before = not (kind == "first" and s == 0)
                if j == 0:
                    lay.pe_operands_ready(pe, k, kind, m, u)
                for c in range(CHUNKS):
                    if before:
                        pe.wait_ge(exp_done, (pair - 1) * CHUNKS + c + 1)
                    cols = slice(c * BANK, min(c * BANK + BANK, keys + keys % 2))
                    passes = lay.score_passes(m, u, j)
                    for i, (queries, keys_t) in enumerate(passes):
                        mm = nc.tensor.matmul(score_ps[:, cols], queries, keys_t[:, cols], start=(i == 0), stop=(i == len(passes) - 1))
                    mm.then_inc(scores_ready, 1)
                    if before and c != 2:
                        turn(k, kind, s, min(c, 2))
                    if c == 2 and (s, "b") in table[kind]:
                        what, number = table[kind][s, "b"]
                        job(what, base(kind, k) + number, m, kind, k, s)
                i, part = (s // QUAD - 1, s % QUAD - 1) if s % QUAD else (s // QUAD - 2, CHUNKS - 1)
                if not (kind == "first" and i < 0):
                    weigh_values(k, i, part)
                if (s, "a") in table[kind]:
                    what, number = table[kind][s, "a"]
                    job(what, base(kind, k) + number, m, kind, k, s)
                if before:
                    turn(k, kind, s, CHUNKS - 1)

        lay.pe_start(pe)
        for n, what in enumerate(prepare):
            job(what, n, 1, "start", 0, 0)
        body(0, "first")
        with pe.Fori(1, BODIES - 1) as k:
            body(k, "mid")
        body(BODIES - 1, "last")
        for c in range(CHUNKS):
            pe.wait_ge(exp_done, (BATCH * PAIRS - 1) * CHUNKS + c + 1)
            turn(BODIES, "mid", 0, c)
        weigh_values(BODIES, -2, CHUNKS - 1)
        job(("norm",), base("last", BODIES - 1) + len(table["last"]), 0, "mid", BODIES, 3)
        for part in range(CHUNKS):
            weigh_values(BODIES, -1, part)
        if lay.last_output:
            job(("out",), base("last", BODIES - 1) + len(table["last"]) + 1, 0, "mid", BODIES, 5)

    @block.scalar
    def _(act):
        def take(what, n, m, q):
            act.wait_ge(scratch_ready, n + 1)
            if what[0] == "norm":
                if not (isinstance(q, int) and q == 0):
                    act.wait_ge(pv_taken, q)
                nc.scalar.activation(norm[:], scratch[:, 0:lay.norm_cols], ACT.Copy).then_inc(scratch_free, 1)
            else:
                lay.act_take(act, what, m)

        def at(k, kind, s, pos):
            if (s, pos) in table[kind]:
                what, n = table[kind][s, pos]
                take(what, base(kind, k) + n, (s // PAIRS + 1) % 2, 4 * k + (s - 7) // QUAD)

        def copy_turned(k, kind, s):
            pair = k * SLOTS + s - 1
            u, j = (s - 1) // QUAD % QUADS, (s - 1) % QUAD
            act.wait_ge(turned, pair * CHUNKS + 3)
            if j == 0 and not (kind == "first" and s < 2 * QUAD):
                act.wait_ge(pv_done, CHUNKS * (4 * k + (s - 1) // QUAD - 1))
            nc.scalar.activation(prob_t[u][:, 8:12, P * j:P * j + P], turn_ps[0][:].rearrange("p (t q) -> p t q", t=4),
                                 ACT.Copy).then_inc(copied_act, 1)

        def body(k, kind):
            for s in range(SLOTS):
                at(k, kind, s, "b")
                if not (kind == "first" and s == 0):
                    copy_turned(k, kind, s)
                pair, j = k * SLOTS + s, s % QUAD
                if not (kind == "first" and s < 2):
                    act.wait_ge(turned, (pair - 1) * CHUNKS)
                if j == 0 and not (kind == "first" and s < 2 * QUAD):
                    act.wait_ge(den_done, 4 * k + s // QUAD - 1)
                act.wait_ge(neg_max_done, pair + 1)
                for c in range(CHUNKS):
                    cols = quad_chunk(c, keys)
                    nc.scalar.activation(prob[s % 2][:, cols], score_ps[:, cols], ACT.Exp, bias=neg_max[:, s % 2:s % 2 + 1],
                                         accum_out=sums[:, (s // QUAD) % 2, j, c:c + 1]).then_inc(exp_done, 1)
                    if c == 1:
                        at(k, kind, s, "a")

        lay.act_start(act)
        for n, what in enumerate(prepare):
            take(what, n, 0, None)
        body(0, "first")
        with act.Fori(1, BODIES - 1) as k:
            body(k, "mid")
        body(BODIES - 1, "last")
        copy_turned(BODIES, "mid", 0)
        take(("norm",), base("last", BODIES - 1) + len(table["last"]), 0, 2 * BATCH - 1)

    @block.vector
    def _(dve):
        def maximum(k, s, c):
            dve.wait_ge(scores_ready, (k * SLOTS + s) * CHUNKS + c + 1)
            nc.vector.reduce_max(chunk_max[:, s % 2, c:c + 1], score_ps[:, quad_chunk(c, keys)], AX_X).then_inc(chunk_max_done, 1)

        def copy_turned(k, kind, s, c):
            pair = k * SLOTS + s - 1
            u, j = (s - 1) // QUAD % QUADS, (s - 1) % QUAD
            if c == 0 and j == 0 and not (kind == "first" and s < 2 * QUAD):
                dve.wait_ge(pv_done, CHUNKS * (4 * k + (s - 1) // QUAD - 1))
            dve.wait_ge(turned, pair * CHUNKS + c + 1)
            if c < 3:
                last = nc.vector.tensor_copy(prob_t[u][:, 4 * c:4 * c + 4, P * j:P * j + P],
                                             turn_ps[c][:].rearrange("p (t q) -> p t q", t=4))
            else:
                for i, (rows, _) in enumerate(groups[c]):
                    last = nc.vector.tensor_copy(prob_t[u][0:rows, 12 + i, P * j:P * j + P], turn_ps[1][0:rows, P * i:P * i + P])
            last.then_inc(copied_dve, 1)

        def denominators(q, par):
            dve.wait_ge(exp_done, (q + 1) * QUAD * CHUNKS)
            if not (isinstance(q, int) and q == 0):
                dve.wait_ge(diag_done, q)
            nc.vector.tensor_reduce(den[:], sums[:, par], AX_X, ALU.add).then_inc(den_done, 1)
            dve.wait_ge(den_done, q + 1)
            nc.vector.reciprocal(rden[:], den[:]).then_inc(rden_done, 1)

        def finish_quad(k, i, taken):
            q = 4 * k + i
            dve.wait_ge(pv_done, CHUNKS * (q + 1))
            dve.wait_ge(scratch_free, taken)
            lay.dve_finish(dve, q, i, k)

        def body(k, kind):
            for s in range(SLOTS):
                before = not (kind == "first" and s == 0)
                maximum(k, s, 0)
                lay.dve_between(dve, k, kind, s, 0)
                if s and (s - 1, "a") in table[kind]:
                    lay.dve_take(dve, table[kind][s - 1, "a"], base(kind, k), k, kind, s - 1)
                if before:
                    copy_turned(k, kind, s, 0)
                for c in range(1, CHUNKS):
                    maximum(k, s, c)
                    if c < CHUNKS - 1:
                        lay.dve_between(dve, k, kind, s, c)
                pair = k * SLOTS + s
                dve.wait_ge(chunk_max_done, (pair + 1) * CHUNKS)
                if not (kind == "first" and s < 2):
                    dve.wait_ge(exp_done, (pair - 1) * CHUNKS)
                nc.vector.tensor_reduce(neg_max[:, s % 2:s % 2 + 1], chunk_max[:, s % 2, :], AX_X, ALU.max,
                                        negate=True).then_inc(neg_max_done, 1)
                if (s, "b") in table[kind]:
                    lay.dve_take(dve, table[kind][s, "b"], base(kind, k), k, kind, s)
                if before:
                    copy_turned(k, kind, s, 1)
                    copy_turned(k, kind, s, 3)
                if s % QUAD == 1 and not (kind == "first" and s < QUAD):
                    denominators(4 * k + s // QUAD - 1, (s // QUAD - 1) % 2)
                if s % QUAD == 0 and not (kind == "first" and s < 2 * QUAD):
                    finish_quad(k, s // QUAD - 2, own.number_after(k, kind, s - 1, "a"))
                lay.dve_extra(dve, k, kind, s)

        lay.dve_start(dve)
        body(0, "first")
        with dve.Fori(1, BODIES - 1) as k:
            body(k, "mid")
        body(BODIES - 1, "last")
        for c in (0, 1, 3):
            copy_turned(BODIES, "mid", 0, c)
        denominators(2 * BATCH - 1, 1)
        finish_quad(BODIES, -2, own.number_after(BODIES - 1, "last", 15, "a"))
        finish_quad(BODIES, -1, base("last", BODIES - 1) + len(table["last"]) + 1)
        lay.dve_end(dve)


def cross_attention_0(nc, g, dram):
    SCALE = E0 ** -0.5
    N_LOADED = 16 * (2 + 4 + 3 + 2 * QUAD)
    lay = Named()
    lay.tag, lay.keys, lay.norm_cols, lay.last_output = "a_", CTX, P, False
    lay.tiles = [(P if t < FULL else TAIL, P * t) for t in range(FULL + 1)]
    widths = [min(BANK, CTX - BANK * c) for c in range(CHUNKS)]
    jobs = [("ctx_t", 0), ("ctx_t", 1), ("ctx_t", 2), ("ctx_t", 3), None, ("k", 0), ("v", 0), ("norm",),
            ("v", 1), ("k", 1), None, ("k", 2), None, ("tail",), ("v", 2), ("norm",)]
    lay.jobs = [jobs, jobs]
    K_JOBS = 4
    k_number = {job: i for i, job in enumerate(j for j in jobs if j and j[0] in ("k", "tail"))}

    with ExitStack() as ctx:
        t = Named()

        def allocate(own):
            sb, sem = own.sb, own.sem
            lay.own = own
            t.xn = sb("xn", [P, TOK_TILES, D])
            t.xn_t = sb("xn_t", [P, TOKENS])
            t.stats = sb("stats", [P, TOK_TILES, 6])
            t.mean_var = sb("mean_var", [P, TOK_TILES, 2])
            t.rstd = sb("rstd", [P, TOK_TILES])
            t.half = sb("half", [P, TOK_TILES])
            t.wq2 = sb("wq2", [P, QUADS, 2, 64])
            t.wk, t.bk = sb("wk", [P, D]), sb("bk", [P, 1])
            t.wv = sb("wv", [P, D])
            t.bq2, t.bqs, t.bv_rows = (sb(n, [P, QUADS]) for n in ("bq2", "bqs", "bv_rows"))
            t.q2 = sb("q2", [P, QUADS, TOKENS])
            t.q_hi = sb("q_hi", [P, QUADS, TOKENS])
            t.q_lo = sb("q_lo", [P, QUADS, TOKENS])
            t.q_bd = sb("q_bd", [P, 2, QUADS, 2, 8, SEQ], F32R)
            t.ctx = sb("ctx", [P, FULL + 1, D])
            t.ctx_t = sb("ctx_t", [P, CTX])
            t.k_sp = [[sb(f"k{m}{u}", [P, CTX + 1], F32R) for u in range(QUADS)] for m in range(2)]
            t.val = [sb(f"val{m}", [P, FULL + 1, D + 16]) for m in range(2)]
            t.heads = sb("heads", [P, P])
            t.loaded, t.ctx_loaded, t.zeroed, t.stat, t.aggr = (sem(n) for n in ("loaded", "ctx_loaded", "zeroed", "stat", "aggr"))
            t.eps, t.rstd_done, t.xn_done, t.xn_turned, t.xn_t_done = (sem(n) for n in ("eps", "rstd_done", "xn_done", "xn_turned", "xn_t_done"))
            t.q_proj, t.q_done, t.q_split, t.bqs_done, t.pads_set = (sem(n) for n in ("q_proj", "q_done", "q_split", "bqs_done", "pads_set"))
            t.q_bd_done, t.masked, t.weights_loaded = sem("q_bd_done"), sem("masked"), sem("weights_loaded")

        lay.allocate = allocate

        def load_ctx(sp, b):
            sp.dma_start(t.ctx[:, 0:FULL, :],
                         dram.ctx[bass.ds(b, 1), 0:FULL * P, :].rearrange("o (p t) d -> p (o t) d", t=FULL)).then_inc(t.ctx_loaded, 16)
            sp.dma_start(t.ctx[0:TAIL, FULL, :],
                         dram.ctx[bass.ds(b, 1), FULL * P:CTX, :].rearrange("o p d -> p (o d)")).then_inc(t.ctx_loaded, 16)

        def sync_start(sp):
            own = lay.own
            sp.dma_start(g.x_tok[:], dram.x.rearrange("(t b) s d -> (b s) t d", b=2)).then_inc(t.loaded, 16)
            sp.dma_start(g.consts[:], dram.consts).then_inc(t.loaded, 16)
            load_ctx(sp, 0)
            for half in range(2):
                rows = slice(64 * half, 64 * half + 64)
                sp.dma_start(t.bq2[rows, :], dram.L0_xattn_bq.rearrange("(u r) -> r u", u=QUADS)).then_inc(t.loaded, 16)
                sp.dma_start(t.wq2[:, :, half, :], dram.L0_xattn_wq.rearrange("d (u r) -> d u r", u=QUADS)).then_inc(t.loaded, 16)
            sp.dma_start(t.wk[:], dram.L0_xattn_wk).then_inc(t.loaded, 16)
            sp.dma_start(t.bk[:], dram.L0_xattn_bk.rearrange("(r o) -> r o", o=1)).then_inc(t.loaded, 16)
            sp.dma_start(t.wv[:], dram.L0_xattn_wv).then_inc(t.loaded, 16)
            sp.wait_ge(t.zeroed, 5)
            for j in range(QUAD):
                sp.dma_start(t.bv_rows[32 * j:32 * j + 16, :],
                             dram.L0_xattn_bv.rearrange("(u j r) -> j r u", u=QUADS, j=QUAD)[j]).then_inc(t.loaded, 16)
                sp.dma_start(g.wo_rows[32 * j:32 * j + 16, :, :],
                             dram.L0_xattn_wo.rearrange("(u j r) n -> j r u n", u=QUADS, j=QUAD)[j]).then_inc(t.loaded, 16)
            sp.wait_ge(own.scratch_ready, CHUNKS)
            load_ctx(sp, 1)
            load_rest_0(sp, g, dram, t.weights_loaded)

        def sync_end(sp):
            sp.wait_ge(t.weights_loaded, LOADS_0)

        def sync_body(sp, k, kind):
            if kind != "last":
                for m in range(2):
                    sp.wait_ge(lay.own.scratch_ready, lay.own.number_after(k, kind, PAIRS * m + 1, "a"))
                    load_ctx(sp, 2 * k + m + 2)

        lay.sync_start, lay.sync_body, lay.sync_end = sync_start, sync_body, sync_end

        def block_diagonal(b, m):
            heads = g.consts[:, C_HEADROWS:C_HEADROWS + 8].unsqueeze(2).broadcast_to([P, 8, SEQ])
            for u in range(QUADS):
                for part, q in enumerate((t.q_hi, t.q_lo)):
                    mine = q[:, u, bass.ds(b * SEQ, SEQ)].unsqueeze(1).broadcast_to([P, 8, SEQ])
                    nc.gpsimd.tensor_tensor(t.q_bd[:, m, u, part], mine, heads, ALU.mult).then_inc(t.q_bd_done, 1)

        def pool_start(pool):
            nc.gpsimd.memset(t.half[:], -0.5).then_inc(t.zeroed, 1)
            nc.gpsimd.memset(t.bv_rows[:], 0.0).then_inc(t.zeroed, 1)
            nc.gpsimd.memset(g.wo_rows[:], 0.0).then_inc(t.zeroed, 1)
            for m in range(2):
                nc.gpsimd.memset(t.val[m][:, :, D:], 0.0).then_inc(t.zeroed, 1)
            pool.wait_ge(t.eps, 1)
            pool.wait_ge(t.zeroed, 5)
            nc.gpsimd.tensor_tensor(t.rstd[:], t.rstd[:], t.half[:], ALU.pow).then_inc(t.rstd_done, 1)
            pool.wait_ge(t.q_split, 2 * QUADS)
            block_diagonal(0, 0)

        def pool_prepare(pool, k, kind, m):
            b = 2 * k + m + 1
            if not (kind == "first" and m == 0):
                pool.wait_ge(lay.own.scores_ready, (b - 1) * PAIRS * CHUNKS)
            block_diagonal(b, (m + 1) % 2)

        lay.pool_start, lay.pool_prepare = pool_start, pool_prepare

        def q_bank(own, i):
            return (own.score_ps[:, 2 * BANK:3 * BANK], own.score_ps[:, 3 * BANK:4 * BANK], own.turn_ps[0][:], own.turn_ps[1][:])[i]

        def pe_start(pe):
            own = lay.own
            pe.wait_ge(t.loaded, N_LOADED)
            for i in range(TOK_TILES):
                pe.wait_ge(t.xn_done, i + 1)
                nc.tensor.transpose(own.score_ps[:, P * i:P * i + P], t.xn[:, i, :], g.consts[:, C_IDENT:C_IDENT + P]).then_inc(t.xn_turned, 1)
            for c in range(2):
                pe.wait_ge(t.xn_t_done, c + 1)
            for u in range(QUADS):
                for c in range(2):
                    nc.tensor.matmul(q_bank(own, 2 * u + c), t.wq2[:, u], t.xn_t[:, c * BANK:c * BANK + BANK],
                                     start=True, stop=True).then_inc(t.q_proj, 1)
            pe.wait_ge(t.q_done, 2 * QUADS)
            pe.wait_ge(t.pads_set, 2 * QUADS)

        def values(pe, tiles, c0):
            for i, (rows, col) in enumerate(tiles):
                last = nc.tensor.matmul(lay.own.scratch[0:rows, c0 + P * i:c0 + P * i + D], t.ctx_t[:, col:col + rows], t.wv[:],
                                        start=True, stop=True)
            return last

        def pe_job(pe, what, m, kind, k, s):
            scratch = lay.own.scratch
            if what[0] == "ctx_t":
                c = what[1]
                if c == 0:
                    pe.wait_ge(t.ctx_loaded, 32 if kind == "start" else (2 * k + m + 2) * 32)
                for i in range(4 * c, min(4 * c + 4, FULL + 1)):
                    rows = lay.tiles[i][0]
                    last = nc.tensor.transpose(scratch[:, P * (i - 4 * c):P * (i - 4 * c) + rows], t.ctx[0:rows, i, :],
                                               g.consts[0:rows, C_IDENT:C_IDENT + rows])
                return last
            if what[0] == "k":
                return nc.tensor.matmul(scratch[:, 0:BANK], t.wk[:], t.ctx_t[:, quad_chunk(what[1], CTX)], start=True, stop=True)
            if what[0] == "v":
                return values(pe, lay.tiles[4 * what[1]:4 * what[1] + 4], 0)
            nc.tensor.matmul(scratch[:, 0:TAIL], t.wk[:], t.ctx_t[:, quad_chunk(3, CTX)], start=True, stop=True)
            return values(pe, lay.tiles[FULL:], 2 * P)

        def pe_norm(pe, diag):
            for j in range(QUAD):
                last = nc.tensor.matmul(lay.own.scratch[32 * j:32 * j + 32, 0:P], g.consts[:, C_PAIRROWS:C_PAIRROWS + 32],
                                        diag[:, j, :], start=True, stop=True)
            return last

        def pe_operands_ready(pe, k, kind, m, u):
            pe.wait_ge(t.q_bd_done, (2 * k + m) * 4 + 2 * u + 2)
            if u == 0 and not (kind == "first" and m == 0):
                pe.wait_ge(lay.own.scratch_free, lay.own.number_after(k, kind, PAIRS * m - 1, "b"))
            elif u == 0:
                pe.wait_ge(lay.own.scratch_free, len([j for j in jobs if j and j[0] != "norm"]))

        def pe_values(pe, m, u, tiles):
            for i in tiles:
                rows = lay.tiles[i][0]
                for j in range(QUAD):
                    v0 = 16 * (QUAD * u + j)
                    last = nc.tensor.matmul(lay.own.pv_ps[32 * j:32 * j + 32, 0:P], t.val[m][0:rows, i, v0:v0 + 32],
                                            lay.own.prob_t[u][0:rows, i, P * j:P * j + P], start=(i == 0), stop=(i == FULL))
            return last

        lay.pe_start, lay.pe_job, lay.pe_norm, lay.split_diag = pe_start, pe_job, pe_norm, None
        lay.pe_operands_ready, lay.pe_values = pe_operands_ready, pe_values
        lay.score_passes = lambda m, u, j: [(t.q_bd[:, m, u, part, 2 * j:2 * j + 2, :], t.k_sp[m][u]) for part in range(2)]

        def act_start(act):
            own = lay.own
            act.wait_ge(t.loaded, N_LOADED)
            act.wait_ge(t.bqs_done, 1)
            for u in range(QUADS):
                for c in range(2):
                    act.wait_ge(t.q_proj, 2 * u + c + 1)
                    nc.scalar.activation(t.q2[:, u, c * BANK:c * BANK + BANK], q_bank(own, 2 * u + c), ACT.Identity,
                                         bias=t.bqs[:, u:u + 1], scale=SCALE).then_inc(t.q_done, 1)

        def keys_high(c, m):
            for u in range(QUADS):
                rows = slice(64 * u, 64 * u + 64)
                last = nc.scalar.activation(t.k_sp[m][u][rows, quad_chunk(c, CTX)], lay.own.scratch[rows, 0:widths[c]], ACT.Identity,
                                            bias=t.bk[rows, :])
            last.then_inc(lay.own.half_taken, 1)

        def act_take(act, what, m):
            own = lay.own
            scratch = own.scratch
            if what[0] == "ctx_t":
                c = what[1]
                nc.scalar.activation(t.ctx_t[:, quad_chunk(c, CTX)], scratch[:, 0:widths[c]], ACT.Copy).then_inc(own.scratch_free, 1)
            elif what[0] == "k":
                keys_high(what[1], m)
            elif what[0] == "v":
                c = what[1]
                nc.scalar.activation(t.val[m][:, 4 * c:4 * c + 4, 0:D], scratch[:].rearrange("p (t d) -> p t d", t=4),
                                     ACT.Copy).then_inc(own.scratch_free, 1)
            else:
                nc.scalar.activation(t.val[m][0:TAIL, FULL, 0:D], scratch[0:TAIL, 2 * P:3 * P], ACT.Copy)
                keys_high(3, m)

        lay.act_start, lay.act_take = act_start, act_take

        def keys_low(dve, what, b, m):
            own = lay.own
            dve.wait_ge(own.half_taken, K_JOBS * b + k_number[what] + 1)
            c = what[1] if what[0] == "k" else 3
            for u in range(QUADS):
                rows, others = slice(64 * u, 64 * u + 64), slice(64 - 64 * u, P - 64 * u)
                last = nc.vector.scalar_tensor_tensor(t.k_sp[m][u][others, quad_chunk(c, CTX)], own.scratch[rows, 0:widths[c]],
                                                      t.bk[rows, :], t.k_sp[m][u][rows, quad_chunk(c, CTX)].bitcast(F32),
                                                      ALU.add, ALU.subtract)
            last.then_inc(own.scratch_free, 1)

        def dve_take(dve, entry, base, k, kind, s):
            what = entry[0]
            if what[0] in ("k", "tail"):
                m = s // PAIRS
                keys_low(dve, what, 2 * k + m + 1, (m + 1) % 2)

        def dve_start(dve):
            own = lay.own
            for m in range(2):
                for u in range(QUADS):
                    nc.vector.memset(t.k_sp[m][u][:, CTX:CTX + 1].bitcast(U32), 0).then_inc(t.pads_set, 1)
            dve.wait_ge(t.loaded, N_LOADED)
            nc.vector.tensor_scalar(t.bqs[:], t.bq2[:], SCALE, None, ALU.mult).then_inc(t.bqs_done, 1)
            for i in range(TOK_TILES):
                nc.vector.bn_stats(t.stats[:, i, :], g.x_tok[:, i, :]).then_inc(t.stat, 1)
            dve.wait_ge(t.stat, TOK_TILES)
            for i in range(TOK_TILES):
                nc.vector.bn_aggr(t.mean_var[:, i, :], t.stats[:, i, :]).then_inc(t.aggr, 1)
            dve.wait_ge(t.aggr, TOK_TILES)
            nc.vector.tensor_scalar(t.rstd[:], t.mean_var[:, :, 1], LN_EPS, None, ALU.add).then_inc(t.eps, 1)
            dve.wait_ge(t.rstd_done, 1)
            for i in range(TOK_TILES):
                nc.vector.tensor_scalar(t.xn[:, i, :], g.x_tok[:, i, :], t.mean_var[:, i, 0:1], t.rstd[:, i:i + 1],
                                        ALU.subtract, ALU.mult).then_inc(t.xn_done, 1)
            for c in range(2):
                dve.wait_ge(t.xn_turned, 4 * c + 4)
                nc.vector.tensor_copy(t.xn_t[:, c * BANK:c * BANK + BANK], own.score_ps[:, c * BANK:c * BANK + BANK]).then_inc(t.xn_t_done, 1)
            for u in range(QUADS):
                dve.wait_ge(t.q_done, 2 * u + 2)
                nc.vector.tensor_copy(t.q_hi[:, u, :].bitcast(F32R), t.q2[:, u, :]).then_inc(t.q_split, 1)
                dve.wait_ge(t.q_split, 2 * u + 1)
                nc.vector.tensor_tensor(t.q_lo[:, u, :], t.q2[:, u, :], t.q_hi[:, u, :], ALU.subtract).then_inc(t.q_split, 1)
            for what in jobs:
                if what and what[0] in ("k", "tail"):
                    keys_low(dve, what, 0, 0)

        def dve_finish(dve, q, i, k):
            own = lay.own
            b, u = 2 * k + i // QUADS, i % QUADS
            nc.vector.tensor_tensor(t.heads[:], own.pv_ps[:, 0:P], own.norm[:], ALU.mult).then_inc(t.masked, 1)
            dve.wait_ge(t.masked, q + 1)
            nc.vector.scalar_tensor_tensor(g.act_t[:, u, bass.ds(b * SEQ, SEQ)], t.heads[:, 0:SEQ], t.bv_rows[:, u:u + 1],
                                           t.heads[:, SEQ:P], ALU.add, ALU.add).then_inc(own.pv_taken, 1)

        lay.dve_start, lay.dve_take, lay.dve_finish = dve_start, dve_take, dve_finish
        lay.dve_between = lay.dve_extra = lambda *a: None
        lay.dve_end = lambda dve: None
        attend(nc, g, lay, ctx)


EXPERTS, FF_BLOCKS = 8, 4
LOADS_0, LOADS_1 = 16 * 8, 16 * 11
WIDTH = 4
ROUNDS = TOK_TILES // WIDTH
BANK_SETS = 2


def scope(nc, ctx, tag):
    def sb(name, shape, dt=F32):
        return ctx.enter_context(nc.sbuf_tensor(tag + name, shape, dt))

    def pair(name, shape, dt=F32):
        return [sb(f"{name}{j}", shape, dt) for j in range(WIDTH)]

    def bank(name, shape, n=BANK_SETS):
        return [ctx.enter_context(nc.psum_tensor(f"{tag}{name}{j}", shape, F32)) for j in range(n)]

    sem = semaphores_of_part(nc, ctx, tag)

    def sems(names):
        return [sem(n) for n in names.split()]

    return sb, pair, bank, sem, sems


def rest_0_buffers(sb):
    return (sb("raw_0", [P, 4, D]), sb("router", [EXPERTS, D]), sb("w1_0", [P, EXPERTS, P]), sb("w2_0", [P, EXPERTS, D]),
            sb("bo", [P, D]), sb("ln2_w", [P, D]), sb("ln2_b", [P, D]))


def load_rest_0(sp, g, dram, loaded):
    raw, router, w1, w2, bo, ln2_w, ln2_b = g.rest_0
    for dst, src in ((raw[:, 0:3, :], dram.L0_attn_W_KQV.rearrange("(m k) d -> k m d", k=P)),
                     (raw[:, 3, :], dram.L0_attn_W_O),
                     (router[:], dram.L0_ffn_router_w),
                     (w1[:], dram.L0_ffn_w1.rearrange("d (e w) -> d e w", e=EXPERTS)),
                     (w2[:], dram.L0_ffn_w2.rearrange("(e w) d -> w e d", e=EXPERTS)),
                     (bo[:], dram.L0_xattn_bo.partition_broadcast(P)),
                     (ln2_w[:], dram.L1_xattn_ln2_w.partition_broadcast(P)),
                     (ln2_b[:], dram.L1_xattn_ln2_b.partition_broadcast(P))):
        sp.dma_start(dst, src).then_inc(loaded, 16)


def rest_1_buffers(sb):
    return (sb("raw_1", [P, 4, D]), sb("mix", [P, 1]), sb("decay_in", [P, 1]), sb("first_in", [P, 1]),
            sb("w1_1", [P, FF_BLOCKS * P]), sb("b1", [P, FF_BLOCKS]), sb("w2_1", [P, FF_BLOCKS, D]), sb("b2", [P, D]))


def load_rest_1(sp, g, dram, loaded):
    raw, mix, decay_in, first_in, w1, b1, w2, b2 = g.rest_1
    for dst, src in ((raw[:, 0, :], dram.L1_attn_Wk), (raw[:, 1, :], dram.L1_attn_Wv),
                     (raw[:, 2, :], dram.L1_attn_Wr), (raw[:, 3, :], dram.L1_attn_Wo),
                     (mix[:], dram.L1_attn_time_mix.rearrange("a b d -> d (a b)")),
                     (decay_in[:], dram.L1_attn_time_decay.broadcast_to([HEADS, E0])),
                     (first_in[:], dram.L1_attn_time_first.broadcast_to([HEADS, E0])),
                     (w1[:], dram.L1_ffn_w1),
                     (b1[:], dram.L1_ffn_b1.rearrange("(m f) -> f m", f=P)),
                     (w2[:], dram.L1_ffn_w2.rearrange("(m f) d -> f m d", f=P)),
                     (b2[:], dram.L1_ffn_b2.partition_broadcast(P))):
        sp.dma_start(dst, src).then_inc(loaded, 16)


def tile_of(x_tok, tile):
    return x_tok[:, bass.ds(tile, 1), :].rearrange("p o d -> p (o d)")


def wait_apart(engine, sem, count, waits):
    engine.wait_ge(sem, count)
    engine.sem_inc(waits, 1)


def bank_is_read(pe, read, read_before, k, j):
    if j >= BANK_SETS:
        pe.wait_ge(read, WIDTH * k + j - BANK_SETS + 1)
    elif read_before is not None:
        pe.wait_ge(read_before, WIDTH * k + j + WIDTH - BANK_SETS + 1)


class Norm:

    def __init__(self, nc, name, pair, sem, half, waits):
        self.nc, self.half, self.waits = nc, half, waits
        self.stats, self.mean_var, self.eps, self.rstd = (pair(name + n, shape) for n, shape in (
            ("_stats", [P, 6]), ("_mean_var", [P, 2]), ("_eps", [P, 1]), ("_rstd", [P, 1])))
        self.out = pair(name + "_out", [P, D])
        self.stat_done, self.aggr_done, self.eps_done, self.rstd_done, self.done = (
            sem(f"{name}_{n}") for n in ("stat_done", "aggr_done", "eps_done", "rstd_done", "done"))

    def statistics(self, dve, j, count, rows):
        self.nc.vector.bn_stats(self.stats[j][:], rows).then_inc(self.stat_done, 1)
        wait_apart(dve, self.stat_done, count, self.waits)
        self.nc.vector.bn_aggr(self.mean_var[j][:], self.stats[j][:]).then_inc(self.aggr_done, 1)
        dve.wait_ge(self.aggr_done, count)
        self.nc.vector.tensor_scalar(self.eps[j][:], self.mean_var[j][:, 1:2], LN_EPS, None, ALU.add).then_inc(self.eps_done, 1)

    def root(self, pool, j, count):
        pool.wait_ge(self.eps_done, count)
        self.nc.gpsimd.tensor_tensor(self.rstd[j][:], self.eps[j][:], self.half[:], ALU.pow).then_inc(self.rstd_done, 1)

    def normalise(self, dve, j, count, rows):
        dve.wait_ge(self.rstd_done, count)
        self.nc.vector.tensor_scalar(self.out[j][:], rows, self.mean_var[j][:, 0:1], self.rstd[j][:], ALU.subtract,
                                     ALU.mult).then_inc(self.done, 1)


def fold_resampler_weights(nc, g, dram):
    TURNED = 3 * PAIRS
    with ExitStack() as ctx:
        sb, _, _, _, sems = scope(nc, ctx, "f_")
        raw, raw_o = sb("raw", [P, TURNED, P]), sb("raw_o", [P, PAIRS, D])
        turned = sb("turned", [P, TURNED, P])
        ps = [ctx.enter_context(nc.psum_tensor(f"f_ps{i}", [P, 4, P], F32)) for i in range(2)]
        s = Named()
        s.loaded, s.turned, s.copied, s.made, s.taken = sems("loaded turned copied made taken")
        GROUPS = TURNED // 4
        ctx.enter_context(nc.allow_non_contiguous_dma(reason="small vectors and permuted weights"))
        block = ctx.enter_context(nc.Block())

        @block.sync
        def _(sp):
            sp.dma_start(raw[:, 0:PAIRS, :], dram.L1_xattn_Wq.rearrange("d (n k) -> d n k", k=P)).then_inc(s.loaded, 16)
            for i in range(2):
                blocks = slice(i * PAIRS, i * PAIRS + PAIRS)
                sp.dma_start(raw[:, PAIRS:3 * PAIRS, :][:, blocks, :],
                             dram.L1_xattn_Wkv.rearrange("d (n k) -> d n k", k=P)[:, blocks, :]).then_inc(s.loaded, 16)
            sp.dma_start(raw_o[:], dram.L1_xattn_Wo.rearrange("(n k) d -> k n d", k=P)).then_inc(s.loaded, 16)

        @block.tensor
        def _(pe):
            pe.wait_ge(s.loaded, 64)
            for i in range(GROUPS):
                if i >= 2:
                    pe.wait_ge(s.copied, i - 1)
                for n in range(4):
                    last = nc.tensor.transpose(ps[i % 2][:, n, :], raw[:, 4 * i + n, :], g.consts[:, C_IDENT:C_IDENT + P])
                last.then_inc(s.turned, 1)
            pe.wait_ge(s.copied, GROUPS)
            for i in range(HEADS // 2):
                if i >= 2:
                    pe.wait_ge(s.taken, i - 1)
                half = slice(64 * (i % 2), 64 * (i % 2) + 64)
                for n in range(2):
                    b = 2 * (i // 2) + n
                    nc.tensor.matmul(ps[i % 2][:, n, :], turned[half, b, :], turned[half, PAIRS + b, :], start=True, stop=True)
                    last = nc.tensor.matmul(ps[i % 2][:, 2 + n, :], turned[half, 2 * PAIRS + b, :], raw_o[half, b, :],
                                            start=True, stop=True)
                last.then_inc(s.made, 1)

        @block.scalar
        def _(act):
            for i in range(0, GROUPS, 2):
                act.wait_ge(s.turned, i + 1)
                nc.scalar.activation(turned[:, 4 * i:4 * i + 4, :], ps[0][:], ACT.Copy).then_inc(s.copied, 1)
                act.wait_ge(s.copied, i + 2)

        @block.vector
        def _(dve):
            for i in range(1, GROUPS, 2):
                dve.wait_ge(s.turned, i + 1)
                dve.wait_ge(s.copied, i)
                nc.vector.tensor_copy(turned[:, 4 * i:4 * i + 4, :], ps[1][:]).then_inc(s.copied, 1)
            for i in range(HEADS // 2):
                heads = slice(i // 2 * 4 + i % 2, i // 2 * 4 + i % 2 + 3, 2)
                dve.wait_ge(s.made, i + 1)
                nc.vector.tensor_copy(g.qk[:, heads, :], ps[i % 2][:, 0:2, :])
                nc.vector.tensor_copy(g.wvo[:, heads, :], ps[i % 2][:, 2:4, :]).then_inc(s.taken, 1)


def rest_of_layer_0(nc, g, dram):
    SCALE = E0 ** -0.5
    with ExitStack() as ctx:
        sb, pair, bank, sem, sems = scope(nc, ctx, "b_")
        ident = g.consts[:, C_IDENT:C_IDENT + P]
        raw, router, w1, w2, bo, ln2_w, ln2_b = g.rest_0
        w_t = sb("w_t", [P, 4, D])
        w_swap = sb("w_swap", [P, 2, D])
        router_t = sb("router_t", [P, EXPERTS])
        half = sb("half", [P, 1])
        heads_t = pair("heads_t", [P, QUADS, P])
        x1, x2, x3 = pair("x1", [P, D]), pair("x2", [P, D]), pair("x3", [P, D])
        xn_t, xn2_t, lat_t = pair("xn_t", [P, P]), pair("xn2_t", [P, P]), pair("lat_t", [P, P])
        rot1, rot2, kq = pair("rot1", [P, 4, SEQ]), pair("rot2", [P, 4, SEQ]), pair("kq", [P, 4, SEQ])
        k_bd = pair("k_bd", [P, 2, 4, SEQ])
        q_bd = pair("q_bd", [P, 4, 2, SEQ])
        v_bd = pair("v_bd", [P, 2 * PAIRS, 16])
        sc = pair("sc", [P, HEADS, SEQ])
        top, den, rden = pair("top", [P, HEADS]), pair("den", [P, HEADS]), pair("rden", [P, HEADS])
        prob_t = pair("prob_t", [P, PAIRS, P])
        attn, attn_t = pair("attn", [P, D]), pair("attn_t", [P, P])
        gate = pair("gate", [P, EXPERTS])
        best, place, place_f = pair("best", [P, 8]), pair("place", [P, 8], U32), pair("place_f", [P, 2])
        total, share = pair("total", [P, 1]), pair("share", [P, 2])
        cw1, cw = pair("cw1", [P, EXPERTS]), pair("cw", [P, EXPERTS])
        relu = [t[:].rearrange("p h k -> p (h k)").rearrange("p (e w) -> p e w", e=EXPERTS) for t in sc]
        act, weighted, mixed = prob_t, relu, pair("mixed", [P, D])
        lat_w, lat = pair("lat_w", [P, D]), pair("lat", [P, D])
        q_out = pair("q_out", [P, 2, HEADS, SEQ])
        ps_a, ps_b, ps_c = bank("ps_a", [P, BANK]), bank("ps_b", [P, BANK]), bank("ps_c", [P, 2 * BANK])
        s = Named()
        s.waits, s.half_set, s.w_turned, s.w_copied = sems("waits half_set w_turned w_copied")
        s.w_swapped, s.staged, s.projected, s.x1_part, s.x1_done = sems("w_swapped staged projected x1_part x1_done")
        s.xn_turned, s.xn_copied, s.qkv_done, s.rot1_done, s.rot2_done = sems("xn_turned xn_copied qkv_done rot1_done rot2_done")
        s.kq_done, s.k_bd_done, s.q_bd_done, s.v_bd_done, s.scored = sems("kq_done k_bd_done q_bd_done v_bd_done scored")
        s.scaled, s.max_done, s.shifted, s.exp_done, s.den_done = sems("scaled max_done shifted exp_done den_done")
        s.rden_done, s.p_turned, s.p_copied, s.weighed, s.attn_done = sems("rden_done p_turned p_copied weighed attn_done")
        s.attn_turned, s.attn_copied, s.attended, s.x2_done, s.xn2_turned = sems("attn_turned attn_copied attended x2_done xn2_turned")
        s.xn2_copied, s.routed, s.gated, s.best_done, s.place_done = sems("xn2_copied routed gated best_done place_done")
        s.placef_done, s.total_done, s.inverse_done, s.share_done, s.cw1_done = sems("placef_done total_done inverse_done share_done cw1_done")
        s.cw_done, s.hidden, s.relu_done, s.act_done, s.expert_done = sems("cw_done hidden relu_done act_done expert_done")
        s.weighted_done, s.mixed_done, s.x3_done, s.latw_done, s.lat_done = sems("weighted_done mixed_done x3_done latw_done lat_done")
        s.rows_copied, s.lat_turned, s.lat_copied, s.q_made, s.q_copied = sems("rows_copied lat_turned lat_copied q_made q_copied")
        s.stored = sem("stored")
        ln_a, ln_b, ln_c, ln_d = (Norm(nc, n, pair, sem, half, s.waits) for n in ("ln_a", "ln_b", "ln_c", "ln_d"))
        tiles = range(WIDTH)
        ctx.enter_context(nc.allow_non_contiguous_dma(reason="small vectors and permuted weights"))
        block = ctx.enter_context(nc.Block())

        @block.sync
        def _(sp):
            sp.sem_inc(s.stored, 16)
            with sp.Fori(0, ROUNDS) as k:
                for j in tiles:
                    sp.wait_ge(s.q_copied, WIDTH * (2 * k + 1) + j + 1)
                    for b in range(2):
                        sp.dma_start(dram.q1[bass.ds(2 * (WIDTH * k + j) + b, 1)].rearrange("o p n -> p (o n)"),
                                     q_out[j][:, b].rearrange("p h q -> p (h q)")).then_inc(s.stored, 16)
            sp.wait_ge(s.stored, 16 * (BATCH + 1))

        @block.tensor
        def _(pe):
            def turn(out, block):
                return nc.tensor.transpose(out, block, ident)

            for i in range(4):
                turn(ps_b[0][:, P * i:P * i + P], raw[:, i, :])
            nc.tensor.transpose(ps_a[0][:, 0:EXPERTS], router[:], g.consts[0:EXPERTS, C_IDENT:C_IDENT + EXPERTS]).then_inc(s.w_turned, 1)
            pe.wait_ge(s.w_swapped, 2)
            with pe.Fori(0, ROUNDS) as k:
                for j in tiles:
                    pe.wait_ge(s.staged, WIDTH * k + j + 1)
                    bank_is_read(pe, s.x1_part, None, k, j)
                    for u in range(QUADS):
                        mm = nc.tensor.matmul(ps_a[j % BANK_SETS][:, 0:D], heads_t[j][:, u], g.wo_rows[:, u], start=(u == 0), stop=(u == QUADS - 1))
                    mm.then_inc(s.projected, 1)
                for j in tiles:
                    pe.wait_ge(ln_a.done, WIDTH * k + j + 1)
                    bank_is_read(pe, s.xn_copied, s.x1_part, k, j)
                    turn(ps_a[j % BANK_SETS][:, 128:256], ln_a.out[j][:]).then_inc(s.xn_turned, 1)
                for j in tiles:
                    pe.wait_ge(s.xn_copied, WIDTH * k + j + 1)
                    bank_is_read(pe, s.v_bd_done, s.xn_copied, k, j)
                    bank_is_read(pe, s.rot2_done, None, k, j)
                    for i, w in enumerate((w_t[:, 0], w_t[:, 1], w_swap[:, 0], w_swap[:, 1])):
                        nc.tensor.matmul(ps_b[j % BANK_SETS][:, P * i:P * i + P], w, xn_t[j][:], start=True, stop=True)
                    for b in range(2):
                        for h in range(2):
                            mm = nc.tensor.matmul(ps_a[j % BANK_SETS][64 * h:64 * h + 64, 256 + P * b:256 + P * b + P],
                                                  xn_t[j][:, 64 * b:64 * b + 64], w_t[:, 2], start=True, stop=True)
                    mm.then_inc(s.qkv_done, 1)
                for j in tiles:
                    pe.wait_ge(s.k_bd_done, WIDTH * k + j + 1)
                    pe.wait_ge(s.q_bd_done, WIDTH * k + j + 1)
                    bank_is_read(pe, s.scaled, None, k, j)
                    for b in range(2):
                        for r in range(4):
                            mm = nc.tensor.matmul(ps_c[j % BANK_SETS][64 * b:64 * b + 64, 256 * r:256 * r + 256], q_bd[j][:, r, b, :],
                                                  k_bd[j][:, b].rearrange("p h k -> p (h k)"), start=True, stop=True)
                    mm.then_inc(s.scored, 1)
                for j in tiles:
                    pe.wait_ge(s.exp_done, WIDTH * k + j + 1)
                    bank_is_read(pe, s.p_copied, s.scaled, k, j)
                    for i in range(PAIRS):
                        mm = turn(ps_c[j % BANK_SETS][:, P * i:P * i + P], sc[j][:, 2 * i:2 * i + 2, :].rearrange("p h k -> p (h k)"))
                    mm.then_inc(s.p_turned, 1)
                for j in tiles:
                    pe.wait_ge(s.p_copied, WIDTH * k + j + 1)
                    pe.wait_ge(s.v_bd_done, WIDTH * k + j + 1)
                    bank_is_read(pe, s.attn_done, s.rot2_done, k, j)
                    for b in range(2):
                        for i in range(PAIRS):
                            mm = nc.tensor.matmul(ps_b[j % BANK_SETS][64 * b:64 * b + 64, 16 * i:16 * i + 16], prob_t[j][:, i, 64 * b:64 * b + 64],
                                                  v_bd[j][:, PAIRS * b + i, :], start=True, stop=True)
                    mm.then_inc(s.weighed, 1)
                for j in tiles:
                    pe.wait_ge(s.attn_done, WIDTH * k + j + 1)
                    bank_is_read(pe, s.attn_copied, s.attn_done, k, j)
                    turn(ps_b[j % BANK_SETS][:, 128:256], attn[j][:]).then_inc(s.attn_turned, 1)
                for j in tiles:
                    pe.wait_ge(s.attn_copied, WIDTH * k + j + 1)
                    bank_is_read(pe, s.x2_done, s.attn_copied, k, j)
                    nc.tensor.matmul(ps_b[j % BANK_SETS][:, 256:384], attn_t[j][:], w_t[:, 3], start=True, stop=True).then_inc(s.attended, 1)
                for j in tiles:
                    pe.wait_ge(ln_b.done, WIDTH * k + j + 1)
                    bank_is_read(pe, s.xn2_copied, s.x2_done, k, j)
                    turn(ps_b[j % BANK_SETS][:, 384:512], ln_b.out[j][:]).then_inc(s.xn2_turned, 1)
                for j in tiles:
                    pe.wait_ge(s.xn2_copied, WIDTH * k + j + 1)
                    bank_is_read(pe, s.gated, s.v_bd_done, k, j)
                    nc.tensor.matmul(ps_a[j % BANK_SETS][:, 0:EXPERTS], xn2_t[j][:], router_t[:], start=True, stop=True).then_inc(s.routed, 1)
                for j in tiles:
                    bank_is_read(pe, s.relu_done, s.p_copied, k, j)
                    for e in range(EXPERTS):
                        mm = nc.tensor.matmul(ps_c[j % BANK_SETS][:, P * e:P * e + P], w1[:, e, :], xn2_t[j][:], start=True, stop=True)
                    mm.then_inc(s.hidden, 1)
                for j in tiles:
                    pe.wait_ge(s.act_done, WIDTH * k + j + 1)
                    bank_is_read(pe, s.weighted_done, s.relu_done, k, j)
                    for e in range(EXPERTS):
                        mm = nc.tensor.matmul(ps_c[j % BANK_SETS][:, P * e:P * e + P], act[j][:, e, :], w2[:, e, :], start=True, stop=True)
                    mm.then_inc(s.expert_done, 1)
                for j in tiles:
                    pe.wait_ge(s.lat_done, WIDTH * k + j + 1)
                    bank_is_read(pe, s.lat_copied, s.gated, k, j)
                    turn(ps_a[j % BANK_SETS][:, 128:256], lat[j][:]).then_inc(s.lat_turned, 1)
                for part in range(2):
                    for j in tiles:
                        pe.wait_ge(s.lat_copied, WIDTH * k + j + 1)
                        if part or j >= BANK_SETS:
                            pe.wait_ge(s.q_copied, WIDTH * (2 * k + part) + j - BANK_SETS + 1)
                        else:
                            pe.wait_ge(s.weighted_done, WIDTH * (k + 1) + j - BANK_SETS + 1)
                        for h in range(8):
                            mm = nc.tensor.matmul(ps_c[j % BANK_SETS][:, P * h:P * h + P], g.qk[:, 8 * part + h, :], lat_t[j][:], start=True, stop=True)
                        mm.then_inc(s.q_made, 1)

        @block.scalar
        def _(sc_e):
            def copy(out, in_, done, **kw):
                nc.scalar.activation(out, in_, ACT.Copy, **kw).then_inc(done, 1)

            sc_e.wait_ge(s.w_turned, 1)
            copy(w_t[:].rearrange("p m k -> p (m k)"), ps_b[0][:], s.w_copied)
            copy(router_t[:], ps_a[0][:, 0:EXPERTS], s.w_copied)
            with sc_e.Fori(0, ROUNDS) as k:
                sc_e.wait_ge(s.rows_copied, WIDTH * k + 1)
                for j in tiles:
                    copy(heads_t[j][:], g.act_t[:, :, bass.ds(P * (WIDTH * k + j), P)], s.staged)
                for j in tiles:
                    sc_e.wait_ge(s.xn_turned, WIDTH * k + j + 1)
                    copy(xn_t[j][:], ps_a[j % BANK_SETS][:, 128:256], s.xn_copied)
                for j in tiles:
                    sc_e.wait_ge(s.shifted, WIDTH * k + j + 1)
                    nc.scalar.activation(sc[j][:], sc[j][:], ACT.Exp).then_inc(s.exp_done, 1)
                for j in tiles:
                    sc_e.wait_ge(s.p_turned, WIDTH * k + j + 1)
                    copy(prob_t[j][:].rearrange("p i q -> p (i q)"), ps_c[j % BANK_SETS][:], s.p_copied)
                for j in tiles:
                    sc_e.wait_ge(s.attn_turned, WIDTH * k + j + 1)
                    copy(attn_t[j][:], ps_b[j % BANK_SETS][:, 128:256], s.attn_copied)
                for j in tiles:
                    sc_e.wait_ge(s.xn2_turned, WIDTH * k + j + 1)
                    copy(xn2_t[j][:], ps_b[j % BANK_SETS][:, 384:512], s.xn2_copied)
                for j in tiles:
                    sc_e.wait_ge(s.routed, WIDTH * k + j + 1)
                    nc.scalar.activation(gate[j][:], ps_a[j % BANK_SETS][:, 0:EXPERTS], ACT.Sigmoid).then_inc(s.gated, 1)
                for j in tiles:
                    sc_e.wait_ge(s.hidden, WIDTH * k + j + 1)
                    nc.scalar.activation(relu[j].rearrange("p e w -> p (e w)"), ps_c[j % BANK_SETS][:], ACT.Relu).then_inc(s.relu_done, 1)
                for j in tiles:
                    sc_e.wait_ge(s.lat_turned, WIDTH * k + j + 1)
                    copy(lat_t[j][:], ps_a[j % BANK_SETS][:, 128:256], s.lat_copied)
                sc_e.wait_ge(s.stored, 16 * (2 * WIDTH * k + 1))
                for part in range(2):
                    for j in tiles:
                        sc_e.wait_ge(s.q_made, WIDTH * (2 * k + part) + j + 1)
                        copy(q_out[j][:, :, 8 * part:8 * part + 8, :], ps_c[j % BANK_SETS][:].rearrange("p (h b q) -> p b h q", h=8, b=2),
                             s.q_copied, scale=SEQ ** -0.5)

        @block.gpsimd
        def _(pool):
            nc.gpsimd.memset(half[:], -0.5).then_inc(s.half_set, 1)
            pool.wait_ge(s.half_set, 1)
            with pool.Fori(0, ROUNDS) as k:
                pool.wait_ge(s.rows_copied, WIDTH * k + 1)
                for j in tiles:
                    ln_a.root(pool, j, WIDTH * k + j + 1)
                for j in tiles:
                    pool.wait_ge(s.rot1_done, WIDTH * k + j + 1)
                    pool.wait_ge(s.rot2_done, WIDTH * k + j + 1)
                    nc.gpsimd.tensor_tensor(kq[j][:], rot1[j][:], rot2[j][:], ALU.add).then_inc(s.kq_done, 1)
                for ln in (ln_b, ln_c, ln_d):
                    for j in tiles:
                        ln.root(pool, j, WIDTH * k + j + 1)

        @block.vector
        def _(dve):
            tt, ts, stt, reduce = nc.vector.tensor_tensor, nc.vector.tensor_scalar, nc.vector.scalar_tensor_tensor, nc.vector.tensor_reduce
            dve.wait_ge(s.w_copied, 2)
            for odd in range(2):
                nc.vector.tensor_copy(w_swap[:].rearrange("p m (r o) -> p m r o", o=2)[:, :, :, odd],
                                      w_t[:, 0:2].rearrange("p m (r o) -> p m r o", o=2)[:, :, :, 1 - odd]).then_inc(s.w_swapped, 1)
            cos, sin = (g.consts[:, c:c + SEQ].unsqueeze(1).broadcast_to([P, 4, SEQ]) for c in (C_COS, C_SIN))
            causal = g.consts[:, C_CAUSAL:C_CAUSAL + SEQ].unsqueeze(1).broadcast_to([P, HEADS, SEQ])
            iota = g.consts[:, C_IOTA:C_IOTA + EXPERTS]
            dve.sem_inc(s.rows_copied, 1)
            with dve.Fori(0, ROUNDS) as k:
                dve.wait_ge(s.rows_copied, WIDTH * k + 1)
                for j in tiles:
                    n = WIDTH * k + j + 1
                    dve.wait_ge(s.projected, n)
                    tt(x1[j][:], ps_a[j % BANK_SETS][:, 0:D], tile_of(g.x_tok, WIDTH * k + j), ALU.add).then_inc(s.x1_part, 1)
                    dve.wait_ge(s.x1_part, n)
                    tt(x1[j][:], x1[j][:], bo[:], ALU.add).then_inc(s.x1_done, 1)
                for j in tiles:
                    dve.wait_ge(s.x1_done, WIDTH * k + j + 1)
                    ln_a.statistics(dve, j, WIDTH * k + j + 1, x1[j][:])
                for j in tiles:
                    ln_a.normalise(dve, j, WIDTH * k + j + 1, x1[j][:])
                for j in tiles:
                    dve.wait_ge(s.qkv_done, WIDTH * k + j + 1)
                    tt(rot1[j][:], ps_b[j % BANK_SETS][:, 0:256].rearrange("p (m q) -> p m q", q=SEQ), cos, ALU.mult).then_inc(s.rot1_done, 1)
                    tt(rot2[j][:], ps_b[j % BANK_SETS][:, 256:512].rearrange("p (m q) -> p m q", q=SEQ), sin, ALU.mult).then_inc(s.rot2_done, 1)
                    tt(v_bd[j][:], ps_a[j % BANK_SETS][:, 256:512].rearrange("p (m r) -> p m r", r=16),
                       g.consts[:, C_PAIRROWS:C_PAIRROWS + 16].unsqueeze(1).broadcast_to([P, 2 * PAIRS, 16]), ALU.mult).then_inc(s.v_bd_done, 1)
                for j in tiles:
                    dve.wait_ge(s.kq_done, WIDTH * k + j + 1)
                    tt(k_bd[j][:], kq[j][:, 0:2, :].unsqueeze(2).broadcast_to([P, 2, 4, SEQ]),
                       g.consts[:, C_QUADROWS:C_QUADROWS + 4].unsqueeze(1).unsqueeze(3).broadcast_to([P, 2, 4, SEQ]),
                       ALU.mult).then_inc(s.k_bd_done, 1)
                    tt(q_bd[j][:], kq[j][:, 2:4, :].unsqueeze(1).broadcast_to([P, 4, 2, SEQ]),
                       g.consts[:, C_GROUPROWS:C_GROUPROWS + 4].unsqueeze(2).unsqueeze(3).broadcast_to([P, 4, 2, SEQ]),
                       ALU.mult).then_inc(s.q_bd_done, 1)
                for j in tiles:
                    dve.wait_ge(s.scored, WIDTH * k + j + 1)
                    stt(sc[j][:], ps_c[j % BANK_SETS][:].rearrange("p (h q) -> p h q", q=SEQ), SCALE, causal, ALU.mult, ALU.add).then_inc(s.scaled, 1)
                for j in tiles:
                    dve.wait_ge(s.scaled, WIDTH * k + j + 1)
                    reduce(top[j][:], sc[j][:], AX_X, ALU.max).then_inc(s.max_done, 1)
                for j in tiles:
                    dve.wait_ge(s.max_done, WIDTH * k + j + 1)
                    tt(sc[j][:], sc[j][:], top[j][:].unsqueeze(2).broadcast_to([P, HEADS, SEQ]), ALU.subtract).then_inc(s.shifted, 1)
                for j in tiles:
                    dve.wait_ge(s.exp_done, WIDTH * k + j + 1)
                    reduce(den[j][:], sc[j][:], AX_X, ALU.add).then_inc(s.den_done, 1)
                for j in tiles:
                    dve.wait_ge(s.den_done, WIDTH * k + j + 1)
                    nc.vector.reciprocal(rden[j][:], den[j][:]).then_inc(s.rden_done, 1)
                for j in tiles:
                    dve.wait_ge(s.weighed, WIDTH * k + j + 1)
                    dve.wait_ge(s.rden_done, WIDTH * k + j + 1)
                    tt(attn[j][:].rearrange("p (h e) -> p h e", e=E0), ps_b[j % BANK_SETS][:, 0:D].rearrange("p (h e) -> p h e", e=E0),
                       rden[j][:].unsqueeze(2).broadcast_to([P, HEADS, E0]), ALU.mult).then_inc(s.attn_done, 1)
                for j in tiles:
                    dve.wait_ge(s.attended, WIDTH * k + j + 1)
                    tt(x2[j][:], ps_b[j % BANK_SETS][:, 256:384], x1[j][:], ALU.add).then_inc(s.x2_done, 1)
                for j in tiles:
                    dve.wait_ge(s.x2_done, WIDTH * k + j + 1)
                    ln_b.statistics(dve, j, WIDTH * k + j + 1, x2[j][:])
                for j in tiles:
                    ln_b.normalise(dve, j, WIDTH * k + j + 1, x2[j][:])
                for j in tiles:
                    dve.wait_ge(s.relu_done, WIDTH * k + j + 1)
                    tt(act[j][:], relu[j], relu[j], ALU.mult).then_inc(s.act_done, 1)
                for j in tiles:
                    n = WIDTH * k + j + 1
                    wait_apart(dve, s.gated, n, s.waits)
                    nc.vector.max(best[j][:], gate[j][:]).then_inc(s.best_done, 1)
                    wait_apart(dve, s.best_done, n, s.waits)
                    nc.vector.max_index(place[j][:], best[j][:], gate[j][:]).then_inc(s.place_done, 1)
                    ts(total[j][:], best[j][:, 0:1], best[j][:, 1:2], 1e-20, ALU.add, ALU.add).then_inc(s.total_done, 1)
                    dve.wait_ge(s.place_done, n)
                    nc.vector.tensor_copy(place_f[j][:], place[j][:, 0:2]).then_inc(s.placef_done, 1)
                    dve.wait_ge(s.total_done, n)
                    nc.vector.reciprocal(total[j][:], total[j][:]).then_inc(s.inverse_done, 1)
                    dve.wait_ge(s.inverse_done, n)
                    ts(share[j][:], best[j][:, 0:2], total[j][:], None, ALU.mult).then_inc(s.share_done, 1)
                    dve.wait_ge(s.share_done, n)
                    dve.wait_ge(s.placef_done, n)
                    ts(cw1[j][:], iota, place_f[j][:, 0:1], share[j][:, 0:1], ALU.is_equal, ALU.mult).then_inc(s.cw1_done, 1)
                    ts(cw[j][:], iota, place_f[j][:, 1:2], share[j][:, 1:2], ALU.is_equal, ALU.mult).then_inc(s.cw1_done, 1)
                    dve.wait_ge(s.cw1_done, 2 * n)
                    tt(cw[j][:], cw[j][:], cw1[j][:], ALU.add).then_inc(s.cw_done, 1)
                for j in tiles:
                    dve.wait_ge(s.expert_done, WIDTH * k + j + 1)
                    dve.wait_ge(s.cw_done, WIDTH * k + j + 1)
                    tt(weighted[j], ps_c[j % BANK_SETS][:].rearrange("p (e d) -> p e d", d=D), cw[j][:].unsqueeze(2).broadcast_to([P, EXPERTS, D]),
                       ALU.mult).then_inc(s.weighted_done, 1)
                for j in tiles:
                    dve.wait_ge(s.weighted_done, WIDTH * k + j + 1)
                    reduce(mixed[j][:], weighted[j].rearrange("p e d -> p d e"), AX_X, ALU.add).then_inc(s.mixed_done, 1)
                for j in tiles:
                    dve.wait_ge(s.mixed_done, WIDTH * k + j + 1)
                    tt(x3[j][:], mixed[j][:], x2[j][:], ALU.add).then_inc(s.x3_done, 1)
                for j in tiles:
                    dve.wait_ge(s.x3_done, WIDTH * k + j + 1)
                    ln_c.statistics(dve, j, WIDTH * k + j + 1, x3[j][:])
                for j in tiles:
                    ln_c.normalise(dve, j, WIDTH * k + j + 1, x3[j][:])
                    nc.vector.tensor_copy(tile_of(g.x_tok, WIDTH * k + j), x3[j][:])
                for j in tiles:
                    dve.wait_ge(ln_c.done, WIDTH * k + j + 1)
                    ln_d.statistics(dve, j, WIDTH * k + j + 1, ln_c.out[j][:])
                for j in tiles:
                    ln_d.normalise(dve, j, WIDTH * k + j + 1, ln_c.out[j][:])
                for j in tiles:
                    dve.wait_ge(ln_d.done, WIDTH * k + j + 1)
                    tt(lat_w[j][:], ln_d.out[j][:], ln2_w[:], ALU.mult).then_inc(s.latw_done, 1)
                for j in tiles:
                    dve.wait_ge(s.latw_done, WIDTH * k + j + 1)
                    tt(lat[j][:], lat_w[j][:], ln2_b[:], ALU.add).then_inc(s.lat_done, 1)
                for j in tiles:
                    dve.wait_ge(s.lat_done, WIDTH * k + j + 1)
                    row = 2 * (WIDTH * k + j)
                    for b in range(2):
                        cp = nc.vector.tensor_copy(g.lat_rows[:, bass.ds(row + b, 1), :].rearrange("p o d -> p (o d)"),
                                                   lat[j][64 * b:64 * b + 64, :])
                    cp.then_inc(s.rows_copied, 1)


def rest_of_layer_1(nc, g, dram, out):
    K_CLAMP, K_EPS = 60.0, 1e-16
    TO_256TH, TO_QUARTER = 1.5 * 2.0 ** 15, 1.5 * 2.0 ** 21
    with ExitStack() as ctx:
        sb, pair, bank, sem, sems = scope(nc, ctx, "d_")
        ident = g.consts[:, C_IDENT:C_IDENT + P]
        raw, mix, decay_in, first_in, w1, b1, w2, b2 = g.rest_1
        w_t = sb("w_t", [P, 4, D])
        unmix, decay, first = sb("unmix", [P, 1]), sb("decay", [P, 1]), sb("first", [P, 1])
        decay_rows = sb("decay_rows", [P, 4, SEQ + 1])
        half, quarter = sb("half", [P, 1]), sb("quarter", [P, 1])
        x = pair("x", [P, D])
        xp = pair("xp", [P, 2, SEQ + 1])
        xm1, xm = pair("xm1", [P, 2, SEQ]), pair("xm", [P, 2, SEQ])
        kc = pair("kc", [P, 2, SEQ])
        kv = pair("kv", [P, 4, SEQ + 1])
        gate = pair("gate", [P, 2, SEQ])
        past, sums = pair("past", [P, 4, SEQ + 1]), pair("sums", [P, 4, SEQ])
        ratio, rwkv = pair("ratio", [P, 2, SEQ]), pair("rwkv", [P, 2, SEQ])
        x5, xn_t = pair("x5", [P, D]), pair("xn_t", [P, P])
        h, hq, over, low, left, rest, g_left, g_right, val = (pair(n, [P, BANK]) for n in (
            "h", "hq", "over", "low", "left", "rest", "g_left", "g_right", "val"))
        o, oq = pair("o", [P, D]), pair("oq", [P, D])
        ps_a, ps_b, ps_c = bank("ps_a", [P, BANK]), bank("ps_b", [P, BANK], WIDTH), bank("ps_c", [P, BANK])
        s = Named()
        s.waits, s.pool_waits, s.set_up, s.w_turned = sems("waits pool_waits set_up w_turned")
        s.w_copied, s.w_exp, s.w_scaled, s.copied, s.xn_turned = sems("w_copied w_exp w_scaled copied xn_turned")
        s.xp_done, s.xm1_done, s.xm_done, s.kvr_done, s.clamped = sems("xp_done xm1_done xm_done kvr_done clamped")
        s.k_done, s.r_done, s.kv_done, s.past_done, s.sums_done = sems("k_done r_done kv_done past_done sums_done")
        s.eps_done, s.inverse_done, s.ratio_done, s.rwkv_done, s.projected = sems("eps_done inverse_done ratio_done rwkv_done projected")
        s.x5_done, s.xn2_turned, s.xn2_copied, s.hidden, s.h_done = sems("x5_done xn2_turned xn2_copied hidden h_done")
        s.hq_done, s.over_done, s.low_done, s.left_done = sems("hq_done over_done low_done left_done")
        s.left2_done, s.rest_done, s.gl_done, s.gr_done = sems("left2_done rest_done gl_done gr_done")
        s.slope_done, s.rise_done, s.val_done, s.rounded = sems("slope_done rise_done val_done rounded")
        s.act_done, s.final, s.o_done, s.oq_done, s.out_done = sems("act_done final o_done oq_done out_done")
        s.stored = sem("stored")
        ln_a, ln_b = (Norm(nc, n, pair, sem, half, s.waits) for n in ("ln_a", "ln_b"))
        tiles = range(WIDTH)
        ctx.enter_context(nc.allow_non_contiguous_dma(reason="small vectors and permuted weights"))
        block = ctx.enter_context(nc.Block())

        @block.sync
        def _(sp):
            sp.sem_inc(s.stored, 16)
            with sp.Fori(0, ROUNDS) as k:
                for j in tiles:
                    sp.wait_ge(s.out_done, WIDTH * k + j + 2)
                    sp.dma_start(out[bass.ds(2 * (WIDTH * k + j), 2)].rearrange("b s d -> (b s) d"), x[j][:]).then_inc(s.stored, 16)
            sp.wait_ge(s.stored, 16 * (TOK_TILES + 1))

        @block.tensor
        def _(pe):
            for i in range(4):
                tr = nc.tensor.transpose(ps_b[0][:, P * i:P * i + P], raw[:, i, :], ident)
            tr.then_inc(s.w_turned, 1)
            pe.wait_ge(s.w_copied, 1)
            with pe.Fori(0, ROUNDS) as k:
                for j in tiles:
                    pe.wait_ge(ln_a.done, WIDTH * k + j + 1)
                    bank_is_read(pe, s.xp_done, None, k, j)
                    nc.tensor.transpose(ps_a[j % BANK_SETS][:, 0:P], ln_a.out[j][:], ident).then_inc(s.xn_turned, 1)
                for j in tiles:
                    pe.wait_ge(s.xm_done, WIDTH * k + j + 1)
                    for i in range(3):
                        mm = nc.tensor.matmul(ps_b[j][:, P * i:P * i + P], w_t[:, i], xm[j][:].rearrange("p b q -> p (b q)"),
                                              start=True, stop=True)
                    mm.then_inc(s.kvr_done, 1)
                for j in tiles:
                    pe.wait_ge(s.rwkv_done, WIDTH * k + j + 1)
                    nc.tensor.matmul(ps_b[j][:, 384:512], rwkv[j][:].rearrange("p b q -> p (b q)"), w_t[:, 3], start=True,
                                     stop=True).then_inc(s.projected, 1)
                for j in tiles:
                    pe.wait_ge(ln_b.done, WIDTH * k + j + 1)
                    bank_is_read(pe, s.xn2_copied, s.xp_done, k, j)
                    nc.tensor.transpose(ps_a[j % BANK_SETS][:, 128:256], ln_b.out[j][:], ident).then_inc(s.xn2_turned, 1)
                for j in tiles:
                    pe.wait_ge(s.xn2_copied, WIDTH * k + j + 1)
                    bank_is_read(pe, s.h_done, None, k, j)
                    for m in range(FF_BLOCKS):
                        mm = nc.tensor.matmul(ps_c[j % BANK_SETS][:, P * m:P * m + P], w1[:, P * m:P * m + P], xn_t[j][:], start=True, stop=True)
                    mm.then_inc(s.hidden, 1)
                for j in tiles:
                    pe.wait_ge(s.act_done, WIDTH * k + j + 1)
                    bank_is_read(pe, s.o_done, s.xn2_copied, k, j)
                    for m in range(FF_BLOCKS):
                        mm = nc.tensor.matmul(ps_a[j % BANK_SETS][:, 256:384], val[j][:, P * m:P * m + P], w2[:, m], start=(m == 0),
                                              stop=(m == FF_BLOCKS - 1))
                    mm.then_inc(s.final, 1)

        @block.scalar
        def _(act):
            act.wait_ge(s.w_turned, 1)
            nc.scalar.activation(w_t[:].rearrange("p m k -> p (m k)"), ps_b[0][:], ACT.Copy).then_inc(s.w_copied, 1)
            act.wait_ge(s.set_up, 2 + 2 * WIDTH)
            nc.scalar.activation(decay[:], decay_in[:], ACT.Exp).then_inc(s.w_exp, 1)
            nc.scalar.activation(first[:], first_in[:], ACT.Exp).then_inc(s.w_exp, 1)
            act.wait_ge(s.w_exp, 2)
            nc.scalar.activation(decay[:], decay[:], ACT.Exp, scale=-1.0).then_inc(s.w_exp, 1)
            with act.Fori(0, ROUNDS) as k:
                act.wait_ge(s.out_done, WIDTH * k + 1)
                for j in tiles:
                    act.wait_ge(s.xn_turned, WIDTH * k + j + 1)
                    nc.scalar.activation(xp[j][:, :, 1:SEQ + 1], ps_a[j % BANK_SETS][:, 0:P].rearrange("p (b q) -> p b q", b=2),
                                         ACT.Copy).then_inc(s.xp_done, 1)
                for j in tiles:
                    act.wait_ge(s.kvr_done, WIDTH * k + j + 1)
                    nc.scalar.activation(gate[j][:], ps_b[j][:, 256:384].rearrange("p (b q) -> p b q", b=2), ACT.Sigmoid).then_inc(s.r_done, 1)
                for j in tiles:
                    act.wait_ge(s.clamped, WIDTH * k + j + 1)
                    nc.scalar.activation(kv[j][:, 2:4, 1:SEQ + 1], kc[j][:], ACT.Exp).then_inc(s.k_done, 1)
                for j in tiles:
                    act.wait_ge(s.xn2_turned, WIDTH * k + j + 1)
                    nc.scalar.activation(xn_t[j][:], ps_a[j % BANK_SETS][:, 128:256], ACT.Copy).then_inc(s.xn2_copied, 1)
                for j in tiles:
                    act.wait_ge(s.hidden, WIDTH * k + j + 1)
                    for m in range(FF_BLOCKS):
                        cols = slice(P * m, P * m + P)
                        op = nc.scalar.activation(h[j][:, cols], ps_c[j % BANK_SETS][:, cols], ACT.Identity, bias=b1[:, m:m + 1])
                    op.then_inc(s.h_done, 1)
                for j in tiles:
                    act.wait_ge(s.left2_done, WIDTH * k + j + 1)
                    nc.scalar.activation(g_left[j][:], left[j][:], ACT.Gelu).then_inc(s.gl_done, 1)
                    nc.scalar.activation(g_right[j][:], left[j][:], ACT.Gelu, bias=quarter[:]).then_inc(s.gr_done, 1)

        @block.gpsimd
        def _(pool):
            nc.gpsimd.memset(half[:], -0.5).then_inc(s.set_up, 1)
            nc.gpsimd.memset(quarter[:], 0.25).then_inc(s.set_up, 1)
            for j in tiles:
                nc.gpsimd.memset(xp[j][:], 0.0).then_inc(s.set_up, 1)
                nc.gpsimd.memset(kv[j][:], 0.0).then_inc(s.set_up, 1)
            pool.wait_ge(s.set_up, 2 + 2 * WIDTH)
            nc.gpsimd.tensor_scalar(unmix[:], mix[:], -1.0, 1.0, ALU.mult, ALU.add).then_inc(s.set_up, 1)
            pool.wait_ge(s.w_exp, 3)
            nc.gpsimd.tensor_scalar(decay_rows[:], g.consts[:, C_SEQSTART:C_SEQSTART + SEQ + 1].unsqueeze(1).broadcast_to([P, 4, SEQ + 1]),
                                    decay[:], None, ALU.mult).then_inc(s.set_up, 1)
            with pool.Fori(0, ROUNDS) as k:
                pool.wait_ge(s.out_done, WIDTH * k + 1)
                for j in tiles:
                    ln_a.root(pool, j, WIDTH * k + j + 1)
                for j in tiles:
                    ln_b.root(pool, j, WIDTH * k + j + 1)
                for j in tiles:
                    wait_apart(pool, s.hq_done, WIDTH * k + j + 1, s.pool_waits)
                    nc.gpsimd.tensor_scalar(over[j][:], hq[j][:], TO_256TH + 4.0, 0.0, ALU.subtract, ALU.max).then_inc(s.over_done, 1)
                for j in tiles:
                    pool.wait_ge(s.left2_done, WIDTH * k + j + 1)
                    nc.gpsimd.tensor_tensor(rest[j][:], low[j][:], left[j][:], ALU.subtract).then_inc(s.rest_done, 1)

        @block.vector
        def _(dve):
            tt, ts, stt = nc.vector.tensor_tensor, nc.vector.tensor_scalar, nc.vector.scalar_tensor_tensor
            HALF_STEP = 2.0 ** -9

            def flat(rows):
                return rows[:].rearrange("p m q -> p (m q)")

            dve.wait_ge(s.set_up, 4 + 2 * WIDTH)
            dve.sem_inc(s.out_done, 1)
            with dve.Fori(0, ROUNDS) as k:
                dve.wait_ge(s.stored, 16 * (WIDTH * k + 1))
                for j in tiles:
                    nc.vector.tensor_copy(x[j][:], tile_of(g.x_tok, WIDTH * k + j)).then_inc(s.copied, 1)
                for j in tiles:
                    dve.wait_ge(s.copied, WIDTH * k + j + 1)
                    ln_a.statistics(dve, j, WIDTH * k + j + 1, x[j][:])
                for j in tiles:
                    ln_a.normalise(dve, j, WIDTH * k + j + 1, x[j][:])
                for j in tiles:
                    dve.wait_ge(s.xp_done, WIDTH * k + j + 1)
                    ts(xm1[j][:], xp[j][:, :, 0:SEQ], unmix[:], None, ALU.mult).then_inc(s.xm1_done, 1)
                for j in tiles:
                    dve.wait_ge(s.xm1_done, WIDTH * k + j + 1)
                    stt(xm[j][:], xp[j][:, :, 1:SEQ + 1], mix[:], xm1[j][:], ALU.mult, ALU.add).then_inc(s.xm_done, 1)
                for j in tiles:
                    dve.wait_ge(s.r_done, WIDTH * k + j + 1)
                    ts(kc[j][:], ps_b[j][:, 0:P].rearrange("p (b q) -> p b q", b=2), K_CLAMP, None, ALU.min).then_inc(s.clamped, 1)
                for j in tiles:
                    dve.wait_ge(s.k_done, WIDTH * k + j + 1)
                    tt(kv[j][:, 0:2, 1:SEQ + 1], kv[j][:, 2:4, 1:SEQ + 1], ps_b[j][:, 128:256].rearrange("p (b q) -> p b q", b=2),
                       ALU.mult).then_inc(s.kv_done, 1)
                for j in tiles:
                    dve.wait_ge(s.kv_done, WIDTH * k + j + 1)
                    nc.vector.tensor_tensor_scan(flat(past[j]), flat(decay_rows), flat(kv[j]), 0.0, ALU.mult, ALU.add).then_inc(s.past_done, 1)
                for j in tiles:
                    dve.wait_ge(s.past_done, WIDTH * k + j + 1)
                    stt(sums[j][:], kv[j][:, :, 1:SEQ + 1], first[:], past[j][:, :, 0:SEQ], ALU.mult, ALU.add).then_inc(s.sums_done, 1)
                for j in tiles:
                    dve.wait_ge(s.sums_done, WIDTH * k + j + 1)
                    ts(sums[j][:, 2:4, :], sums[j][:, 2:4, :], K_EPS, None, ALU.add).then_inc(s.eps_done, 1)
                    tt(ratio[j][:], gate[j][:], sums[j][:, 0:2, :], ALU.mult).then_inc(s.ratio_done, 1)
                for j in tiles:
                    dve.wait_ge(s.eps_done, WIDTH * k + j + 1)
                    nc.vector.reciprocal(sums[j][:, 2:4, :], sums[j][:, 2:4, :]).then_inc(s.inverse_done, 1)
                for j in tiles:
                    dve.wait_ge(s.inverse_done, WIDTH * k + j + 1)
                    dve.wait_ge(s.ratio_done, WIDTH * k + j + 1)
                    tt(rwkv[j][:], ratio[j][:], sums[j][:, 2:4, :], ALU.mult).then_inc(s.rwkv_done, 1)
                for j in tiles:
                    dve.wait_ge(s.projected, WIDTH * k + j + 1)
                    tt(x5[j][:], ps_b[j][:, 384:512], x[j][:], ALU.add).then_inc(s.x5_done, 1)
                for j in tiles:
                    dve.wait_ge(s.x5_done, WIDTH * k + j + 1)
                    ln_b.statistics(dve, j, WIDTH * k + j + 1, x5[j][:])
                for j in tiles:
                    ln_b.normalise(dve, j, WIDTH * k + j + 1, x5[j][:])
                for j in tiles:
                    dve.wait_ge(s.h_done, WIDTH * k + j + 1)
                    ts(hq[j][:], h[j][:], TO_256TH, TO_256TH - 4.0, ALU.add, ALU.max).then_inc(s.hq_done, 1)
                for j in tiles:
                    dve.wait_ge(s.hq_done, WIDTH * k + j + 1)
                    ts(low[j][:], hq[j][:], TO_256TH + 4.0, TO_256TH, ALU.min, ALU.subtract).then_inc(s.low_done, 1)
                for j in tiles:
                    dve.wait_ge(s.low_done, WIDTH * k + j + 1)
                    ts(left[j][:], low[j][:], 0.125 - HALF_STEP, TO_QUARTER, ALU.subtract, ALU.add).then_inc(s.left_done, 1)
                for j in tiles:
                    dve.wait_ge(s.left_done, WIDTH * k + j + 1)
                    ts(left[j][:], left[j][:], TO_QUARTER, None, ALU.subtract).then_inc(s.left2_done, 1)
                for j in tiles:
                    dve.wait_ge(s.gl_done, WIDTH * k + j + 1)
                    dve.wait_ge(s.gr_done, WIDTH * k + j + 1)
                    tt(g_right[j][:], g_right[j][:], g_left[j][:], ALU.subtract).then_inc(s.slope_done, 1)
                for j in tiles:
                    dve.wait_ge(s.slope_done, WIDTH * k + j + 1)
                    dve.wait_ge(s.rest_done, WIDTH * k + j + 1)
                    stt(val[j][:], rest[j][:], 4.0, g_right[j][:], ALU.mult, ALU.mult).then_inc(s.rise_done, 1)
                for j in tiles:
                    dve.wait_ge(s.rise_done, WIDTH * k + j + 1)
                    tt(val[j][:], val[j][:], g_left[j][:], ALU.add).then_inc(s.val_done, 1)
                for j in tiles:
                    dve.wait_ge(s.val_done, WIDTH * k + j + 1)
                    dve.wait_ge(s.over_done, WIDTH * k + j + 1)
                    stt(val[j][:], val[j][:], TO_256TH, over[j][:], ALU.add, ALU.add).then_inc(s.rounded, 1)
                for j in tiles:
                    dve.wait_ge(s.rounded, WIDTH * k + j + 1)
                    ts(val[j][:], val[j][:], TO_256TH, None, ALU.subtract).then_inc(s.act_done, 1)
                for j in tiles:
                    n = WIDTH * k + j + 1
                    dve.wait_ge(s.final, n)
                    tt(o[j][:], ps_a[j % BANK_SETS][:, 256:384], b2[:], ALU.add).then_inc(s.o_done, 1)
                    dve.wait_ge(s.o_done, n)
                    ts(oq[j][:], o[j][:], TO_256TH, None, ALU.add).then_inc(s.oq_done, 1)
                    dve.wait_ge(s.oq_done, n)
                    stt(x[j][:], oq[j][:], TO_256TH, x5[j][:], ALU.subtract, ALU.add).then_inc(s.out_done, 1)


def cross_attention_1(nc, g, dram):
    LAT = FULL + 1
    KEYS = CTX + SEQ
    lay = Named()
    lay.tag, lay.keys, lay.norm_cols, lay.last_output = "c_", KEYS, BANK, True
    lay.tiles = [(P if t < FULL else TAIL, P * t) for t in range(FULL + 1)] + [(SEQ, CTX)]
    xt = [("x_t", c) for c in range(CHUNKS)]
    half = [None] * 7 + [("norm",), None, xt[0], xt[1], None, xt[2], None, xt[3], ("norm",)]
    lay.jobs = [half[:11] + [("out",)] + half[12:], half]

    with ExitStack() as ctx:
        t = Named()

        def allocate(own):
            sb, sem = own.sb, own.sem
            lay.own = own
            t.ctx = sb("ctx", [P, FULL + 1, D])
            t.stats = sb("stats", [P, FULL + 1, 6])
            t.mean_var = sb("mean_var", [P, FULL + 1, 2])
            t.rstd, t.shift, t.half = (sb(n, [P, FULL + 1]) for n in ("rstd", "shift", "half"))
            t.weight, t.bias = sb("ln_w", [P, D]), sb("ln_b", [P, D])
            t.xn = [sb(f"xn{m}", [P, LAT + 1, D]) for m in range(2)]
            t.x_hi = [sb(f"x_hi{m}", [P, KEYS + 1], F32R) for m in range(2)]
            t.x_lo = [sb(f"x_lo{m}", [P, KEYS + 1], F32R) for m in range(2)]
            t.q_raw = sb("q_raw", [P, HEADS * SEQ])
            t.q_hi = [sb(f"q_hi{m}", [P, HEADS * SEQ], F32R) for m in range(2)]
            t.q_lo = [sb(f"q_lo{m}", [P, HEADS * SEQ], F32R) for m in range(2)]
            t.u_t = sb("u_t", [P, HEADS, 2, SEQ])
            t.ones, t.ones_r = sb("ones", [P, P]), sb("ones_r", [P, P], F32R)
            t.rden_hi, t.rden_lo = sb("rden_hi", [P, QUAD], F32R), sb("rden_lo", [P, QUAD])
            t.diag_hi, t.diag_lo = sb("diag_hi", [P, QUAD, P], F32R), sb("diag_lo", [P, QUAD, P], F32R)
            t.rden_split = sem("rden_split")
            t.waits, t.pool_waits, t.loaded, t.ctx_loaded, t.q_loaded, t.set_up, t.stat = (sem(n) for n in ("waits", "pool_waits", "loaded", "ctx_loaded", "q_loaded", "set_up", "stat"))
            t.aggr, t.eps, t.rstd_done, t.shift_done, t.centred = (sem(n) for n in ("aggr", "eps", "rstd_done", "shift_done", "centred"))
            t.weighted, t.xn_done, t.q_split, t.pads_set, t.weights_loaded = (sem(n) for n in ("weighted", "xn_done", "q_split", "pads_set", "weights_loaded"))

        lay.allocate = allocate

        def load_ctx(sp, b):
            sp.dma_start(t.ctx[:, 0:FULL, :],
                         dram.ctx[bass.ds(b, 1), 0:FULL * P, :].rearrange("o (p t) d -> p (o t) d", t=FULL)).then_inc(t.ctx_loaded, 16)
            sp.dma_start(t.ctx[0:TAIL, FULL, :],
                         dram.ctx[bass.ds(b, 1), FULL * P:CTX, :].rearrange("o p d -> p (o d)")).then_inc(t.ctx_loaded, 16)

        def load_q(sp, b):
            sp.dma_start(t.q_raw[:], dram.q1[bass.ds(b, 1)].rearrange("o p n -> p (o n)")).then_inc(t.q_loaded, 16)

        def sync_start(sp):
            load_ctx(sp, 0)
            load_q(sp, 0)
            sp.dma_start(t.weight[:], dram.L1_xattn_ln1_w.partition_broadcast(P)).then_inc(t.loaded, 16)
            sp.dma_start(t.bias[:], dram.L1_xattn_ln1_b.partition_broadcast(P)).then_inc(t.loaded, 16)
            sp.wait_ge(t.q_split, 2)
            load_q(sp, 1)
            sp.wait_ge(t.xn_done, CHUNKS)
            load_ctx(sp, 1)
            load_rest_1(sp, g, dram, t.weights_loaded)

        def sync_body(sp, k, kind):
            if kind != "last":
                for m in range(2):
                    b = 2 * k + m + 2
                    sp.wait_ge(t.q_split, 2 * b)
                    load_q(sp, b)
                    sp.wait_ge(t.xn_done, CHUNKS * b)
                    load_ctx(sp, b)

        lay.sync_start, lay.sync_body, lay.sync_end = sync_start, sync_body, lambda sp: sp.wait_ge(t.weights_loaded, LOADS_1)

        def split_queries(pool, b, m):
            wait_apart(pool, t.q_loaded, (b + 1) * 16, t.pool_waits)
            nc.gpsimd.tensor_copy(t.q_hi[m][:], t.q_raw[:]).then_inc(t.q_split, 1)
            pool.wait_ge(t.q_split, 2 * b + 1)
            nc.gpsimd.tensor_tensor(t.q_lo[m][:], t.q_raw[:], t.q_hi[m][:].bitcast(F32), ALU.subtract).then_inc(t.q_split, 1)

        def factors(pool, b):
            pool.wait_ge(t.eps, 2 * (b + 1))
            nc.gpsimd.tensor_tensor(t.rstd[:], t.rstd[:], t.half[:], ALU.pow).then_inc(t.rstd_done, 1)
            pool.wait_ge(t.rstd_done, b + 1)
            nc.gpsimd.tensor_tensor(t.shift[:], t.shift[:], t.rstd[:], ALU.mult).then_inc(t.shift_done, 1)

        def normed_rows(eng, ops, b, m, first, waits):
            wait_apart(eng, t.shift_done, b + 1, waits)
            for i in range(FULL + 1):
                rows = lay.tiles[i][0]
                ops.tensor_scalar(t.ctx[0:rows, i, :], t.ctx[0:rows, i, :], t.rstd[0:rows, i:i + 1], t.shift[0:rows, i:i + 1],
                                  ALU.mult, ALU.add).then_inc(t.centred, 1)
            for c in range(CHUNKS):
                n = 4 if c < 3 else 1
                rows, tiles = (P if c < 3 else TAIL), slice(4 * c, 4 * c + n)
                eng.wait_ge(t.centred, (FULL + 1) * b + 4 * c + n)
                w, bias = (v[0:rows].unsqueeze(1).broadcast_to([rows, n, D]) for v in (t.weight, t.bias))
                ops.tensor_tensor(t.ctx[0:rows, tiles, :], t.ctx[0:rows, tiles, :], w, ALU.mult).then_inc(t.weighted, 1)
                if not first:
                    eng.wait_ge(lay.own.pv_done, CHUNKS * (QUADS * (b - 1) - 1) + c + 1)
                eng.wait_ge(t.weighted, CHUNKS * b + c + 1)
                if c == 3:
                    ops.tensor_copy(t.xn[m][0:SEQ, LAT, :], g.lat_rows[:, bass.ds(b, 1), :].rearrange("p o d -> p (o d)"))
                ops.tensor_tensor(t.xn[m][0:rows, tiles, :], t.ctx[0:rows, tiles, :], bias, ALU.add).then_inc(t.xn_done, 1)

        def pool_start(pool):
            nc.gpsimd.memset(t.half[:], -0.5).then_inc(t.set_up, 1)
            nc.gpsimd.memset(t.ones[:], 1.0).then_inc(t.set_up, 1)
            pool.wait_ge(t.set_up, 2)
            nc.gpsimd.tensor_copy(t.ones_r[:], t.ones[:]).then_inc(t.set_up, 1)
            factors(pool, 0)
            split_queries(pool, 0, 0)

        def pool_prepare(pool, k, kind, m):
            b = 2 * k + m + 1
            first = kind == "first" and m == 0
            if not first:
                pool.wait_ge(lay.own.scores_ready, (b - 1) * PAIRS * CHUNKS)
            split_queries(pool, b, (m + 1) % 2)
            factors(pool, b)
            normed_rows(pool, nc.gpsimd, b, (m + 1) % 2, first, t.pool_waits)

        lay.pool_start, lay.pool_prepare = pool_start, pool_prepare

        def pe_start(pe):
            pe.wait_ge(t.set_up, 3)
            pe.wait_ge(t.pads_set, 4)

        def pe_job(pe, what, m, kind, k, s):
            own = lay.own
            if what[0] == "x_t":
                c = what[1]
                b = 0 if kind == "start" else 2 * k + m + 1
                par = 0 if kind == "start" else (m + 1) % 2
                pe.wait_ge(t.xn_done, CHUNKS * b + c + 1)
                for i, (rows, col) in enumerate(lay.tiles[4 * c:4 * c + 4]):
                    c0 = col - BANK * c
                    last = nc.tensor.transpose(own.scratch[:, c0:c0 + rows], t.xn[par][0:rows, 4 * c + i, :],
                                               g.consts[0:rows, C_IDENT:C_IDENT + rows])
                return last
            pe.wait_ge(own.pv_taken, 4 * k)
            for h in range(HEADS):
                last = nc.tensor.matmul(own.scratch[:, 0:D], t.u_t[:, h], g.wvo[:, h, :], start=(h == 0), stop=(h == HEADS - 1))
            return last

        def pe_operands_ready(pe, k, kind, m, u):
            if u == 0:
                pe.wait_ge(t.q_split, 2 * (2 * k + m) + 2)
                pe.wait_ge(lay.own.scratch_free, CHUNKS if kind == "first" and m == 0 else
                           lay.own.number_after(k, kind, PAIRS * m - 2, "b"))

        def pe_values(pe, m, u, tiles):
            for i in tiles:
                if i < len(lay.tiles):
                    rows = lay.tiles[i][0]
                    last = nc.tensor.matmul(lay.own.pv_ps[:], t.xn[m][0:rows, i, :], lay.own.prob_t[u][0:rows, i, :],
                                            start=(i == 0), stop=(i == LAT))
            return last

        lay.pe_start, lay.pe_job = pe_start, pe_job

        def split_diag(pool, q, rden, ident, diag_done):
            wait_apart(pool, lay.own.rden_done, q + 1, t.pool_waits)
            nc.gpsimd.tensor_copy(t.rden_hi[:], rden[:]).then_inc(t.rden_split, 1)
            pool.wait_ge(t.rden_split, 2 * q + 1)
            nc.gpsimd.tensor_tensor(t.rden_lo[:], rden[:], t.rden_hi[:].bitcast(F32), ALU.subtract).then_inc(t.rden_split, 1)
            pool.wait_ge(t.rden_split, 2 * q + 2)
            for out, part in ((t.diag_hi, t.rden_hi[:].bitcast(F32)), (t.diag_lo, t.rden_lo[:])):
                last = nc.gpsimd.tensor_tensor(out[:], ident.unsqueeze(1).broadcast_to([P, QUAD, P]),
                                               part.unsqueeze(2).broadcast_to([P, QUAD, P]), ALU.mult)
            last.then_inc(diag_done, 1)

        def pe_norm(pe, diag):
            nc.tensor.matmul(lay.own.scratch[:], t.ones_r[:], t.diag_hi[:].rearrange("p j q -> p (j q)"), start=True, stop=False)
            return nc.tensor.matmul(lay.own.scratch[:], t.ones_r[:], t.diag_lo[:].rearrange("p j q -> p (j q)"), start=False, stop=True)

        lay.pe_norm, lay.split_diag = pe_norm, split_diag
        lay.pe_operands_ready, lay.pe_values = pe_operands_ready, pe_values

        def score_passes(m, u, j):
            cols = slice(P * (QUAD * u + j), P * (QUAD * u + j) + P)
            return [(t.q_hi[m][:, cols], t.x_hi[m]), (t.q_hi[m][:, cols], t.x_lo[m]), (t.q_lo[m][:, cols], t.x_hi[m])]

        lay.score_passes = score_passes

        def act_take(act, what, m):
            if what[0] == "x_t":
                cols = quad_chunk(what[1], KEYS)
                nc.scalar.activation(t.x_hi[m][:, cols], lay.own.scratch[:, 0:cols.stop - cols.start], ACT.Copy).then_inc(lay.own.half_taken, 1)

        lay.act_start, lay.act_take = (lambda act: None), act_take

        def x_low(dve, c, b, m):
            cols = quad_chunk(c, KEYS)
            dve.wait_ge(lay.own.half_taken, CHUNKS * b + c + 1)
            nc.vector.tensor_tensor(t.x_lo[m][:, cols], lay.own.scratch[:, 0:cols.stop - cols.start], t.x_hi[m][:, cols].bitcast(F32),
                                    ALU.subtract).then_inc(lay.own.scratch_free, 1)

        def add_output(dve, tile):
            row = g.x_tok[:, bass.ds(tile, 1), :].rearrange("p o d -> p (o d)")
            nc.vector.tensor_tensor(row, lay.own.scratch[:, 0:D], row, ALU.add).then_inc(lay.own.scratch_free, 1)

        def dve_take(dve, entry, base, k, kind, s):
            what, n = entry
            if what[0] == "x_t":
                x_low(dve, what[1], 2 * k + s // PAIRS + 1, (s // PAIRS + 1) % 2)
            elif what[0] == "out":
                dve.wait_ge(lay.own.scratch_ready, base + n + 1)
                add_output(dve, k - 1)

        def statistics(dve, b, i):
            if i == 0:
                dve.wait_ge(t.ctx_loaded, (b + 1) * 32)
            rows = lay.tiles[i][0]
            nc.vector.bn_stats(t.stats[0:rows, i, :], t.ctx[0:rows, i, :]).then_inc(t.stat, 1)

        def means(dve, b, tiles):
            wait_apart(dve, t.stat, (FULL + 1) * b + tiles[-1] + 1, t.waits)
            for i in tiles:
                rows = lay.tiles[i][0]
                nc.vector.bn_aggr(t.mean_var[0:rows, i, :], t.stats[0:rows, i, :]).then_inc(t.aggr, 1)
            if tiles[-1] == FULL:
                dve.wait_ge(t.aggr, (FULL + 1) * (b + 1))
                if not (isinstance(b, int) and b == 0):
                    dve.wait_ge(t.xn_done, CHUNKS * b)
                nc.vector.tensor_scalar(t.rstd[:], t.mean_var[:, :, 1], LN_EPS, None, ALU.add).then_inc(t.eps, 1)
                nc.vector.tensor_scalar(t.shift[:], t.mean_var[:, :, 0], -1.0, None, ALU.mult).then_inc(t.eps, 1)

        def dve_start(dve):
            for v in t.x_hi + t.x_lo:
                nc.vector.memset(v[:, KEYS:KEYS + 1].bitcast(U32), 0).then_inc(t.pads_set, 1)
            nc.vector.memset(t.mean_var[:], 0.0).then_inc(t.pads_set, 1)
            dve.wait_ge(t.pads_set, 5)
            for i in range(FULL + 1):
                statistics(dve, 0, i)
            means(dve, 0, list(range(FULL + 1)))
            dve.wait_ge(t.loaded, 32)
            normed_rows(dve, nc.vector, 0, 0, True, t.waits)
            for c in range(CHUNKS):
                x_low(dve, c, 0, 0)

        def dve_between(dve, k, kind, s, c):
            m, n = divmod(s, PAIRS)
            if n < 3 and not (kind == "last" and m == 1):
                statistics(dve, 2 * k + m + 1, 4 * n + c)

        def dve_extra(dve, k, kind, s):
            m, n = divmod(s, PAIRS)
            if n < 3 and not (kind == "last" and m == 1):
                b = 2 * k + m + 1
                for i in range(4 * n + 3, 4 * n + 4 + n // 2):
                    statistics(dve, b, i)
                means(dve, b, list(range(4 * n, 4 * n + 4 + n // 2)))

        def dve_finish(dve, q, i, k):
            own = lay.own
            m, u = i // QUADS % 2, i % QUADS
            if i == 0 and not (isinstance(k, int) and k == 0):
                dve.wait_ge(own.scratch_ready, own.number_after(k, "mid" if not isinstance(k, int) else "last", 5, "a"))
            nc.vector.tensor_tensor(t.u_t[:, 8 * u:8 * u + 8, m, :], own.pv_ps[:].rearrange("p (h q) -> p h q", h=8),
                                    own.norm[:].rearrange("p (h q) -> p h q", h=8), ALU.mult).then_inc(own.pv_taken, 1)

        def dve_end(dve):
            own = lay.own
            n = own.base("last", BODIES - 1) + len(own.table["last"]) + 2
            dve.wait_ge(own.scratch_ready, n)
            add_output(dve, BODIES - 1)

        lay.dve_start, lay.dve_take, lay.dve_finish, lay.dve_extra, lay.dve_end = dve_start, dve_take, dve_finish, dve_extra, dve_end
        lay.dve_between = dve_between
        attend(nc, g, lay, ctx)


def constant_columns():
    import numpy as np
    p = np.arange(P)
    c = np.zeros((P, C_END), np.float32)
    c[:, C_IDENT:C_IDENT + P] = np.eye(P)
    r = np.arange(32)
    c[:, C_PAIRROWS:C_PAIRROWS + 32] = (p[:, None] // SEQ == r[None] // E0) & (r[None] < 2 * E0)
    c[:, C_HEADROWS:C_HEADROWS + 8] = (p[:, None] % 64) // E0 == np.arange(8)[None]
    c[:, C_CAUSAL:C_CAUSAL + SEQ] = np.where(np.arange(SEQ)[None] <= p[:, None] % SEQ, 0.0, -1e30)
    freq = (1.0 / 10000.0 ** (np.arange(0, E0, 2, dtype=np.float32) / E0)).astype(np.float32)
    angle = np.arange(SEQ, dtype=np.float32)[None] * freq[(p % E0) // 2][:, None]
    c[:, C_COS:C_COS + SEQ] = np.cos(angle)
    c[:, C_SIN:C_SIN + SEQ] = np.sin(angle) * np.where(p % 2 == 0, -1.0, 1.0)[:, None]
    c[:, C_IOTA:C_IOTA + 8] = np.arange(8)[None]
    c[:, C_SEQSTART:C_SEQSTART + SEQ + 1] = (np.arange(SEQ + 1) > 0)[None]
    c[:, C_QUADROWS:C_QUADROWS + 4] = p[:, None] % 32 // E0 == np.arange(4)[None]
    c[:, C_GROUPROWS:C_GROUPROWS + 4] = p[:, None] // 32 == np.arange(4)[None]
    return c


def build(nc, tensors, consts, out):
    dram = Named()
    dram.x, dram.ctx, dram.consts = tensors["x"], tensors["ctx_1024"], consts
    dram.L0_xattn_wq, dram.L0_xattn_bq, dram.L0_xattn_wk, dram.L0_xattn_bk = (
        tensors["L0_xattn_wq"], tensors["L0_xattn_bq"], tensors["L0_xattn_wk"], tensors["L0_xattn_bk"])
    dram.L0_xattn_wv, dram.L0_xattn_bv, dram.L0_xattn_wo, dram.L0_xattn_bo = (
        tensors["L0_xattn_wv"], tensors["L0_xattn_bv"], tensors["L0_xattn_wo"], tensors["L0_xattn_bo"])
    dram.L0_attn_W_KQV, dram.L0_attn_W_O = (
        tensors["L0_attn_W_KQV"], tensors["L0_attn_W_O"])
    dram.L0_ffn_router_w, dram.L0_ffn_w1, dram.L0_ffn_w2 = (
        tensors["L0_ffn_router_w"], tensors["L0_ffn_w1"], tensors["L0_ffn_w2"])
    dram.L1_xattn_ln1_w, dram.L1_xattn_ln1_b, dram.L1_xattn_ln2_w, dram.L1_xattn_ln2_b = (
        tensors["L1_xattn_ln1_w"], tensors["L1_xattn_ln1_b"], tensors["L1_xattn_ln2_w"], tensors["L1_xattn_ln2_b"])
    dram.L1_xattn_Wq, dram.L1_xattn_Wkv, dram.L1_xattn_Wo = (
        tensors["L1_xattn_Wq"], tensors["L1_xattn_Wkv"], tensors["L1_xattn_Wo"])
    dram.L1_attn_time_decay, dram.L1_attn_time_first, dram.L1_attn_time_mix, dram.L1_attn_Wk = (
        tensors["L1_attn_time_decay"], tensors["L1_attn_time_first"], tensors["L1_attn_time_mix"], tensors["L1_attn_Wk"])
    dram.L1_attn_Wv, dram.L1_attn_Wr, dram.L1_attn_Wo = (
        tensors["L1_attn_Wv"], tensors["L1_attn_Wr"], tensors["L1_attn_Wo"])
    dram.L1_ffn_w1, dram.L1_ffn_b1, dram.L1_ffn_w2, dram.L1_ffn_b2 = (
        tensors["L1_ffn_w1"], tensors["L1_ffn_b1"], tensors["L1_ffn_w2"], tensors["L1_ffn_b2"])
    dram.q1 = nc.dram_tensor("absorbed_queries", (BATCH, P, HEADS * SEQ), F32, kind="Internal").ap()
    with ExitStack() as kept:
        def sb(name, shape):
            return kept.enter_context(nc.sbuf_tensor(name, shape, F32))

        g = Named()
        g.x_tok = sb("x_tok", [P, TOK_TILES, D])
        g.consts = sb("consts", [P, C_END])
        g.act_t = sb("act_t", [P, QUADS, TOKENS])
        g.wo_rows = sb("wo_rows", [P, QUADS, D])
        g.rest_0 = rest_0_buffers(sb)
        cross_attention_0(nc, g, dram)
        g.lat_rows = sb("lat_rows", [SEQ, BATCH, D])
        g.wvo = sb("wvo", [P, HEADS, D])
        g.rest_1 = rest_1_buffers(sb)
        with nc.sbuf_tensor("qk", [P, HEADS, D], F32) as g.qk:
            fold_resampler_weights(nc, g, dram)
            rest_of_layer_0(nc, g, dram)
        cross_attention_1(nc, g, dram)
        rest_of_layer_1(nc, g, dram, out)


_OUT = ((BATCH, SEQ, D), "float32")


def kernel(**inputs):
    import numpy as _np
    import concourse.bacc as _bacc
    from concourse import mybir as _mybir
    from concourse.bass_utils import run_bass_kernel_spmd as _run

    nc = _bacc.Bacc("TRN2", target_bir_lowering=False, num_devices=1)
    arrays, tensors = {}, {}
    for name in inputs:
        a = _np.ascontiguousarray(inputs[name])
        arrays[f"in_{name}_dram"] = a
        tensors[name] = nc.dram_tensor(f"in_{name}_dram", a.shape, _mybir.dt.from_np(a.dtype), kind="ExternalInput").ap()
    table = constant_columns()
    arrays["in_consts_dram"] = table
    consts = nc.dram_tensor("in_consts_dram", table.shape, _mybir.dt.from_np(table.dtype), kind="ExternalInput").ap()
    out = nc.dram_tensor("out_0_dram", _OUT[0], _mybir.dt.from_np(_np.dtype(_OUT[1])), kind="ExternalOutput").ap()
    build(nc, tensors, consts, out)
    r = _run(nc, [arrays], core_ids=[0])
    return r.results[0]["out_0_dram"]
```
